# Optimizing a Trainium2 kernel written in Bass

```python
import numpy as np
import jax
import jax.numpy as jnp

def _softmax(x, axis=-1):
    return jax.nn.softmax(x, axis=axis)

def _gelu(x):
    return jax.nn.gelu(x, approximate=True)

def _silu(x):
    return jax.nn.silu(x)

def _sigmoid(x):
    return jax.nn.sigmoid(x)

def _layernorm(x, axis=-1, eps=1e-05):
    m = jnp.mean(x, axis=axis, keepdims=True)
    v = jnp.var(x, axis=axis, keepdims=True)
    return (x - m) / jnp.sqrt(v + eps)

def _scatter_add(tgt, idx, src, axis=0):
    return tgt.at[idx].add(src)

def _segment_sum(src, seg, n):
    return jax.ops.segment_sum(src, seg, n)
kernel_name = 'mk_xattn_ffn_d1_seqx_r8_4426e5'

def setup_inputs(seed: int=0):
    np.random.seed(seed)
    _w = jnp.asarray

    def _rec_inputs():
        import jax
        import jax.numpy as jnp
        _rk = jax.random.key(seed)
        x = 7.22e-05 + 1 * jax.random.normal(jax.random.fold_in(_rk, 1), (64, 128, 128), jnp.float32)
        _lenS = 128 - jax.random.randint(jax.random.fold_in(_rk, 7), (64,), 0, max(1, 128 // 4) + 1, jnp.int32)
        _lenS2 = 120 - jax.random.randint(jax.random.fold_in(_rk, 8), (64,), 0, max(1, 120 // 4) + 1, jnp.int32)
        _ctx_1024P = jax.random.normal(jax.random.fold_in(_rk, 11), (64, 16, 128), jnp.float32)
        _ctx_1024c = jax.random.dirichlet(jax.random.fold_in(_rk, 511), 0.3 * jnp.ones((16,), jnp.float32), (64, 120))
        _ctx_1024t = jnp.einsum('bsk,bkd->bsd', _ctx_1024c, _ctx_1024P)
        _ctx_1024t = _ctx_1024t * jax.lax.rsqrt(jnp.mean(jnp.square(_ctx_1024t)) + 1e-12) * 0.953939
        ctx_1024 = 4.13588e-05 + 0.999923 * (_ctx_1024t + 0.3 * jax.random.normal(jax.random.fold_in(_rk, 611), (64, 120, 128), jnp.float32))
        _validS = jnp.arange(128)[None, :] < _lenS[:, None]
        _validS2 = jnp.arange(120)[None, :] < _lenS2[:, None]
        _causal = jnp.tril(jnp.ones((128, 128), dtype=bool))
        mask_BxS2_bf0 = jnp.logical_not(jnp.ones((64, 120), dtype=bool))
        return (x, ctx_1024, mask_BxS2_bf0)
    x, ctx_1024, mask_BxS2_bf0 = _rec_inputs()

    def _L0_xattn_setup():
        import jax, jax.numpy as jnp
        import numpy as np
        DIM = 128
        N_HEAD = 16
        BS, QLEN, KLEN = (4, 256, 256)
        key = jax.random.key(seed)
        ks = jax.random.split(key, 12)
        s = 1.0 / np.sqrt(DIM)
        inp = {'q_in': jax.random.normal(ks[0], (BS, QLEN, DIM), jnp.float32), 'k_in': jax.random.normal(ks[1], (BS, KLEN, DIM), jnp.float32), 'v_in': jax.random.normal(ks[2], (BS, KLEN, DIM), jnp.float32), 'key_padding_mask': jnp.zeros((BS, KLEN), dtype=bool), 'Wq': jax.random.normal(ks[3], (DIM, DIM), jnp.float32) * s, 'bq': jnp.zeros((DIM,), jnp.float32), 'Wk': jax.random.normal(ks[4], (DIM, DIM), jnp.float32) * s, 'bk': jnp.zeros((DIM,), jnp.float32), 'Wv': jax.random.normal(ks[5], (DIM, DIM), jnp.float32) * s, 'bv': jnp.zeros((DIM,), jnp.float32), 'Wo': jax.random.normal(ks[6], (DIM, DIM), jnp.float32) * s, 'bo': jnp.zeros((DIM,), jnp.float32)}
        return inp
    _L0_xattn_all = _L0_xattn_setup()
    _L0_xattn_in = {k: v for k, v in _L0_xattn_all.items() if k in ('Wq', 'bq', 'Wk', 'bk', 'Wv', 'bv', 'Wo', 'bo')}
    del _L0_xattn_all

    def _L0_ffn_setup():
        import jax, jax.numpy as jnp
        import numpy as np
        E, D, MULT, K = (8, 128, 4, 2)
        B, S = (4, 256)
        H = MULT * D
        key = jax.random.key(seed)
        k0, k1, k2, k3 = jax.random.split(key, 4)
        x = jax.random.normal(k0, (B, S, D), dtype=jnp.float32)
        Wr = jax.random.normal(k1, (E, D), dtype=jnp.float32) * D ** (-0.5)
        W1 = jax.random.normal(k2, (E, D, H), dtype=jnp.float32) * D ** (-0.5)
        b1 = jnp.zeros((E, H), dtype=jnp.float32)
        W2 = jax.random.normal(k3, (E, H, D), dtype=jnp.float32) * H ** (-0.5)
        b2 = jnp.zeros((E, D), dtype=jnp.float32)
        return {'x': x, 'Wr': Wr, 'W1': W1, 'b1': b1, 'W2': W2, 'b2': b2}
    _L0_ffn_all = _L0_ffn_setup()
    _L0_ffn_in = {k: v for k, v in _L0_ffn_all.items() if k in ('Wr', 'W1', 'b1', 'W2', 'b2')}
    del _L0_ffn_all
    return {'x': x, 'ctx_1024': ctx_1024, 'mask_BxS2_bf0': mask_BxS2_bf0, 'L0_xattn_Wq': _L0_xattn_in['Wq'], 'L0_xattn_bq': _L0_xattn_in['bq'], 'L0_xattn_Wk': _L0_xattn_in['Wk'], 'L0_xattn_bk': _L0_xattn_in['bk'], 'L0_xattn_Wv': _L0_xattn_in['Wv'], 'L0_xattn_bv': _L0_xattn_in['bv'], 'L0_xattn_Wo': _L0_xattn_in['Wo'], 'L0_xattn_bo': _L0_xattn_in['bo'], 'L0_ffn_Wr': _L0_ffn_in['Wr'], 'L0_ffn_W1': _L0_ffn_in['W1'], 'L0_ffn_b1': _L0_ffn_in['b1'], 'L0_ffn_W2': _L0_ffn_in['W2'], 'L0_ffn_b2': _L0_ffn_in['b2']}

def reference(x, ctx_1024, mask_BxS2_bf0, L0_xattn_Wq, L0_xattn_bq, L0_xattn_Wk, L0_xattn_bk, L0_xattn_Wv, L0_xattn_bv, L0_xattn_Wo, L0_xattn_bo, L0_ffn_Wr, L0_ffn_W1, L0_ffn_b1, L0_ffn_W2, L0_ffn_b2):
    import jax
    import jax.numpy as jnp

    def _L0_xattn_ref(q_in, k_in, v_in, key_padding_mask, Wq, bq, Wk, bk, Wv, bv, Wo, bo):
        import jax, jax.numpy as jnp
        import numpy as np
        DIM = 128
        N_HEAD = 16
        BS, QLEN, KLEN = (4, 256, 256)
        bs, q_len, _ = q_in.shape
        k_len = k_in.shape[1]
        h = N_HEAD
        d = DIM // h
        q = (q_in @ Wq + bq).reshape(bs, q_len, h, d).transpose(0, 2, 1, 3)
        k = (k_in @ Wk + bk).reshape(bs, k_len, h, d).transpose(0, 2, 1, 3)
        v = (v_in @ Wv + bv).reshape(bs, k_len, h, d).transpose(0, 2, 1, 3)
        score = jnp.einsum('bhqd,bhkd->bhqk', q, k) / jnp.sqrt(jnp.float32(d))
        mask = key_padding_mask[:, None, None, :]
        score = jnp.where(mask, jnp.float32(-1e+30), score)
        attn = jax.nn.softmax(score, axis=-1)
        out = jnp.einsum('bhqk,bhkd->bhqd', attn, v).transpose(0, 2, 1, 3).reshape(bs, q_len, DIM)
        return out @ Wo + bo

    def _L0_ffn_ref(x, Wr, W1, b1, W2, b2):
        import jax, jax.numpy as jnp
        import numpy as np
        E, D, MULT, K = (8, 128, 4, 2)
        B, S = (4, 256)
        H = MULT * D
        probs = jax.nn.softmax(jnp.einsum('bsd,ed->bse', x, Wr), axis=-1)
        topv, topi = jax.lax.top_k(probs, K)
        combine = jnp.sum(topv[..., None] * jax.nn.one_hot(topi, E, dtype=x.dtype), axis=2)

        def body(acc, params):
            w1, bb1, w2, bb2, ce = params
            h = jax.nn.gelu(jnp.einsum('bsd,dh->bsh', x, w1) + bb1, approximate=False)
            y = jnp.einsum('bsh,hd->bsd', h, w2) + bb2
            return (acc + ce[..., None] * y, None)
        cE = jnp.moveaxis(combine, -1, 0)
        out, _ = jax.lax.scan(body, jnp.zeros_like(x), (W1, b1, W2, b2, cE))
        return out
    x = x + _L0_xattn_ref(_layernorm(x, axis=-1), ctx_1024, ctx_1024, mask_BxS2_bf0, L0_xattn_Wq, L0_xattn_bq, L0_xattn_Wk, L0_xattn_bk, L0_xattn_Wv, L0_xattn_bv, L0_xattn_Wo, L0_xattn_bo)
    x = x + _L0_ffn_ref(_layernorm(x, axis=-1), L0_ffn_Wr, L0_ffn_W1, L0_ffn_b1, L0_ffn_W2, L0_ffn_b2)
    return x

_drawn_inputs = setup_inputs


def setup_inputs(seed=0):
    import zlib

    import numpy as np

    out = dict(_drawn_inputs(seed))
    spreads = {'L0_xattn_bq': (0.0, 0.1),
     'L0_xattn_bk': (0.0, 0.8),
     'L0_xattn_bv': (0.0, 0.1),
     'L0_xattn_bo': (0.0, 0.1),
     'L0_ffn_b1': (0.0, 0.314),
     'L0_ffn_b2': (0.0, 0.1)}
    factors = {}
    for name, (base, spread) in spreads.items():
        noise = np.random.default_rng([zlib.crc32(name.encode()), seed]).standard_normal(out[name].shape)
        drawn = base * np.exp(spread * noise) if base else spread * noise
        out[name] = jnp.asarray(drawn.astype(out[name].dtype))
    for name, factor in factors.items():
        out[name] = (out[name] * factor).astype(out[name].dtype)
    return out
```

```python
from contextlib import ExitStack

import concourse.bass as bass
from concourse import mybir

F32 = mybir.dt.float32
F32R = mybir.dt.float32r
U32 = mybir.dt.uint32
I32 = mybir.dt.int32
BF16 = mybir.dt.bfloat16
ALU = mybir.AluOpType
ACT = mybir.ActivationFunctionType
AX = mybir.AxisListType

P = 128
MASKED = -float(2**100)
EPS = 1e-5


class At:

    def __init__(self, pair, parity):
        self.pair, self.parity = pair, parity

    def __add__(self, k):
        n = self.parity + k
        return At(self.pair + n // 2 if n // 2 else self.pair, n % 2)

    def count(self, each, more=0):
        return self.pair * (2 * each) + (self.parity * each + more)

    def uses(self, each, more=0):
        return self.pair * each + (each + more)


def moe_attention(nc, x, ctx, mask, Wq, bq, Wk, bk, Wv, bv, Wo, bo, Wr, W1, b1, W2, b2, out):
    B, S, D = x.shape
    KL = ctx.shape[1]
    E, _, HID = W1.shape
    H, DH = 16, 8
    G, J = 4, 4
    R = 32
    HI2, MHI, MLO, MSK = 16, 24, 25, 26
    NCH = B // 2
    HC = HID // P
    TB = 512
    NTOK = B * S
    TN = TB // P
    NT = (2 * NTOK + E * (TB - 1)) // TB
    REGION = NTOK + TB
    SPARE = E * REGION
    ROW = D + 4
    NOWHERE = 1 << 20
    SCALE = float(DH) ** -0.5
    N2 = 2 * S
    K2 = 2 * KL

    with ExitStack() as st:
        sb = lambda name, shape, dt=F32: st.enter_context(nc.sbuf_tensor(name, shape, dt))
        sem = lambda name: st.enter_context(nc.semaphore(name))
        two = lambda name: [sem(f"{name}{k}") for k in range(2)]

        xres = sb("xres", [P, B, D])
        x2s = sb("x2s", [P, N2])
        ctxin = [sb(f"ctxin{k}", [KL, 2, D]) for k in range(2)]
        xn = [sb(f"xn{k}", [P, 2, D]) for k in range(2)]
        rows = [sb(f"rows{k}", [P, 2, 2, ROW]) for k in range(2)]
        xcT = [sb(f"xcT{k}", [P, N2 + K2]) for k in range(2)]
        xcTh = [sb(f"xcTh{k}", [P, N2 + K2], F32R) for k in range(2)]
        xcTl = [sb(f"xcTl{k}", [P, N2 + K2], F32R) for k in range(2)]
        part = [sb(f"part{k}", [P, 2 * N2], F32R) for k in range(2)]
        qs = [sb(f"qs{k}", [P, 2, G, S], F32R) for k in range(2)]
        ks = [sb(f"ks{k}", [P, G, K2], F32R) for k in range(2)]
        qb = [sb(f"qb{k}", [P, 2, G, J, S], F32R) for k in range(2)]
        kb = [sb(f"kb{k}", [P, G, J, K2], F32R) for k in range(2)]
        vs_all = [sb(f"vs{k}", [P, 2, H, R]) for k in range(2)]
        vs = [v[0:KL] for v in vs_all]
        NP = 4
        pt_all = [sb(f"pt{k}", [P, J, S]) for k in range(NP)]
        pt = [p[0:KL] for p in pt_all]
        mx = sb("mx", [P, J, 2, G])
        negm = [sb(f"negm{k}", [J * G * 2, 2, S], F32R) for k in range(2)]
        ots = [sb(f"ots{k}", [P, G, S]) for k in range(2)]
        rden = sb("rden", [P, G, J])
        on = sb("on", [P, H, DH])
        onT = sb("onT", [P, S])
        wq3 = [sb(f"wq{k}", [P, G, J, R], F32R) for k in ("hi", "lo")]
        wk3 = [sb(f"wk{k}", [P, G, J, R], F32R) for k in ("hi", "lo")]
        wst = ots[1][:].rearrange("p g (j r) -> p g j r", j=J)
        wraw = sb("wraw", [P, 4, D])
        brow = sb("brow", [3, 2, D])
        bst = [p[0:3].rearrange("p g (j r) -> p g j r", j=J) for p in pt_all]
        augw = part[0][0:3, :].rearrange("p (g j r) -> p g j r", g=G, j=J)
        aug = [sb(f"aug{k}", [3, G, J, R], F32R) for k in "qk"]
        augx = [sb(f"augx{k}", [3, K2], F32R) for k in range(2)]
        ones2 = sb("ones2", [2, N2], F32R)
        masku = sb("masku", [B, KL], mask.dtype)
        maskf = sb("maskf", [B, KL], F32R)
        keep = sb("keep", [3, 1])
        rowsel = [sb(f"rowsel{k}", [P, 1]) for k in "qk"]
        bvb = sb("bvb", [P, 2, D])
        bob = sb("bob", [P, D])
        ident = sb("ident", [P, P])
        wrT = sb("wrT", [P, E])
        wrraw = sb("wrraw", [E, D])
        stats = sb("stats", [P, 4, 6])
        mv = sb("mv", [P, 4, 2])
        ve = sb("ve", [P, 4])
        y0 = sb("y0", [P, 4])
        y1 = sb("y1", [P, 4])
        y3 = sb("y3", [P, 4])
        lnv = sb("lnv", [P, 4])
        y2 = sb("y2", [P, 4])
        rstd = sb("rstd", [P, 4])
        top = sb("top", [P, 2, 8])
        topd = sb("topd", [P, 2, 8])
        tope = sb("tope", [P, 2, 8])
        tsum = sb("tsum", [P, 2])
        tinv = sb("tinv", [P, 2])
        tidx = sb("tidx", [P, 2, 8], U32)
        prob = sb("prob", [P, B, 2])
        pick = sb("pick", [P, 4])
        hot = sb("hot", [P, 2, 2, E], BF16)
        taken = sb("taken", [P, 2, E], BF16)
        taken2 = sb("taken2", [P, E], BF16)
        before = sb("before", [P, E], BF16)
        tri = sb("tri", [P, P], BF16)
        trif = sb("trif", [P, P])
        ones = sb("ones", [P, P], BF16)
        eidx = sb("eidx", [P, E])
        region = sb("region", [P, E])
        place = sb("place", [P, 2, E])
        placed = sb("placed", [P, 4, E])
        posf = sb("posf", [P, 4])
        posi = [sb(f"posi{k}", [P, 4], I32) for k in range(2)]
        idf = sb("idf", [P, 4])
        zrows = sb("zrows", [P, TN, ROW])
        cnt = sb("cnt", [1, E])
        thr = sb("thr", [1, E, NTOK // TB])
        over = sb("over", [1, E, NTOK // TB])
        cum = [sb(f"cum{k}", [1, E]) for k in range(4)]
        tix = sb("tix", [1, NT, E])
        past = sb("past", [1, NT, E])
        pastn = sb("pastn", [1, NT, E])
        tile_e = sb("tile_e", [1, NT])
        tile_s = sb("tile_s", [1, NT])
        tile_r = [sb(f"tile_r{k}", [1, NT]) for k in range(3)]
        tail_r = sb("tail_r", [1, E])
        tab_e = sb("tab_e", [1, NT], I32)
        tab_r = sb("tab_r", [1, NT], I32)
        tab_t = sb("tab_t", [1, E], I32)
        bsb = sb("bsb", [P, E, HC + 1])
        wsp = sb("wsp", [P, 2, 2, HID], F32R)
        hid = sb("hid", [P, 2, HID])
        braw = hid[0:E * (HC + 1), 0, 0:P]
        btile = [sb(f"btile{k}", [P, HC + 1]) for k in range(2)]
        idt = [sb(f"idt{k}", [P, TN], I32) for k in range(2)]
        flat = lambda t, spec: t[:].rearrange(f"{spec} -> p ({spec[2:]})")
        kflat = [flat(kb[k], "p g j n") for k in range(2)]
        wtile = [kflat[k][:, 0:4 * HID].rearrange("p (k w n) -> p k w n", k=2, w=2) for k in range(2)]
        xTh, xTl = (kflat[0][:, 4 * HID + i * TB:4 * HID + (i + 1) * TB] for i in range(2))
        hhl = flat(qb[0], "p b g j q").rearrange("p (k c t) -> p k c t", k=2, c=HC)
        xrow = [rows[k][:].rearrange("p a b w -> p (a b) w") for k in range(2)]
        yT = flat(ots[0], "p g q")
        yrow = [vs_all[0][:, k].rearrange("p h r -> p (h r)").rearrange("p (n d) -> p n d", n=TN) for k in range(2)]
        yin = [[pt_all[2 * i + k] for k in range(2)] for i in range(2)]

        bank = [st.enter_context(nc.psum_tensor(f"bank{k}", [P, 512], F32)) for k in range(8)]
        wide = bank[0:3]
        scores = bank[3:5]
        heads = bank[5]
        small = bank[6:8]

        w_in, w_in2 = sem("w_in"), sem("w_in2")
        x_in, ctx_in = two("x_in"), two("ctx_in")
        mask_in, mask_f, mask_dram = sem("mask_in"), sem("mask_f"), sem("mask_dram")
        mask_row = two("mask_row")
        ident_done, pool_done = sem("ident_done"), sem("pool_done")
        prep = sem("prep")
        wr_T, prep2 = sem("wr_T"), sem("prep2")
        ln_done, ln_chain, ln_log, ln_act, dve_chain = (sem(k) for k in ("ln_done", "ln_chain", "ln_log", "ln_act", "dve_chain"))
        tx_full, tx_taken, hi_done, hl_done, xbo_done = (sem(k) for k in ("tx_full", "tx_taken", "hi_done", "hl_done", "xbo_done"))
        w_full, w_part, w_free = sem("w_full"), sem("w_part"), sem("w_free")
        qblk, kblk, mrow = two("qblk"), two("kblk"), two("mrow")
        v_full, v_taken = sem("v_full"), sem("v_taken")
        mx_done, nm_full, nm_split = sem("mx_done"), sem("nm_full"), sem("nm_split")
        b_full, exp_done, pv_done = sem("b_full"), sem("exp_done"), sem("pv_done")
        ot_taken, ott_full, rc_done, on_done = sem("ot_taken"), sem("ott_full"), sem("rc_done"), sem("on_done")
        ont_full, ont_taken, wo_full, x1_done = sem("ont_full"), sem("ont_taken"), sem("wo_full"), sem("x1_done")
        x2t_full, x2t_taken, rl_full, rl_taken = sem("x2t_full"), sem("x2t_taken"), sem("rl_full"), sem("rl_taken")
        top_max, top_sub, top_exp, top_chain, routed = (sem(k) for k in ("top_max", "top_sub", "top_exp", "top_chain", "routed"))
        pos_full, pos_taken, pos_chain, pos_done, hot_done, kept = (
            sem(k) for k in ("pos_full", "pos_taken", "pos_chain", "pos_done", "hot_done", "kept"))
        scat, rows2, ids_done = two("scat"), sem("rows2"), sem("ids_done")
        zrow_done, spare_done, b_in = sem("zrow_done"), sem("spare_done"), sem("b_in")
        wraw_in, wsplit, wsave = sem("wraw_in"), sem("wsplit"), sem("wsave")
        cnt_full, tables, tail_done = sem("cnt_full"), sem("tables"), sem("tail_done")
        x_tile, w_tile, y_out = two("x_tile"), two("w_tile"), two("y_out")
        xt_full, xt_hi, xt_lo, id_done = sem("xt_full"), sem("xt_hi"), sem("xt_lo"), sem("id_done")
        h_full, h_hi, h_val, h_lo = sem("h_full"), sem("h_hi"), sem("h_val"), sem("h_lo")
        yt_full, yt_taken, yr_full, yr_taken = sem("yt_full"), sem("yt_taken"), sem("yr_full"), sem("yr_taken")
        y_in, fin_a, fin_b = two("y_in"), sem("fin_a"), sem("fin_b")
        xd = nc.dram_tensor("xd", (SPARE + TB, ROW), F32, kind="Internal").ap()
        yd = nc.dram_tensor("yd", (2 * NTOK, D), F32, kind="Internal").ap()
        wd = nc.dram_tensor("wd", (E, P, 4 * HID), F32R, kind="Internal").ap()
        maskd = nc.dram_tensor("maskd", (B, KL), F32R, kind="Internal").ap()
        out_done = sem("out_done")

        def slots(eng, body):
            for s in range(-2, 4):
                body(At(s // 2, s % 2), s)
            with eng.Fori(2, NCH // 2 - 2) as pair:
                body(At(pair, 0), None)
                body(At(pair, 1), None)
            for s in range(NCH - 4, NCH + 2):
                body(At(s // 2, s % 2), s)

        def tiles(eng, body):
            for t in range(4):
                body(At(t // 2, t % 2), t)
            with eng.Fori(2, NT // 2) as pair:
                body(At(pair, 0), None)
                body(At(pair, 1), None)
            for t in range(2 * (NT // 2), NT + 1):
                body(At(t // 2, t % 2), t)

        WSLOTS = {n: e for e, n in enumerate((0, 1, *range(NCH - 4, NCH + 2)))}

        def alone(eng, semaphore, value):
            if not isinstance(value, int):
                value = eng.to_reg(value)
                eng.wait_ge(ident_done, 2)
            eng.wait_ge(semaphore, value)

        def exists(s, back):
            return s is None or 0 <= s + back < NCH

        block = st.enter_context(nc.Block())

        @block.sync
        def _(sp):
            for k, w in enumerate((Wq, Wk, Wv, Wo)):
                sp.dma_start(wraw[:, k, :], w).then_inc(w_in, 16)
            for k, b in enumerate((bq, bk)):
                sp.dma_start(brow[:, k, :], b.rearrange("(a n) -> a n", a=1).to_broadcast([3, D])).then_inc(w_in, 16)
            sp.dma_start(wrraw[:, :], Wr).then_inc(w_in, 16)
            sp.dma_start(masku[:, :], mask).then_inc(mask_in, 16)
            sp.dma_start(braw[0:E * HC, :], b1.rearrange("e (c p) -> (e c) p", p=P)).then_inc(b_in, 16)
            sp.dma_start(braw[E * HC:E * HC + E, :], b2).then_inc(b_in, 16)
            for b in range(2):
                sp.dma_start(bvb[:, b, :], bv.rearrange("(a n) -> a n", a=1).to_broadcast([P, D])).then_inc(w_in2, 16)
            sp.dma_start(bob[:, :], bo.rearrange("(a n) -> a n", a=1).to_broadcast([P, D])).then_inc(w_in2, 16)

            def load(c):
                sp.dma_start(xres[:, bass.ds(c.count(2), 2), :],
                             x[bass.ds(c.count(2), 2), :, :].rearrange("b s d -> s b d")).then_inc(x_in[c.parity], 16)
                sp.dma_start(ctxin[c.parity][:, :, :],
                             ctx[bass.ds(c.count(2), 2), :, :].rearrange("b s d -> s b d")).then_inc(ctx_in[c.parity], 16)

            load(At(0, 0))
            load(At(0, 1))
            sp.wait_ge(mask_f, 1)
            sp.dma_start(maskd.bitcast(F32), maskf[:, :].bitcast(F32)).then_inc(mask_dram, 16)
            sp.wait_ge(mask_dram, 16)

            sp.wait_ge(zrow_done, 2)
            sp.dma_start(xd[SPARE:SPARE + TB, :].rearrange("(p n) w -> p n w", p=P), zrows[:, :, :]).then_inc(spare_done, 16)

            def slot(s, n):
                if n in WSLOTS:
                    e = WSLOTS[n]
                    if e >= 1:
                        sp.wait_ge(wsplit, 2 * e)
                    sp.dma_start(hid[:, 0, :], W1[e]).then_inc(wraw_in, 16)
                    sp.dma_start(hid[:, 1, :].rearrange("p (c n) -> p c n", c=HC),
                                 W2[e].rearrange("(c p) n -> p c n", p=P)).then_inc(wraw_in, 16)
                if exists(n, 2):
                    c = s + 2
                    if n is None or n >= 0:
                        sp.wait_ge(w_full, s.count(12, 4))
                    if n is not None and n < 0:
                        sp.wait_ge(prep, 1)
                    sp.dma_start(augx[c.parity][2:3, :].bitcast(F32).rearrange("a (b k) -> a b k", b=2),
                                 maskd.bitcast(F32)[bass.ds(c.count(2), 2), :].rearrange("(a b) k -> a b k", a=1)).then_inc(mask_row[c.parity], 16)
                if exists(n, 3) and n != -2:
                    sp.wait_ge(tx_full, s.count(1, 2))
                    load(s + 3)
                if exists(n, 1):
                    c = s + 1
                    for ready, dense, blocks, done in ((2, ks, kb, kblk), (4, qs, qb, qblk)):
                        sp.wait_ge(w_free, c.count(12, ready))
                        if n is not None and n < 1:
                            sp.wait_ge(pool_done, 4)
                        for j in range(J):
                            src, dst = (x[c.parity][R * j:R * j + R] for x in (dense, blocks))
                            if blocks is qb:
                                src, dst = src.rearrange("p b g q -> p (b g) q"), dst.rearrange("p b g j q -> p (b g) j q")
                            sp.dma_start(dst[:, :, j, :].bitcast(F32), src.bitcast(F32)).then_inc(done[c.parity], 16)
                    sp.wait_ge(nm_split, c.count(2, 2))
                    sp.wait_ge(qblk[c.parity], c.uses(64))
                    for j in range(J):
                        for half in range(2):
                            row = R * j + MHI + half
                            sp.dma_start(qb[c.parity][row:row + 1].rearrange("a b g j q -> a (b g) j q")[:, :, j, :].bitcast(F32),
                                         negm[c.parity][8 * j:8 * j + 8, half, :].bitcast(F32)).then_inc(mrow[c.parity], 16)

                if n in WSLOTS:
                    sp.wait_ge(wsplit, 2 * (WSLOTS[n] + 1))
                    sp.dma_start(wd[WSLOTS[n]].bitcast(F32), wsp[:].rearrange("p k w n -> p (k w n)").bitcast(F32)).then_inc(wsave, 16)

            slots(sp, slot)
            sp.wait_ge(tables, 1)
            for e in range(E):
                row = sp.value_load(tab_t[0:1, e:e + 1], min_val=0, max_val=SPARE - TB)
                sp.dma_start(xd[bass.ds(row, TB), :].rearrange("(p n) w -> p n w", p=P), zrows[:, :, :]).then_inc(tail_done, 16)
            for k in range(2):
                sp.wait_ge(scat[k], 64 * (NCH // 2))
            sp.wait_ge(wsave, 16 * E)
            sp.wait_ge(tail_done, 16 * E)
            sp.wait_ge(spare_done, 16)

            def tile(t, n):
                if n == NT:
                    return
                k = t.parity
                e = sp.value_load(tab_e[0:1, bass.ds(t.count(1), 1)], min_val=0, max_val=E - 1)
                row = sp.value_load(tab_r[0:1, bass.ds(t.count(1), 1)], min_val=0, max_val=SPARE)
                if n is None or n >= 2:
                    sp.wait_ge(xt_full, t.count(1, -1))
                    sp.wait_ge(id_done, t.count(1, -1))
                sp.dma_start(xrow[k][:, :, :], xd[bass.ds(row, TB), :].rearrange("(p n) w -> p n w", p=P)).then_inc(x_tile[k], 16)
                if n is None or n >= 2:
                    sp.wait_ge(yt_full, t.count(1, -1))
                    sp.wait_ge(yt_taken, t.count(1, -1))
                sp.dma_start(wtile[k][:].rearrange("p k w n -> p (k w n)").bitcast(F32),
                             wd.bitcast(F32)[bass.ds(e, 1)].rearrange("a p n -> (a p) n")).then_inc(w_tile[k], 16)
                sp.dma_start(btile[k][:, :], bsb[:, bass.ds(e, 1), :].rearrange("p a c -> p (a c)")).then_inc(w_tile[k], 16)

            tiles(sp, tile)

            NQ = B // TN
            for k in range(2):
                last = NT - 1 - (NT - 1 - k) % 2
                sp.wait_ge(y_out[k], 64 * (last // 2 + 1))

            def load_y(q):
                k = q.parity
                for i in range(2):
                    sp.dma_start(yin[i][k][:, :, :],
                                 yd[bass.ds(q.count(TB, i * NTOK), TB), :].rearrange("(b t) d -> t b d", t=P)).then_inc(y_in[k], 16)

            def store(q):
                sp.wait_ge(fin_b, q.count(1, 1))
                sp.dma_start(out[bass.ds(q.count(TN), TN), :, :].rearrange("b s d -> s b d"),
                             xres[:, bass.ds(q.count(TN), TN), :]).then_inc(out_done, 16)

            load_y(At(0, 0))
            load_y(At(0, 1))
            with sp.Fori(0, NQ // 2 - 1) as pair:
                for k in range(2):
                    store(At(pair, k))
                    load_y(At(pair, k) + 2)
            store(At(NQ // 2 - 1, 0))
            store(At(NQ // 2 - 1, 1))
            sp.wait_ge(out_done, 16 * NQ)

        @block.gpsimd
        def _(pool):
            g = nc.gpsimd
            g.memset(ident[:, :], 0.0).then_inc(ident_done, 1)
            pool.wait_ge(ident_done, 1)
            g.affine_select(out=ident[:, :], in_=ident[:, :], compare_op=ALU.not_equal, fill=1.0, base=0,
                            pattern=[[-1, P]], channel_multiplier=1).then_inc(ident_done, 1)
            for k in range(2):
                g.memset(kb[k][:, :, :, :].bitcast(F32), 0.0).then_inc(pool_done, 1)
                g.memset(qb[k][:].bitcast(F32), 0.0).then_inc(pool_done, 1)

            g.memset(trif[:, :], 1.0).then_inc(kept, 1)
            pool.wait_ge(kept, 1)
            g.affine_select(out=trif[:, :], in_=trif[:, :], compare_op=ALU.is_gt, fill=0.0, base=0,
                            pattern=[[1, P]], channel_multiplier=-1).then_inc(kept, 1)
            g.memset(zrows[:, :, :], 0.0).then_inc(zrow_done, 1)
            pool.wait_ge(zrow_done, 1)
            g.memset(zrows[:, :, D:D + 1].bitcast(I32), NOWHERE).then_inc(zrow_done, 1)
            for k in range(2):
                g.memset(rows[k][:, :, :, D:ROW], 0.0).then_inc(kept, 1)
            g.iota(eidx[:, :], [[1, E]], base=0, channel_multiplier=0, allow_small_or_imprecise_dtypes=True).then_inc(kept, 1)
            g.iota(region[:, :], [[REGION, E]], base=0, channel_multiplier=0, allow_small_or_imprecise_dtypes=True).then_inc(kept, 1)
            g.iota(idf[:, :], [[S, 2], [NTOK, 2]], base=0, channel_multiplier=1, allow_small_or_imprecise_dtypes=True).then_inc(kept, 1)
            g.iota(thr[:], [[0, E], [TB, NTOK // TB]], base=0, channel_multiplier=0, allow_small_or_imprecise_dtypes=True).then_inc(kept, 1)
            g.iota(tix[:], [[1, NT], [0, E]], base=0, channel_multiplier=0, allow_small_or_imprecise_dtypes=True).then_inc(kept, 1)
            pool.wait_ge(kept, 9)

            def slot(s, n):
                if n in WSLOTS:
                    e = WSLOTS[n]
                    pool.wait_ge(wraw_in, 32 * (e + 1))
                    if e >= 1:
                        pool.wait_ge(wsave, 16 * e)
                    g.tensor_scalar(wsp[:, 0], hid[:], 1.0, 0.0, ALU.mult, ALU.add).then_inc(wsplit, 1)
                    pool.wait_ge(wsplit, 2 * e + 1)
                    g.tensor_tensor(wsp[:, 1], hid[:], wsp[:, 0], ALU.subtract).then_inc(wsplit, 1)
                if exists(n, 2):
                    c = s + 2
                    k = c.parity
                    pool.wait_ge(tx_taken, c.count(1, 1))
                    if n is None or n >= 0:
                        alone(pool, w_full, s.count(12, 4))
                    g.tensor_scalar(xcTh[k][:, :], xcT[k][:, :], 1.0, 0.0, ALU.mult, ALU.add).then_inc(hi_done, 1)
                    alone(pool, hi_done, c.count(1, 1))
                    g.tensor_tensor(xcTl[k][:, :], xcT[k][:, :], xcTh[k][:, :], ALU.subtract).then_inc(hl_done, 1)
                if exists(n, 2):
                    if n == -2:
                        pool.wait_ge(w_in2, 48)
                    alone(pool, ln_done, c.count(1, 1))
                    for b in range(2):
                        xb = xres[:, bass.ds(c.count(2, b), 1), :]
                        last = g.tensor_tensor(xb, xb, bob[:, :].rearrange("p (a d) -> p a d", a=1), ALU.add)
                    last.then_inc(xbo_done, 1)
                if exists(n, -2):
                    r = s + -2
                    alone(pool, pos_done, r.count(1, 1))
                    for bk in range(4):
                        g.indirect_dma_start(xd, bass.IndirectOffsetOnAxis(ap=posi[r.parity][:, bk:bk + 1], axis=0),
                                             rows[r.parity][:, bk // 2, bk % 2, :], None,
                                             bounds_check=SPARE - 1, oob_is_err=False).then_inc(scat[r.parity], 16)
                if exists(n, -1):
                    r = s + -1
                    alone(pool, ln_done, r.count(1, 4))
                    rw = rows[r.parity]
                    g.tensor_scalar(rw[:, :, 1, 0:D], rw[:, :, 0, 0:D], 1.0, 0.0, ALU.mult, ALU.add).then_inc(rows2, 1)
                    g.tensor_scalar(rw[:, :, :, D:D + 1].bitcast(I32).rearrange("p b k a -> p (b k a)"), idf[:, :], 1.0, 0.0, ALU.mult, ALU.add).then_inc(rows2, 1)
                    alone(pool, rows2, r.count(3, 2))
                    g.tensor_scalar(idf[:, :], idf[:, :], 1.0, float(N2), ALU.mult, ALU.add).then_inc(rows2, 1)
                    alone(pool, rows2, r.count(3, 3))

            slots(pool, slot)

            def scatter(t):
                k = t.parity
                alone(pool, yr_taken, t.count(1, 1))
                for j in range(TN):
                    g.indirect_dma_start(yd, bass.IndirectOffsetOnAxis(ap=idt[k][:, j:j + 1], axis=0), yrow[k][:, j, :], None,
                                         bounds_check=2 * NTOK - 1, oob_is_err=False).then_inc(y_out[k], 16)

            def tile(t, n):
                k = t.parity
                if n != NT:
                    alone(pool, x_tile[k], t.uses(16))
                    if n is None or n >= 2:
                        alone(pool, y_out[k], t.uses(64, -64))
                    g.tensor_copy(idt[k][:, :], xrow[k][:, :, D:D + 1].bitcast(I32).rearrange("p n a -> p (n a)")).then_inc(id_done, 1)
                if n != 0:
                    if n != NT:
                        alone(pool, id_done, t.count(1, 1))
                    scatter(t + -1)

            tiles(pool, tile)

        @block.vector
        def _(dve):
            v = nc.vector
            chain = [0]

            def link(ins):
                chain[0] += 1
                ins.then_inc(dve_chain, 1)
                dve.wait_ge(dve_chain, chain[0])

            def put(ins):
                chain[0] += 1
                ins.then_inc(dve_chain, 1)

            put(v.memset(wst[:], 0.0))
            for k in range(4):
                put(v.memset(bst[k][:], 0.0))
            put(v.memset(mv[:], 1.0))
            put(v.memset(stats[:], 1.0))
            put(v.memset(ones2[:].bitcast(F32), 1.0))
            for k in range(2):
                put(v.memset(augx[k][:].bitcast(F32), 1.0))
                link(v.memset(vs[k][:], 0.0))
                put(v.memset(vs[k][:, :, :, DH:DH + 1], 1.0))
            put(v.memset(bst[2][:, :, :, MSK:MSK + 1], MASKED))
            put(v.memset(bst[0][:, :, :, MSK:MSK + 1], 1.0))
            put(v.memset(bst[1][:, :, :, MHI:MLO + 1], 1.0))
            dve.wait_ge(mask_in, 16)
            v.tensor_copy(maskf[:, :], masku[:, :]).then_inc(mask_f, 1)
            dve.wait_ge(ident_done, 2)
            idv = ident[:, :].rearrange("p (j r) -> p j r", j=J)
            for k, r0 in ((0, 16), (1, 8)):
                put(v.tensor_reduce(rowsel[k][:, :], idv[:, :, r0:r0 + 8], op=ALU.add, axis=AX.XY))
            dve.wait_ge(w_in, 7 * 16)
            link(v.tensor_scalar(keep[:, :], ident[0:3, 2:3], -1.0, 1.0, ALU.mult, ALU.add))
            for k in range(2):
                bsrc = brow[:, k, :].rearrange("a (g j d) -> a (g j) d", g=G, j=J)
                for c in range(3):
                    link(v.tensor_copy(bst[k][:].rearrange("a g j r -> a (g j) r")[:, :, 8 * c:8 * c + 8], bsrc))
            for k in range(2):
                link(v.tensor_scalar(bst[k][:], bst[k][:], keep[:, 0:1], None, ALU.mult))
                if k == 1:
                    link(v.scalar_tensor_tensor(bst[3][:], bst[2][:], ident[0:3, 2:3], bst[1][:], ALU.mult, ALU.add))
                src = bst[3] if k == 1 else bst[0]
                link(v.tensor_scalar(augw[:], src[:], ident[0:3, 1:2], None, ALU.mult))
                link(v.tensor_tensor(aug[k][:], src[:], augw[:], ALU.subtract))
            for raw, halves in ((1, wk3), (0, wq3)):
                wsrc = wraw[:, raw, :].rearrange("p (h d) -> p h d", h=H)
                for c in range(3):
                    link(v.tensor_copy(wst[:].rearrange("p g j r -> p (g j) r")[:, :, 8 * c:8 * c + 8], wsrc))
                link(v.tensor_copy(halves[0][:], wst[:]))
                link(v.tensor_tensor(halves[1][:], wst[:], halves[0][:], ALU.subtract))
            dve.wait_ge(wr_T, 2)
            link(v.tensor_copy(bsb[:, :, 0:HC], small[0][:, E:E + E * HC].rearrange("p (e c) -> p e c", e=E)))
            link(v.tensor_copy(bsb[:, :, HC:HC + 1], small[0][:, E + E * HC:2 * E + E * HC].rearrange("p (e a) -> p e a", a=1)))
            v.tensor_copy(wrT[:, :], small[0][:, 0:E]).then_inc(prep, 1)
            dve.wait_ge(w_in2, 48)
            dve.wait_ge(kept, 9)
            link(v.tensor_copy(tri[:, :], trif[:, :]))
            link(v.memset(ones[:, :], 1.0))
            link(v.memset(before[:, :], 0.0))

            def normalise(m, first):
                s, k = m
                src = small[0][:, :].rearrange("p (h r) -> p h r", h=H)
                dve.wait_ge(ott_full, s.count(2, k + 1))
                if not first:
                    dve.wait_ge(on_done, s.count(2, k))
                v.reciprocal(rden[:].rearrange("p g j -> p (g j)"), src[:, :, DH]).then_inc(rc_done, 1)
                dve.wait_ge(rc_done, s.count(2, k + 1))
                if not first:
                    dve.wait_ge(ont_full, s.count(2, k))
                v.tensor_tensor(on[:], src[:, :, 0:DH],
                                rden[:].rearrange("p g (j a) -> p (g j) a", a=1).to_broadcast([P, H, DH]),
                                ALU.mult).then_inc(on_done, 1)

            def residual(m):
                s, k = m
                dve.wait_ge(wo_full, s.count(2, k + 1))
                dve.wait_ge(xbo_done, s.count(1, 0 if k < 0 else 1))
                xb = xres[:, bass.ds(s.count(2, k), 1), :].rearrange("p a d -> p (a d)")
                v.tensor_tensor(xb, small[1][:, 0:D], xb, ALU.add).then_inc(x1_done, 1)

            def slot(s, n):
                c = s + 1
                k = c.parity
                LN = 7
                lnbase = (s + 2).count(LN)
                if exists(n, 1) and (n is None or n >= 1):
                    dve.wait_ge(b_full, s.count(8))
                    dve.wait_ge(pv_done, s.count(8))

                def unsplit(u):
                    dve.wait_ge(w_part, c.count(4, u + 1))
                    gs = slice(2 * (u % 2), 2 * (u % 2) + 2)
                    if u < 2:
                        views = ks[k][:, gs, :], wide[u % 3][:, 0:2 * K2], part[u % 2][:, 0:2 * K2]
                        views = (views[0], *(w.rearrange("p (g n) -> p g n", g=2) for w in views[1:]))
                    else:
                        views = qs[k][:, :, gs, :], *(w[:, 0:2 * N2].rearrange("p (g b q) -> p b g q", g=2, b=2)
                                                      for w in (wide[u % 3], part[u % 2]))
                    v.tensor_tensor(*views, ALU.subtract).then_inc(w_free, 1)

                if exists(n, 1):
                    unsplit(0)
                    unsplit(1)
                if exists(n, -1):
                    normalise((s, -1), False)
                if exists(n, 1):
                    unsplit(2)
                    unsplit(3)
                if exists(n, -1):
                    residual((s, -1))
                if exists(n, 1):
                    dve.wait_ge(v_full, c.count(1, 1))
                    v.tensor_tensor(vs[k][:, :, :, 0:DH].rearrange("p b h d -> p (b h) d"),
                                    small[0][0:KL, 0:2 * D].rearrange("p (b h d) -> p (b h) d", b=2, h=H),
                                    bvb[0:KL].rearrange("p b (h d) -> p (b h) d", h=H), ALU.add).then_inc(v_taken, 1)
                todo = []
                if exists(n, 2):
                    f = s + 2
                    dve.wait_ge(x_in[f.parity], f.uses(16))
                    todo += [(b, xres[:, bass.ds(f.count(2, b), 1), :]) for b in range(2)]
                if exists(n, -1):
                    dve.wait_ge(x1_done, s.count(2))
                    todo += [(2 + b, xres[:, bass.ds(s.count(2, b - 2), 1), :]) for b in range(2)]
                if todo:
                    if n != -2:
                        dve.wait_ge(ln_done, (s + 2).count(1))
                    for b, src in todo:
                        last = v.bn_stats(stats[:, b, :], src.rearrange("p a d -> p (a d)"))
                    last.then_inc(ln_chain, 1)
                    alone(dve, ln_chain, (s + 2).count(LN, 1))
                    for b, src in todo:
                        last = v.bn_aggr(mv[:, b, :], stats[:, b, :])
                    last.then_inc(ln_chain, 1)
                    dve.wait_ge(ln_chain, (s + 2).count(LN, 2))
                    v.tensor_scalar(ve[:, :], mv[:, :, 1], EPS, None, ALU.add).then_inc(ln_chain, 1)

                def best(u):
                    b, gg = divmod(u, G)
                    dve.wait_ge(w_full, c.count(12, 5 + u))
                    v.tensor_reduce(mx[:, :, b, gg], wide[(4 + u) % 3][:, 0:J * KL].rearrange("p (j k) -> p j k", j=J),
                                    op=ALU.max, axis=AX.X).then_inc(w_free, 1)

                if exists(n, 1):
                    if n is None or n >= 0:
                        dve.wait_ge(nm_full, c.count(1))
                    best(0)
                    best(1)
                if todo:
                    dve.wait_ge(ln_act, (s + 2).count(1, 1))
                    v.tensor_tensor(y1[:, :], y0[:, :], y0[:, :], ALU.mult).then_inc(ln_chain, 1)
                    dve.wait_ge(ln_chain, (s + 2).count(LN, 4))
                    v.tensor_tensor(y2[:, :], y1[:, :], ve[:, :], ALU.mult).then_inc(ln_chain, 1)
                    dve.wait_ge(ln_chain, (s + 2).count(LN, 5))
                    v.tensor_scalar(y3[:, :], y2[:, :], -0.5, 1.5, ALU.mult, ALU.add).then_inc(ln_chain, 1)
                    dve.wait_ge(ln_chain, (s + 2).count(LN, 6))
                    v.tensor_tensor(rstd[:, :], y3[:, :], y0[:, :], ALU.mult).then_inc(ln_chain, 1)
                    dve.wait_ge(ln_chain, (s + 2).count(LN, 7))
                    if exists(n, 2) and (n is None or n >= 0):
                        dve.wait_ge(tx_full, s.count(1, 1))
                    if exists(n, -3):
                        r = s + -1
                        dve.wait_ge(scat[r.parity], r.uses(64, -64))
                        dve.wait_ge(rl_full, s.count(1, -1))
                    for b, src in todo:
                        dst = xn[s.parity][:, b, :] if b < 2 else rows[1 - s.parity][:, b - 2, 0, 0:D]
                        last = v.tensor_scalar(dst, src.rearrange("p a d -> p (a d)"), mv[:, b, 0:1], rstd[:, b:b + 1],
                                               ALU.subtract, ALU.mult)
                    last.then_inc(ln_done, 1)
                if exists(n, -2):
                    r = s + -2
                    C = 3
                    dve.wait_ge(pos_full, r.count(1, 1))
                    v.tensor_tensor(place[:], small[1][:, 16:16 + 2 * E].rearrange("p (b e) -> p b e", b=2),
                                    region[:].rearrange("p (a e) -> p a e", a=1).to_broadcast([P, 2, E]), ALU.add).then_inc(pos_taken, 1)
                    v.tensor_tensor(before[:, :], before[:, :], taken2[:, :], ALU.add).then_inc(pos_chain, 1)
                    dve.wait_ge(pos_taken, r.count(1, 1))
                    for b in range(2):
                        last = v.tensor_tensor(placed[:, 2 * b:2 * b + 2, :], hot[:, b, :, :],
                                               place[:, b:b + 1, :].to_broadcast([P, 2, E]), ALU.mult)
                    last.then_inc(pos_chain, 1)
                    dve.wait_ge(pos_chain, r.count(C, 2))
                    v.tensor_reduce(posf[:, :], placed[:], op=ALU.add, axis=AX.X).then_inc(pos_chain, 1)
                    dve.wait_ge(pos_chain, r.count(C, 3))
                    if exists(n, -4):
                        dve.wait_ge(scat[r.parity], r.uses(64, -64))
                    v.tensor_copy(posi[r.parity][:, :], posf[:, :]).then_inc(pos_done, 1)
                if exists(n, 1):
                    best(2)
                    best(3)
                if exists(n, 0):
                    normalise((s, 0), n == 0)
                if exists(n, 1):
                    for u in range(4, 8):
                        best(u)
                if exists(n, 0):
                    residual((s, 0))
                if exists(n, -1):
                    alone(dve, rl_full, s.count(1))
                    lg = small[1][:, 0:2 * E].rearrange("p (b e) -> p b e", b=2)
                    if n != 1:
                        alone(dve, routed, s.count(1, -1))
                    for b in range(2):
                        last = v.max(top[:, b, :], lg[:, b, :])
                    last.then_inc(top_max, 1)
                    alone(dve, top_max, s.count(1))
                    for b in range(2):
                        last = v.max_index(tidx[:, b, :], top[:, b, :], lg[:, b, :])
                    last.then_inc(rl_taken, 1)
                    v.tensor_tensor(topd[:], top[:], top[:, :, 0:1].to_broadcast([P, 2, E]), ALU.subtract).then_inc(top_sub, 1)
                if exists(n, 1):
                    dve.wait_ge(nm_full, c.count(1, 1))
                    nsrc = small[0][0:J * G * 2, 0:S]
                    v.tensor_scalar(negm[k][:, 0, :], nsrc, -1.0, None, ALU.mult).then_inc(nm_split, 1)
                    dve.wait_ge(nm_split, c.count(2, 1))
                    v.scalar_tensor_tensor(negm[k][:, 1, :], nsrc, -1.0, negm[k][:, 0, :], ALU.mult, ALU.subtract).then_inc(nm_split, 1)
                if exists(n, -1):
                    dve.wait_ge(rl_taken, s.count(1))
                    v.tensor_copy(pick[:, :].rearrange("p (b k) -> p b k", b=2), tidx[:, :, 0:2]).then_inc(top_chain, 1)
                    dve.wait_ge(top_exp, s.count(1))
                    v.tensor_reduce(tsum[:, :], tope[:], op=ALU.add, axis=AX.X).then_inc(top_chain, 1)
                    dve.wait_ge(top_chain, s.count(6, -4))
                    v.reciprocal(tinv[:, :], tsum[:, :]).then_inc(top_chain, 1)
                    dve.wait_ge(top_chain, s.count(6, -3))
                    v.tensor_tensor(prob[:, bass.ds(s.count(2, -2), 2), :], tope[:, :, 0:2],
                                    tinv[:].rearrange("p (b a) -> p b a", a=1).to_broadcast([P, 2, 2]),
                                    ALU.mult).then_inc(routed, 1)
                    if exists(n, -2):
                        dve.wait_ge(pos_done, s.count(1, -1))
                        dve.wait_ge(pos_chain, s.count(3, -3))
                    for b in range(2):
                        last = v.tensor_tensor(hot[:, b], pick[:, 2 * b:2 * b + 2].rearrange("p (k a) -> p k a", a=1).to_broadcast([P, 2, E]),
                                               eidx[:].rearrange("p (a e) -> p a e", a=1).to_broadcast([P, 2, E]), ALU.is_equal)
                    last.then_inc(top_chain, 1)
                    dve.wait_ge(top_chain, s.count(6, -2))
                    v.tensor_tensor(taken[:], hot[:, :, 0, :], hot[:, :, 1, :], ALU.add).then_inc(top_chain, 1)
                    dve.wait_ge(top_chain, s.count(6, -1))
                    v.tensor_tensor(taken2[:, :], taken[:, 0, :], taken[:, 1, :], ALU.add).then_inc(top_chain, 1)

            slots(dve, slot)

            dve.wait_ge(cnt_full, 1)
            link(v.tensor_copy(cnt[:, :], small[0][0:1, 0:E]))
            link(v.tensor_tensor(over[:], cnt[:].rearrange("a (e j) -> a e j", j=1).to_broadcast([1, E, NTOK // TB]), thr[:], ALU.is_gt))
            link(v.tensor_reduce(cum[0][:, :], over[:], op=ALU.add, axis=AX.X))
            for k, step in enumerate((1, 2, 4)):
                old, new = cum[k], cum[k + 1]
                link(v.tensor_copy(new[:, 0:step], old[:, 0:step]))
                link(v.tensor_tensor(new[:, step:E], old[:, step:E], old[:, 0:E - step], ALU.add))
            link(v.tensor_tensor(past[:], tix[:], cum[3][:].rearrange("a (j e) -> a j e", j=1).to_broadcast([1, NT, E]), ALU.is_ge))
            link(v.tensor_reduce(tile_e[:, :], past[:], op=ALU.add, axis=AX.X))
            link(v.tensor_tensor(pastn[:], past[:], cum[0][:].rearrange("a (j e) -> a j e", j=1).to_broadcast([1, NT, E]), ALU.mult))
            link(v.tensor_reduce(tile_s[:, :], pastn[:], op=ALU.add, axis=AX.X))
            link(v.tensor_tensor(tile_r[0][:, :], tix[:, :, 0], tile_s[:, :], ALU.subtract))
            link(v.tensor_scalar(tile_r[1][:, :], tile_e[:, :], float(REGION), None, ALU.mult))
            link(v.scalar_tensor_tensor(tile_r[2][:, :], tile_r[0][:, :], float(TB), tile_r[1][:, :], ALU.mult, ALU.add))
            link(v.tensor_scalar(tab_r[:, :], tile_r[2][:, :], float(SPARE), None, ALU.min))
            link(v.tensor_scalar(tab_e[:, :], tile_e[:, :], float(E - 1), None, ALU.min))
            v.tensor_tensor(tab_t[:, :], cnt[:, :], region[0:1, :], ALU.add).then_inc(tables, 1)

            def lower(t, c):
                dve.wait_ge(h_val, t.count(HC, c + 1))
                v.tensor_tensor(hhl[:, 1, c, :], hid[:, c % 2, :], hhl[:, 0, c, :], ALU.subtract).then_inc(h_lo, 1)

            def lower_x(t):
                dve.wait_ge(xt_hi, t.count(1, 1))
                v.tensor_tensor(xTl[:, :], bank[4][:, :], xTh[:, :], ALU.subtract).then_inc(xt_lo, 1)

            def rows_out(t, first):
                dve.wait_ge(yr_full, t.count(1, 1))
                if not first:
                    dve.wait_ge(y_out[t.parity], t.uses(64, -64))
                v.tensor_copy(yrow[t.parity][:].rearrange("p n d -> p (n d)"), bank[6][:, :]).then_inc(yr_taken, 1)

            def tile(t, n):
                if n == 0:
                    lower_x(t)
                for c in range(HC):
                    if n != NT:
                        lower(t, c)
                if n is None or n + 1 < NT:
                    lower_x(t + 1)
                if n != 0:
                    rows_out(t + -1, n is not None and n <= 2)

            tiles(dve, tile)

            def combine(q):
                dve.wait_ge(y_in[q.parity], q.uses(32))
                for i, done in enumerate((fin_a, fin_b)):
                    if i:
                        dve.wait_ge(fin_a, q.count(1, 1))
                    for b in range(TN):
                        xb = xres[:, bass.ds(q.count(TN, b), 1), :].rearrange("p a d -> p (a d)")
                        last = v.scalar_tensor_tensor(xb, yin[i][q.parity][:, b, :],
                                                      prob[:, bass.ds(q.count(TN, b), 1), i:i + 1].rearrange("p a k -> p (a k)"),
                                                      xb, ALU.mult, ALU.add)
                    last.then_inc(done, 1)

            with dve.Fori(0, B // TN // 2) as pair:
                for k in range(2):
                    combine(At(pair, k))

        @block.scalar
        def _(act):
            a = nc.scalar

            def slot(s, n):
                c = s + 1
                if exists(n, 1):
                    for u in range(4):
                        width = (K2, N2)[u // 2]
                        if n == -1 and u == 0:
                            act.wait_ge(prep, 1)
                        act.wait_ge(w_full, c.count(12, u + 1))
                        if u >= 2:
                            act.wait_ge(w_free, c.count(12, u - 1))
                        a.activation(part[u % 2][:, 0:2 * width], wide[u % 3][:, 0:2 * width],
                                     ACT.Identity, scale=rowsel[1 - u // 2][:, 0:1]).then_inc(w_part, 1)
                        if u == 2 and exists(n, -1):
                            take_on(s, -1)
                elif exists(n, -1):
                    take_on(s, -1)
                for t in range(8):
                    if t == 3 and n != NCH + 1:
                        act.wait_ge(ln_chain, (s + 2).count(7, 3))
                        a.activation(lnv[:, :], ve[:, :], ACT.Ln).then_inc(ln_log, 1)
                        act.wait_ge(ln_log, (s + 2).count(1, 1))
                        a.activation(y0[:, :], lnv[:, :], ACT.Exp, scale=-0.5).then_inc(ln_act, 1)
                    if exists(n, 0):
                        act.wait_ge(b_full, s.count(8, t + 1))
                        if t >= NP:
                            act.wait_ge(pv_done, s.count(8, t - NP + 1))
                        elif n != 0:
                            act.wait_ge(pv_done, s.count(8, t - NP + 1))
                        a.activation(pt[t % NP][:].rearrange("p j q -> p (j q)"), scores[t % 2][0:KL, :], ACT.Exp,
                                     scale=SCALE).then_inc(exp_done, 1)
                    if t == 4 and exists(n, 0):
                        take_heads(s, 0, n)
                    if t == 6 and exists(n, 0):
                        take_on(s, 0)
                    if t == 6 and exists(n, -1):
                        act.wait_ge(x2t_full, s.count(1))
                        if n != 1:
                            act.wait_ge(rl_full, s.count(1, -1))
                        a.activation(x2s[:, :], small[0][:, 0:N2], ACT.Copy).then_inc(x2t_taken, 1)
                if exists(n, -1):
                    act.wait_ge(top_sub, s.count(1))
                    a.activation(tope[:].rearrange("p b e -> p (b e)"), topd[:].rearrange("p b e -> p (b e)"), ACT.Exp).then_inc(top_exp, 1)
                if exists(n, 2):
                    f = s + 2
                    act.wait_ge(tx_full, f.count(1, 1))
                    if n is None or n >= 0:
                        act.wait_ge(hl_done, s.count(1, 1))
                        act.wait_ge(v_full, s.count(1, 1))
                    a.activation(xcT[f.parity][:, :], small[1][:, 0:N2 + K2], ACT.Copy).then_inc(tx_taken, 1)
                if exists(n, 0):
                    take_heads(s, 1, n)

            def take_heads(s, b, n):
                act.wait_ge(pv_done, s.count(8, 4 * b + 4))
                if n != 0:
                    act.wait_ge(ott_full, s.count(2, b - 1))
                a.activation(ots[b][:].rearrange("p g q -> p (g q)"), heads[:, :], ACT.Copy).then_inc(ot_taken, 1)

            def take_on(s, k):
                act.wait_ge(ont_full, s.count(2, k + 1))
                if isinstance(s.pair, int) and s.count(2, k) == 0:
                    pass
                else:
                    act.wait_ge(wo_full, s.count(2, k))
                a.activation(onT[:, :], small[1][:, 0:S], ACT.Copy).then_inc(ont_taken, 1)

            slots(act, slot)

            def upper_x(t):
                act.wait_ge(xt_full, t.count(1, 1))
                a.activation(xTh[:, :], bank[4][:, :], ACT.Copy).then_inc(xt_hi, 1)

            def tile(t, n):
                k = t.parity
                if n == 0:
                    upper_x(t)
                if n == NT:
                    return
                act.wait_ge(w_tile[k], t.uses(32))
                for c in range(HC):
                    act.wait_ge(h_full, t.count(HC, c + 1))
                    a.activation(hhl[:, 0, c, :], bank[c][:, :], ACT.Gelu, bias=btile[k][:, c:c + 1]).then_inc(h_hi, 1)
                    if c >= 2:
                        act.wait_ge(h_lo, t.count(HC, c - 1))
                    elif n != 0:
                        act.wait_ge(h_lo, t.count(HC, c - 1))
                    a.activation(hid[:, c % 2, :], bank[c][:, :], ACT.Gelu, bias=btile[k][:, c:c + 1]).then_inc(h_val, 1)
                if n is None or n + 1 < NT:
                    upper_x(t + 1)
                act.wait_ge(yt_full, t.count(1, 1))
                a.activation(yT[:, :], bank[5][:, :], ACT.Identity, bias=btile[k][:, HC:HC + 1]).then_inc(yt_taken, 1)

            tiles(act, tile)

        @block.tensor
        def _(pe):
            t_ = nc.tensor
            pe.wait_ge(ident_done, 2)
            pe.wait_ge(w_in, 7 * 16)
            pe.wait_ge(b_in, 32)
            t_.transpose(small[0][:, 0:E], wrraw[:, :], ident[0:E, 0:E]).then_inc(wr_T, 1)
            nb = E * (HC + 1)
            t_.transpose(small[0][:, E:E + nb], braw[:, :], ident[0:nb, 0:nb]).then_inc(wr_T, 1)
            pe.wait_ge(prep, 1)

            def project(c, u, n):
                k = c.parity
                halves, cols, am = (((wk3, slice(N2, N2 + K2), aug[1]), (wq3, slice(0, N2), aug[0]))[u // 2])
                width = (K2, N2)[u // 2]
                if n != -1:
                    pe.wait_ge(w_free, c.count(12, u - 2))
                elif u == 3:
                    pe.wait_ge(w_free, 1)
                if u == 0:
                    pe.wait_ge(hl_done, c.count(1, 1))
                    pe.wait_ge(mask_row[k], c.uses(16))
                for gg in range(2):
                    g = 2 * (u % 2) + gg
                    dst = wide[u % 3][:, gg * width:(gg + 1) * width]
                    hi, lo = (w[:, g].rearrange("p j r -> p (j r)") for w in halves)
                    t_.matmul(dst, hi, xcTh[k][:, cols], start=True, stop=False)
                    t_.matmul(dst, hi, xcTl[k][:, cols], start=False, stop=False)
                    t_.matmul(dst, lo, xcTh[k][:, cols], start=False, stop=False)
                    if u < 2:
                        last = t_.matmul(dst, am[0:3, g].rearrange("p j r -> p (j r)"), augx[k][0:3, :], start=False, stop=True)
                    else:
                        last = t_.matmul(dst, am[0:2, g].rearrange("p j r -> p (j r)"), ones2[0:2, :], start=False, stop=True)
                last.then_inc(w_full, 1)

            def values(c, n):
                if n == 0:
                    pe.wait_ge(nm_split, 2)
                elif n != -1:
                    pe.wait_ge(on_done, (c + -1).count(2))
                for b in range(2):
                    last = t_.matmul(small[0][0:KL, b * D:(b + 1) * D],
                                     xcT[c.parity][:, N2 + b * KL:N2 + (b + 1) * KL], wraw[:, 2, :], start=True, stop=True)
                last.then_inc(v_full, 1)

            def turn_heads(s, k):
                pe.wait_ge(ot_taken, s.count(2, k + 1))
                for g in range(G):
                    last = t_.transpose(small[0][:, g * P:(g + 1) * P], ots[k % 2][:, g, :], ident[:, :])
                last.then_inc(ott_full, 1)

            def turn_on(s, k):
                pe.wait_ge(on_done, s.count(2, k + 1))
                t_.transpose(small[1][:, 0:S], on[:].rearrange("p h d -> p (h d)"), ident[:, :]).then_inc(ont_full, 1)

            def project_out(s, k):
                pe.wait_ge(ont_taken, s.count(2, k + 1))
                t_.matmul(small[1][:, 0:D], onT[:, :], wraw[:, 3, :], start=True, stop=True).then_inc(wo_full, 1)

            def by_query(c, u, n):
                b, g = divmod(u, G)
                if u == 0:
                    pe.wait_ge(kblk[c.parity], c.uses(64))
                pe.wait_ge(w_free, c.count(12, 4 + max(u - 2, 0)))
                t_.matmul(wide[(4 + u) % 3][:, 0:J * KL].rearrange("p (j k) -> p j k", j=J), qs[c.parity][:, b, g, :],
                          kb[c.parity][:, g, :, b * KL:(b + 1) * KL], start=True, stop=True).then_inc(w_full, 1)

            def by_key(s, t, n):
                b, g = divmod(t, G)
                if t == 0:
                    pe.wait_ge(mrow[s.parity], s.uses(128))
                if n != 0 or t >= 2:
                    pe.wait_ge(exp_done, s.count(8, t - 1))
                t_.matmul(scores[t % 2][0:KL, :].rearrange("p (j q) -> p j q", j=J), ks[s.parity][:, g, b * KL:(b + 1) * KL],
                          qb[s.parity][:, b, g, :, :], start=True, stop=True).then_inc(b_full, 1)

            def weigh(s, t, n):
                b, g = divmod(t, G)
                pe.wait_ge(exp_done, s.count(8, t + 1))
                if g == 0 and not (n == 0 and b == 0):
                    pe.wait_ge(ot_taken, s.count(2, b))
                for j in range(J):
                    last = t_.matmul(heads[R * j:R * j + R, g * S:(g + 1) * S], vs[s.parity][:, b, G * g + j, :],
                                     pt[t % NP][:, j, :], start=True, stop=True, tile_position=(0, R * j))
                last.then_inc(pv_done, 1)

            def slot(s, n):
                c = s + 1
                if exists(n, 1):
                    project(c, 0, n)
                if exists(n, -1):
                    if n == NCH:
                        pe.wait_ge(x2t_taken, NCH - 1)
                    else:
                        pe.wait_ge(nm_split, s.count(2, 2))
                    turn_heads(s, -1)
                if exists(n, 1):
                    project(c, 1, n)
                    project(c, 2, n)
                if exists(n, -1):
                    if n is not None and n >= NCH - 1:
                        pe.wait_ge(rl_taken, n - 1)
                    else:
                        pe.wait_ge(tx_taken, s.count(1, 2))
                    turn_on(s, -1)
                if exists(n, 1):
                    project(c, 3, n)
                    values(c, n)
                if exists(n, -1):
                    project_out(s, -1)
                if exists(n, 0):
                    by_key(s, 0, n)
                    by_key(s, 1, n)
                for t in range(8):
                    if exists(n, 0):
                        weigh(s, t, n)
                        if t < 6:
                            by_key(s, t + 2, n)
                    if exists(n, -2) and t == 2:
                        pe.wait_ge(x1_done, s.count(2, 0) if exists(n, -1) else 2 * NCH)
                        if n == NCH + 1:
                            pe.wait_ge(rl_taken, NCH)
                        pe.wait_ge(top_chain, s.count(6, -6))
                        for b in range(2):
                            dst = small[1][:, 16 + b * E:16 + (b + 1) * E]
                            t_.matmul(dst, tri[:, :], taken[:, b, :], start=True, stop=False)
                            last = t_.matmul(dst, ones[:, :], before[:, :], start=False, stop=b == 0)
                            if b:
                                last = t_.matmul(dst, ones[:, :], taken[:, 0, :], start=False, stop=True)
                        last.then_inc(pos_full, 1)
                    if exists(n, 1) and 2 <= t < 6:
                        by_query(c, 2 * t - 4, n)
                        by_query(c, 2 * t - 3, n)
                    if exists(n, 0) and t == 4:
                        if exists(n, 1):
                            pe.wait_ge(v_taken, c.count(1, 1))
                        else:
                            pe.wait_ge(on_done, s.count(2))
                        turn_heads(s, 0)
                    if exists(n, -2) and t == 5:
                        pe.wait_ge(pos_taken, s.count(1, -1))
                    if exists(n, 0) and t == 5:
                        if n == 0:
                            pe.wait_ge(tx_taken, 2)
                        else:
                            pe.wait_ge(x1_done, s.count(2))
                        turn_on(s, 0)
                    if exists(n, -1) and t == 6:
                        pe.wait_ge(ln_done, s.count(1, 3))
                        pe.wait_ge(on_done, s.count(2, 1 if exists(n, 0) else 0))
                        for b in range(2):
                            last = t_.transpose(small[0][:, b * S:(b + 1) * S], rows[1 - s.parity][:, b, 0, 0:D], ident[:, :])
                        last.then_inc(x2t_full, 1)
                    if exists(n, 0) and t == 6:
                        project_out(s, 0)
                    if exists(n, -1) and t == 7:
                        pe.wait_ge(x2t_taken, s.count(1))
                        pe.wait_ge(x1_done, s.count(2, 1 if exists(n, 0) else 0))
                        for b in range(2):
                            last = t_.matmul(small[1][:, b * E:(b + 1) * E], x2s[:, b * S:(b + 1) * S],
                                             wrT[:, :], start=True, stop=True)
                        last.then_inc(rl_full, 1)
                if exists(n, 1):
                    pe.wait_ge(w_free, c.count(12, 12))
                    if n == -1:
                        pe.wait_ge(v_taken, 1)
                    elif n == 0:
                        pe.wait_ge(on_done, 1)
                    else:
                        pe.wait_ge(x2t_taken, s.count(1))
                    t_.transpose(small[0][0:J * G * 2, 0:S], mx[:].rearrange("p j b g -> p (j b g)"), ident[:, :]).then_inc(nm_full, 1)
                if exists(n, 2):
                    f = s + 2
                    pe.wait_ge(ln_done, f.count(1, 1))
                    pe.wait_ge(ctx_in[f.parity], f.uses(16))
                    if n == -1:
                        pe.wait_ge(tx_taken, 1)
                    elif n == 0:
                        pe.wait_ge(x1_done, 1)
                    elif n != -2:
                        pe.wait_ge(rl_taken, s.count(1))
                    for b in range(2):
                        t_.transpose(small[1][:, b * S:(b + 1) * S], xn[f.parity][:, b, :], ident[:, :])
                    for b in range(2):
                        last = t_.transpose(small[1][:, N2 + b * KL:N2 + (b + 1) * KL], ctxin[f.parity][:, b, :], ident[0:KL, 0:KL])
                    last.then_inc(tx_full, 1)

            slots(pe, slot)

            pe.wait_ge(pos_chain, 3 * NCH)
            pe.wait_ge(x2t_taken, NCH)
            t_.matmul(small[0][:, 0:E], ones[:, :], before[:, :], start=True, stop=True).then_inc(cnt_full, 1)

            def turn_x(t):
                k = t.parity
                pe.wait_ge(x_tile[k], t.uses(16))
                if not isinstance(t.pair, int) or t.count(1) > 0:
                    pe.wait_ge(xt_lo, t.count(1))
                for j in range(TN):
                    last = t_.transpose(bank[4][:, j * P:(j + 1) * P], xrow[k][:, j, 0:D], ident[:, :])
                last.then_inc(xt_full, 1)

            def turn_y(t):
                pe.wait_ge(yt_taken, t.count(1, 1))
                if not isinstance(t.pair, int) or t.count(1) > 0:
                    pe.wait_ge(yr_taken, t.count(1))
                else:
                    pe.wait_ge(tables, 1)
                for j in range(TN):
                    last = t_.transpose(bank[6][:, j * P:(j + 1) * P], yT[:, j * P:(j + 1) * P], ident[:, :])
                last.then_inc(yr_full, 1)

            def tile(t, n):
                k = t.parity
                if n == 0:
                    pe.wait_ge(pv_done, 8 * NCH)
                    turn_x(t)
                if n != NT:
                    pe.wait_ge(xt_lo, t.count(1, 1))
                    pe.wait_ge(w_tile[k], t.uses(32))
                    w = wtile[k]
                    for c in range(HC):
                        if n != 0:
                            pe.wait_ge(h_val, t.count(HC, c - HC + 1))
                        cs = slice(c * P, (c + 1) * P)
                        t_.matmul(bank[c][:, :], w[:, 0, 0, cs], xTh[:, :], start=True, stop=False)
                        t_.matmul(bank[c][:, :], w[:, 0, 0, cs], xTl[:, :], start=False, stop=False)
                        t_.matmul(bank[c][:, :], w[:, 1, 0, cs], xTh[:, :], start=False, stop=True).then_inc(h_full, 1)
                if n is None or n + 1 < NT:
                    turn_x(t + 1)
                if n != 0:
                    turn_y(t + -1)
                if n != NT:
                    for c in range(HC):
                        cs = slice(c * P, (c + 1) * P)
                        pe.wait_ge(h_hi, t.count(HC, c + 1))
                        t_.matmul(bank[5][:, :], w[:, 0, 1, cs], hhl[:, 0, c, :], start=c == 0, stop=False)
                        t_.matmul(bank[5][:, :], w[:, 1, 1, cs], hhl[:, 0, c, :], start=False, stop=False)
                        pe.wait_ge(h_lo, t.count(HC, c + 1))
                        last = t_.matmul(bank[5][:, :], w[:, 0, 1, cs], hhl[:, 1, c, :], start=False, stop=c == HC - 1)
                    last.then_inc(yt_full, 1)

            tiles(pe, tile)


_INS = ['x', 'ctx_1024', 'mask_BxS2_bf0', 'L0_xattn_Wq', 'L0_xattn_bq', 'L0_xattn_Wk', 'L0_xattn_bk', 'L0_xattn_Wv',
        'L0_xattn_bv', 'L0_xattn_Wo', 'L0_xattn_bo', 'L0_ffn_Wr', 'L0_ffn_W1', 'L0_ffn_b1', 'L0_ffn_W2', 'L0_ffn_b2']


def kernel(**inputs):
    import numpy as _np
    import concourse.bacc as _bacc
    from concourse import mybir as _mybir
    from concourse.bass_utils import run_bass_kernel_spmd as _run

    nc = _bacc.Bacc("TRN2", target_bir_lowering=False, num_devices=1)
    arrays, args = {}, []
    for name in _INS:
        a = _np.ascontiguousarray(inputs[name])
        arrays[f"in_{name}"] = a
        args.append(nc.dram_tensor(f"in_{name}", a.shape, _mybir.dt.from_np(a.dtype), kind="ExternalInput").ap())
    out = nc.dram_tensor("out_0", inputs["x"].shape, F32, kind="ExternalOutput").ap()
    moe_attention(nc, *args, out)
    r = _run(nc, [arrays], core_ids=[0])
    return r.results[0]["out_0"]
```

```python
from contextlib import ExitStack

import concourse.bass as bass
from concourse import mybir

F32 = mybir.dt.float32
F32R = mybir.dt.float32r
U32 = mybir.dt.uint32
I32 = mybir.dt.int32
BF16 = mybir.dt.bfloat16
ALU = mybir.AluOpType
ACT = mybir.ActivationFunctionType
AX = mybir.AxisListType

P = 128
MASKED = -float(2**100)
EPS = 1e-5


class At:

    def __init__(self, pair, parity):
        self.pair, self.parity = pair, parity

    def __add__(self, k):
        n = self.parity + k
        return At(self.pair + n // 2 if n // 2 else self.pair, n % 2)

    def count(self, each, more=0):
        return self.pair * (2 * each) + (self.parity * each + more)

    def uses(self, each, more=0):
        return self.pair * each + (each + more)


def moe_attention(nc, x, ctx, mask, Wq, bq, Wk, bk, Wv, bv, Wo, bo, Wr, W1, b1, W2, b2, out):
    B, S, D = x.shape
    KL = ctx.shape[1]
    E, _, HID = W1.shape
    H, DH = 16, 8
    G, J = 4, 4
    R = 32
    HI2, MHI, MLO, MSK = 16, 24, 25, 26
    NCH = B // 2
    HC = HID // P
    TB = 512
    NTOK = B * S
    TN = TB // P
    NT = (2 * NTOK + E * (TB - 1)) // TB
    REGION = NTOK + TB
    SPARE = E * REGION
    ROW = D + 4
    NOWHERE = 1 << 20
    SCALE = float(DH) ** -0.5
    N2 = 2 * S
    K2 = 2 * KL
    KW = 256

    with ExitStack() as st:
        sb = lambda name, shape, dt=F32: st.enter_context(nc.sbuf_tensor(name, shape, dt))
        sem = lambda name: st.enter_context(nc.semaphore(name))
        two = lambda name: [sem(f"{name}{k}") for k in range(2)]

        xres = sb("xres", [P, B, D])
        x2s = sb("x2s", [P, N2])
        ctxin = [sb(f"ctxin{k}", [KL, 2, D]) for k in range(2)]
        xn = [sb(f"xn{k}", [P, 2, D]) for k in range(2)]
        rows = [sb(f"rows{k}", [P, 2, 2, ROW]) for k in range(2)]
        xcT = [sb(f"xcT{k}", [P, N2 + KW]) for k in range(2)]
        xcTh = [sb(f"xcTh{k}", [P, N2 + KW], F32R) for k in range(2)]
        xcTl = [sb(f"xcTl{k}", [P, N2 + KW], F32R) for k in range(2)]
        part = [sb(f"part{k}", [P, 2 * N2], F32R) for k in range(2)]
        qs = [sb(f"qs{k}", [P, 2, G, S], F32R) for k in range(2)]
        ks = [sb(f"ks{k}", [P, G, K2], F32R) for k in range(2)]
        qb = [sb(f"qb{k}", [P, 2, G, J, S], F32R) for k in range(2)]
        kb = [sb(f"kb{k}", [P, G, J, K2], F32R) for k in range(2)]
        vs_all = [sb(f"vs{k}", [P, 2, H, R]) for k in range(2)]
        vs = [v[0:KL] for v in vs_all]
        NP = 4
        pt_all = [sb(f"pt{k}", [P, J, S]) for k in range(NP)]
        pt = [p[0:KL] for p in pt_all]
        mx = sb("mx", [P, 2, G, J])
        negm = [sb(f"negm{k}", [J * G * 2, 2, S], F32R) for k in range(2)]
        ots = [sb(f"ots{k}", [P, G, S]) for k in range(2)]
        rden = sb("rden", [P, G, J])
        on = sb("on", [P, H, DH])
        onT = sb("onT", [P, S])
        wq3 = [sb(f"wq{k}", [P, G, J, R], F32R) for k in ("hi", "lo")]
        wk3 = [sb(f"wk{k}", [P, G, J, R], F32R) for k in ("hi", "lo")]
        wst = ots[1][:].rearrange("p g (j r) -> p g j r", j=J)
        wraw = sb("wraw", [P, 4, D])
        brow = sb("brow", [3, 2, D])
        bst = [p[0:3].rearrange("p g (j r) -> p g j r", j=J) for p in pt_all]
        augw = part[0][0:3, :].rearrange("p (g j r) -> p g j r", g=G, j=J)
        aug = [sb(f"aug{k}", [3, G, J, R], F32R) for k in "qk"]
        augx = [sb(f"augx{k}", [3, KW], F32R) for k in range(2)]
        ones2 = sb("ones2", [2, N2], F32R)
        masku = sb("masku", [B, KL], mask.dtype)
        maskf = sb("maskf", [B, KL], F32R)
        keep = sb("keep", [3, 1])
        rowsel = [sb(f"rowsel{k}", [P, 1]) for k in "qk"]
        bvb = sb("bvb", [P, 2, D])
        bob = sb("bob", [P, D])
        ident = sb("ident", [P, P])
        wrT = sb("wrT", [P, E])
        wrraw = sb("wrraw", [E, D])
        stats = sb("stats", [P, 4, 6])
        mv = sb("mv", [P, 4, 2])
        ve = sb("ve", [P, 4])
        nve = sb("nve", [P, 4])
        vbits = sb("vbits", [P, 4], I32)
        ys = [sb(f"y{k}", [P, 4]) for k in range(2)]
        yy = sb("yy", [P, 4])
        vyy = sb("vyy", [P, 4])
        top = sb("top", [P, 2, 8])
        topd = sb("topd", [P, 2, 8])
        tope = sb("tope", [P, 2, 8])
        tsum = sb("tsum", [P, 2])
        tinv = sb("tinv", [P, 2])
        tidx = sb("tidx", [P, 2, 8], U32)
        prob = sb("prob", [P, B, 2])
        pick = sb("pick", [P, 4])
        hot = sb("hot", [P, 2, 2, E], BF16)
        taken = sb("taken", [P, 2, E], BF16)
        taken2 = sb("taken2", [P, E], BF16)
        before = sb("before", [P, E], BF16)
        tri = sb("tri", [P, P], BF16)
        trif = sb("trif", [P, P])
        ones = sb("ones", [P, P], BF16)
        eidx = sb("eidx", [P, E])
        region = sb("region", [P, E])
        place = sb("place", [P, 2, E])
        placed = sb("placed", [P, 4, E])
        posf = sb("posf", [P, 4])
        posi = [sb(f"posi{k}", [P, 4], I32) for k in range(2)]
        idf = sb("idf", [P, 4])
        zrows = sb("zrows", [P, TN, ROW])
        cnt = sb("cnt", [1, E])
        thr = sb("thr", [1, E, NTOK // TB])
        over = sb("over", [1, E, NTOK // TB])
        cum = [sb(f"cum{k}", [1, E]) for k in range(4)]
        tix = sb("tix", [1, NT, E])
        past = sb("past", [1, NT, E])
        pastn = sb("pastn", [1, NT, E])
        tile_e = sb("tile_e", [1, NT])
        tile_s = sb("tile_s", [1, NT])
        tile_r = [sb(f"tile_r{k}", [1, NT]) for k in range(3)]
        tail_r = sb("tail_r", [1, E])
        tab_e = sb("tab_e", [1, NT], I32)
        tab_r = sb("tab_r", [1, NT], I32)
        tab_t = sb("tab_t", [1, E], I32)
        bsb = sb("bsb", [P, E, HC + 1])
        wsp = sb("wsp", [P, 2, 2, HID], F32R)
        hid = sb("hid", [P, 2, HID])
        braw = hid[0:E * (HC + 1), 0, 0:P]
        btile = [sb(f"btile{k}", [P, HC + 1]) for k in range(2)]
        idt = [sb(f"idt{k}", [P, TN], I32) for k in range(2)]
        flat = lambda t, spec: t[:].rearrange(f"{spec} -> p ({spec[2:]})")
        kflat = [flat(kb[k], "p g j n") for k in range(2)]
        wtile = [kflat[k][:, 0:4 * HID].rearrange("p (k w n) -> p k w n", k=2, w=2) for k in range(2)]
        xTh, xTl = (kflat[0][:, 4 * HID + i * TB:4 * HID + (i + 1) * TB] for i in range(2))
        hhl = flat(qb[0], "p b g j q").rearrange("p (k c t) -> p k c t", k=2, c=HC)
        xrow = [rows[k][:].rearrange("p a b w -> p (a b) w") for k in range(2)]
        yT = flat(ots[0], "p g q")
        yrow = [vs_all[0][:, k].rearrange("p h r -> p (h r)").rearrange("p (n d) -> p n d", n=TN) for k in range(2)]
        yin = [[pt_all[2 * i + k] for k in range(2)] for i in range(2)]

        bank = [st.enter_context(nc.psum_tensor(f"bank{k}", [P, 512], F32)) for k in range(8)]
        wide = bank[0:3]
        scores = bank[3:5]
        heads = bank[5]
        small = bank[6:8]

        w_in, w_in2 = sem("w_in"), sem("w_in2")
        x_in, ctx_in = two("x_in"), two("ctx_in")
        mask_in, mask_f, mask_dram = sem("mask_in"), sem("mask_f"), sem("mask_dram")
        mask_row = two("mask_row")
        ident_done, pool_done = sem("ident_done"), sem("pool_done")
        prep = sem("prep")
        wr_T, prep2 = sem("wr_T"), sem("prep2")
        lnx_done, ln2_done, ln_chain, dve_chain = sem("lnx_done"), sem("ln2_done"), sem("ln_chain"), sem("dve_chain")
        tx_full, tx_taken, hi_done, hl_done, xbo_done = (sem(k) for k in ("tx_full", "tx_taken", "hi_done", "hl_done", "xbo_done"))
        w_full, w_part, w_free = sem("w_full"), sem("w_part"), sem("w_free")
        qblk, kblk, mrow = two("qblk"), two("kblk"), two("mrow")
        v_full, v_taken = sem("v_full"), sem("v_taken")
        mx_done, nm_full, nm_split = sem("mx_done"), sem("nm_full"), sem("nm_split")
        b_full, exp_done, pv_done = sem("b_full"), sem("exp_done"), sem("pv_done")
        ot_taken, ott_full, rc_done, on_done = sem("ot_taken"), sem("ott_full"), sem("rc_done"), sem("on_done")
        ont_full, ont_taken, wo_full, x1_done = sem("ont_full"), sem("ont_taken"), sem("wo_full"), sem("x1_done")
        x2t_full, x2t_taken, rl_full, rl_taken = sem("x2t_full"), sem("x2t_taken"), sem("rl_full"), sem("rl_taken")
        top_max, top_sub, top_exp, top_chain, routed = (sem(k) for k in ("top_max", "top_sub", "top_exp", "top_chain", "routed"))
        pos_full, pos_taken, pos_chain, pos_done, hot_done, kept = (
            sem(k) for k in ("pos_full", "pos_taken", "pos_chain", "pos_done", "hot_done", "kept"))
        scat, rows2, ids_done = two("scat"), sem("rows2"), sem("ids_done")
        zrow_done, spare_done, b_in = sem("zrow_done"), sem("spare_done"), sem("b_in")
        wraw_in, wsplit, wsave = sem("wraw_in"), sem("wsplit"), sem("wsave")
        cnt_full, tables, tail_done = sem("cnt_full"), sem("tables"), sem("tail_done")
        x_tile, w_tile, y_out = two("x_tile"), two("w_tile"), two("y_out")
        xt_full, xt_hi, xt_lo, id_done = sem("xt_full"), sem("xt_hi"), sem("xt_lo"), sem("id_done")
        h_full, h_hi, h_val, h_lo = sem("h_full"), sem("h_hi"), sem("h_val"), sem("h_lo")
        yt_full, yt_taken, yr_full, yr_taken = sem("yt_full"), sem("yt_taken"), sem("yr_full"), sem("yr_taken")
        y_in, fin_a, fin_b = two("y_in"), sem("fin_a"), sem("fin_b")
        xd = nc.dram_tensor("xd", (SPARE + TB, ROW), F32, kind="Internal").ap()
        yd = nc.dram_tensor("yd", (2 * NTOK, D), F32, kind="Internal").ap()
        wd = nc.dram_tensor("wd", (E, P, 4 * HID), F32R, kind="Internal").ap()
        maskd = nc.dram_tensor("maskd", (B, KL), F32R, kind="Internal").ap()
        out_done = sem("out_done")

        def slots(eng, body):
            for s in range(-3, 4):
                body(At(s // 2, s % 2), s)
            with eng.Fori(2, NCH // 2 - 2) as pair:
                body(At(pair, 0), None)
                body(At(pair, 1), None)
            for s in range(NCH - 4, NCH + 2):
                body(At(s // 2, s % 2), s)

        def tiles(eng, body):
            for t in range(4):
                body(At(t // 2, t % 2), t)
            with eng.Fori(2, NT // 2) as pair:
                body(At(pair, 0), None)
                body(At(pair, 1), None)
            for t in range(2 * (NT // 2), NT + 1):
                body(At(t // 2, t % 2), t)

        WSLOTS = {n: e for e, n in enumerate((0, 1, *range(NCH - 4, NCH + 2)))}

        def alone(eng, semaphore, value):
            if not isinstance(value, int):
                value = eng.to_reg(value)
                eng.wait_ge(ident_done, 2)
            eng.wait_ge(semaphore, value)

        def exists(s, back):
            return s is None or 0 <= s + back < NCH

        block = st.enter_context(nc.Block())

        @block.sync
        def _(sp):
            for k, w in enumerate((Wq, Wk, Wv, Wo)):
                sp.dma_start(wraw[:, k, :], w).then_inc(w_in, 16)
            for k, b in enumerate((bq, bk)):
                sp.dma_start(brow[:, k, :], b.rearrange("(a n) -> a n", a=1).to_broadcast([3, D])).then_inc(w_in, 16)
            sp.dma_start(wrraw[:, :], Wr).then_inc(w_in, 16)
            sp.dma_start(masku[:, :], mask).then_inc(mask_in, 16)
            sp.dma_start(braw[0:E * HC, :], b1.rearrange("e (c p) -> (e c) p", p=P)).then_inc(b_in, 16)
            sp.dma_start(braw[E * HC:E * HC + E, :], b2).then_inc(b_in, 16)
            for b in range(2):
                sp.dma_start(bvb[:, b, :], bv.rearrange("(a n) -> a n", a=1).to_broadcast([P, D])).then_inc(w_in2, 16)
            sp.dma_start(bob[:, :], bo.rearrange("(a n) -> a n", a=1).to_broadcast([P, D])).then_inc(w_in2, 16)

            def load_x(c):
                sp.dma_start(xres[:, bass.ds(c.count(2), 2), :],
                             x[bass.ds(c.count(2), 2), :, :].rearrange("b s d -> s b d")).then_inc(x_in[c.parity], 16)

            def load_ctx(c):
                sp.dma_start(ctxin[c.parity][:, :, :],
                             ctx[bass.ds(c.count(2), 2), :, :].rearrange("b s d -> s b d")).then_inc(ctx_in[c.parity], 16)

            load_x(At(0, 0))
            load_ctx(At(0, 0))
            load_ctx(At(0, 1))
            sp.wait_ge(mask_f, 1)
            sp.dma_start(maskd.bitcast(F32), maskf[:, :].bitcast(F32)).then_inc(mask_dram, 16)
            sp.wait_ge(mask_dram, 16)

            sp.wait_ge(zrow_done, 2)
            sp.dma_start(xd[SPARE:SPARE + TB, :].rearrange("(p n) w -> p n w", p=P), zrows[:, :, :]).then_inc(spare_done, 16)

            def slot(s, n):
                if n in WSLOTS:
                    e = WSLOTS[n]
                    if e >= 1:
                        sp.wait_ge(wsplit, 2 * e)
                    sp.dma_start(hid[:, 0, :], W1[e]).then_inc(wraw_in, 16)
                    sp.dma_start(hid[:, 1, :].rearrange("p (c n) -> p c n", c=HC),
                                 W2[e].rearrange("(c p) n -> p c n", p=P)).then_inc(wraw_in, 16)
                if exists(n, 2):
                    c = s + 2
                    if n is None or n >= 0:
                        sp.wait_ge(w_full, s.count(12, 4))
                    if n is not None and n < 0:
                        sp.wait_ge(prep, 1)
                    sp.dma_start(augx[c.parity][2:3, 0:K2].bitcast(F32).rearrange("a (b k) -> a b k", b=2),
                                 maskd.bitcast(F32)[bass.ds(c.count(2), 2), :].rearrange("(a b) k -> a b k", a=1)).then_inc(mask_row[c.parity], 16)
                if exists(n, 4):
                    if exists(n, 2):
                        sp.wait_ge(lnx_done, s.count(1, 3))
                    load_x(s + 4)
                if exists(n, 3) and (n is None or n >= -1):
                    sp.wait_ge(tx_full, s.count(1, 2))
                    load_ctx(s + 3)
                if exists(n, 1):
                    c = s + 1
                    for ready, dense, blocks, done in ((2, ks, kb, kblk), (4, qs, qb, qblk)):
                        sp.wait_ge(w_free, c.count(12, ready))
                        if n is not None and n < 1:
                            sp.wait_ge(pool_done, 4)
                        for j in range(J):
                            src, dst = (x[c.parity][R * j:R * j + R] for x in (dense, blocks))
                            if blocks is qb:
                                src, dst = src.rearrange("p b g q -> p (b g) q"), dst.rearrange("p b g j q -> p (b g) j q")
                            sp.dma_start(dst[:, :, j, :].bitcast(F32), src.bitcast(F32)).then_inc(done[c.parity], 16)
                    sp.wait_ge(nm_split, c.count(2, 2))
                    sp.wait_ge(qblk[c.parity], c.uses(64))
                    for half in range(2):
                        row = MHI + half
                        sp.dma_start(qb[c.parity][row:row + 1].rearrange("a b g j q -> a (b g j) q").bitcast(F32),
                                     negm[c.parity][:, half, :].bitcast(F32)).then_inc(mrow[c.parity], 16)

                if n in WSLOTS:
                    sp.wait_ge(wsplit, 2 * (WSLOTS[n] + 1))
                    sp.dma_start(wd[WSLOTS[n]].bitcast(F32), wsp[:].rearrange("p k w n -> p (k w n)").bitcast(F32)).then_inc(wsave, 16)

            slots(sp, slot)
            sp.wait_ge(tables, 1)
            for e in range(E):
                row = sp.value_load(tab_t[0:1, e:e + 1], min_val=0, max_val=SPARE - TB)
                sp.dma_start(xd[bass.ds(row, TB), :].rearrange("(p n) w -> p n w", p=P), zrows[:, :, :]).then_inc(tail_done, 16)
            for k in range(2):
                sp.wait_ge(scat[k], 64 * (NCH // 2))
            sp.wait_ge(wsave, 16 * E)
            sp.wait_ge(tail_done, 16 * E)
            sp.wait_ge(spare_done, 16)

            def tile(t, n):
                if n == NT:
                    return
                k = t.parity
                e = sp.value_load(tab_e[0:1, bass.ds(t.count(1), 1)], min_val=0, max_val=E - 1)
                row = sp.value_load(tab_r[0:1, bass.ds(t.count(1), 1)], min_val=0, max_val=SPARE)
                if n is None or n >= 2:
                    sp.wait_ge(xt_full, t.count(1, -1))
                    sp.wait_ge(id_done, t.count(1, -1))
                sp.dma_start(xrow[k][:, :, :], xd[bass.ds(row, TB), :].rearrange("(p n) w -> p n w", p=P)).then_inc(x_tile[k], 16)
                if n is None or n >= 2:
                    sp.wait_ge(yt_full, t.count(1, -1))
                    sp.wait_ge(yt_taken, t.count(1, -1))
                sp.dma_start(wtile[k][:].rearrange("p k w n -> p (k w n)").bitcast(F32),
                             wd.bitcast(F32)[bass.ds(e, 1)].rearrange("a p n -> (a p) n")).then_inc(w_tile[k], 16)
                sp.dma_start(btile[k][:, :], bsb[:, bass.ds(e, 1), :].rearrange("p a c -> p (a c)")).then_inc(w_tile[k], 16)

            tiles(sp, tile)

            NQ = B // TN
            for k in range(2):
                last = NT - 1 - (NT - 1 - k) % 2
                sp.wait_ge(y_out[k], 64 * (last // 2 + 1))

            def load_y(q):
                k = q.parity
                for i in range(2):
                    sp.dma_start(yin[i][k][:, :, :],
                                 yd[bass.ds(q.count(TB, i * NTOK), TB), :].rearrange("(b t) d -> t b d", t=P)).then_inc(y_in[k], 16)

            def store(q):
                sp.wait_ge(fin_b, q.count(1, 1))
                sp.dma_start(out[bass.ds(q.count(TN), TN), :, :].rearrange("b s d -> s b d"),
                             xres[:, bass.ds(q.count(TN), TN), :]).then_inc(out_done, 16)

            load_y(At(0, 0))
            load_y(At(0, 1))
            with sp.Fori(0, NQ // 2 - 1) as pair:
                for k in range(2):
                    store(At(pair, k))
                    load_y(At(pair, k) + 2)
            store(At(NQ // 2 - 1, 0))
            store(At(NQ // 2 - 1, 1))
            sp.wait_ge(out_done, 16 * NQ)

        @block.gpsimd
        def _(pool):
            g = nc.gpsimd
            g.memset(ident[:, :], 0.0).then_inc(ident_done, 1)
            pool.wait_ge(ident_done, 1)
            g.affine_select(out=ident[:, :], in_=ident[:, :], compare_op=ALU.not_equal, fill=1.0, base=0,
                            pattern=[[-1, P]], channel_multiplier=1).then_inc(ident_done, 1)
            for k in range(2):
                g.memset(kb[k][:, :, :, :].bitcast(F32), 0.0).then_inc(pool_done, 1)
                g.memset(qb[k][:].bitcast(F32), 0.0).then_inc(pool_done, 1)

            g.memset(trif[:, :], 1.0).then_inc(kept, 1)
            pool.wait_ge(kept, 1)
            g.affine_select(out=trif[:, :], in_=trif[:, :], compare_op=ALU.is_gt, fill=0.0, base=0,
                            pattern=[[1, P]], channel_multiplier=-1).then_inc(kept, 1)
            g.memset(zrows[:, :, :], 0.0).then_inc(zrow_done, 1)
            pool.wait_ge(zrow_done, 1)
            g.memset(zrows[:, :, D:D + 1].bitcast(I32), NOWHERE).then_inc(zrow_done, 1)
            for k in range(2):
                g.memset(rows[k][:, :, :, D:ROW], 0.0).then_inc(kept, 1)
            g.iota(eidx[:, :], [[1, E]], base=0, channel_multiplier=0, allow_small_or_imprecise_dtypes=True).then_inc(kept, 1)
            g.iota(region[:, :], [[REGION, E]], base=0, channel_multiplier=0, allow_small_or_imprecise_dtypes=True).then_inc(kept, 1)
            g.iota(idf[:, :], [[S, 2], [NTOK, 2]], base=0, channel_multiplier=1, allow_small_or_imprecise_dtypes=True).then_inc(kept, 1)
            g.iota(thr[:], [[0, E], [TB, NTOK // TB]], base=0, channel_multiplier=0, allow_small_or_imprecise_dtypes=True).then_inc(kept, 1)
            g.iota(tix[:], [[1, NT], [0, E]], base=0, channel_multiplier=0, allow_small_or_imprecise_dtypes=True).then_inc(kept, 1)
            pool.wait_ge(kept, 9)

            def slot(s, n):
                if n in WSLOTS:
                    e = WSLOTS[n]
                    pool.wait_ge(wraw_in, 32 * (e + 1))
                    if e >= 1:
                        pool.wait_ge(wsave, 16 * e)
                    g.tensor_scalar(wsp[:, 0], hid[:], 1.0, 0.0, ALU.mult, ALU.add).then_inc(wsplit, 1)
                    pool.wait_ge(wsplit, 2 * e + 1)
                    g.tensor_tensor(wsp[:, 1], hid[:], wsp[:, 0], ALU.subtract).then_inc(wsplit, 1)
                if exists(n, 2):
                    c = s + 2
                    if n == -2:
                        pool.wait_ge(w_in2, 48)
                    alone(pool, lnx_done, c.count(1, 1))
                    for b in range(2):
                        xb = xres[:, bass.ds(c.count(2, b), 1), :]
                        last = g.tensor_tensor(xb, xb, bob[:, :].rearrange("p (a d) -> p a d", a=1), ALU.add)
                    last.then_inc(xbo_done, 1)
                if exists(n, 2):
                    k = c.parity
                    pool.wait_ge(tx_taken, c.count(1, 1))
                    if n is None or n >= 0:
                        alone(pool, w_full, s.count(12, 4))
                    g.tensor_scalar(xcTh[k][:, :], xcT[k][:, :], 1.0, 0.0, ALU.mult, ALU.add).then_inc(hi_done, 1)
                    alone(pool, hi_done, c.count(1, 1))
                    g.tensor_tensor(xcTl[k][:, :], xcT[k][:, :], xcTh[k][:, :], ALU.subtract).then_inc(hl_done, 1)
                if exists(n, -1):
                    r = s + -1
                    alone(pool, ln2_done, r.count(1, 1))
                    rw = rows[r.parity]
                    g.tensor_scalar(rw[:, :, 1, 0:D], rw[:, :, 0, 0:D], 1.0, 0.0, ALU.mult, ALU.add).then_inc(rows2, 1)
                    g.tensor_scalar(rw[:, :, :, D:D + 1].bitcast(I32).rearrange("p b k a -> p (b k a)"), idf[:, :], 1.0, 0.0, ALU.mult, ALU.add).then_inc(rows2, 1)
                    alone(pool, rows2, r.count(3, 2))
                    g.tensor_scalar(idf[:, :], idf[:, :], 1.0, float(N2), ALU.mult, ALU.add).then_inc(rows2, 1)
                    alone(pool, rows2, r.count(3, 3))
                if exists(n, -2):
                    r = s + -2
                    alone(pool, pos_done, r.count(1, 1))
                    for bk in range(4):
                        g.indirect_dma_start(xd, bass.IndirectOffsetOnAxis(ap=posi[r.parity][:, bk:bk + 1], axis=0),
                                             rows[r.parity][:, bk // 2, bk % 2, :], None,
                                             bounds_check=SPARE - 1, oob_is_err=False).then_inc(scat[r.parity], 16)

            slots(pool, slot)

            def scatter(t):
                k = t.parity
                alone(pool, yr_taken, t.count(1, 1))
                for j in range(TN):
                    g.indirect_dma_start(yd, bass.IndirectOffsetOnAxis(ap=idt[k][:, j:j + 1], axis=0), yrow[k][:, j, :], None,
                                         bounds_check=2 * NTOK - 1, oob_is_err=False).then_inc(y_out[k], 16)

            def tile(t, n):
                k = t.parity
                if n != NT:
                    alone(pool, x_tile[k], t.uses(16))
                    if n is None or n >= 2:
                        alone(pool, y_out[k], t.uses(64, -64))
                    g.tensor_copy(idt[k][:, :], xrow[k][:, :, D:D + 1].bitcast(I32).rearrange("p n a -> p (n a)")).then_inc(id_done, 1)
                if n != 0:
                    if n != NT:
                        alone(pool, id_done, t.count(1, 1))
                    scatter(t + -1)

            tiles(pool, tile)

        @block.vector
        def _(dve):
            v = nc.vector
            chain = [0]

            def link(ins):
                chain[0] += 1
                ins.then_inc(dve_chain, 1)
                dve.wait_ge(dve_chain, chain[0])

            def put(ins):
                chain[0] += 1
                ins.then_inc(dve_chain, 1)

            put(v.memset(wst[:], 0.0))
            for k in range(4):
                put(v.memset(bst[k][:], 0.0))
            put(v.memset(mv[:], 1.0))
            put(v.memset(stats[:], 1.0))
            put(v.memset(ones2[:].bitcast(F32), 1.0))
            for k in range(2):
                put(v.memset(augx[k][:].bitcast(F32), 1.0))
                put(v.memset(xcT[k][:, N2 + K2:N2 + KW], 0.0))
                link(v.memset(vs[k][:], 0.0))
                put(v.memset(vs[k][:, :, :, DH:DH + 1], 1.0))
            put(v.memset(bst[2][:, :, :, MSK:MSK + 1], MASKED))
            put(v.memset(bst[0][:, :, :, MSK:MSK + 1], 1.0))
            put(v.memset(bst[1][:, :, :, MHI:MLO + 1], 1.0))
            dve.wait_ge(mask_in, 16)
            v.tensor_copy(maskf[:, :], masku[:, :]).then_inc(mask_f, 1)
            dve.wait_ge(ident_done, 2)
            idv = ident[:, :].rearrange("p (j r) -> p j r", j=J)
            for k, r0 in ((0, 16), (1, 8)):
                put(v.tensor_reduce(rowsel[k][:, :], idv[:, :, r0:r0 + 8], op=ALU.add, axis=AX.XY))
            dve.wait_ge(w_in, 7 * 16)
            link(v.tensor_scalar(keep[:, :], ident[0:3, 2:3], -1.0, 1.0, ALU.mult, ALU.add))
            for k in range(2):
                bsrc = brow[:, k, :].rearrange("a (g j d) -> a (g j) d", g=G, j=J)
                for c in range(3):
                    link(v.tensor_copy(bst[k][:].rearrange("a g j r -> a (g j) r")[:, :, 8 * c:8 * c + 8], bsrc))
            for k in range(2):
                link(v.tensor_scalar(bst[k][:], bst[k][:], keep[:, 0:1], None, ALU.mult))
                if k == 1:
                    link(v.scalar_tensor_tensor(bst[3][:], bst[2][:], ident[0:3, 2:3], bst[1][:], ALU.mult, ALU.add))
                src = bst[3] if k == 1 else bst[0]
                link(v.tensor_scalar(augw[:], src[:], ident[0:3, 1:2], None, ALU.mult))
                link(v.tensor_tensor(aug[k][:], src[:], augw[:], ALU.subtract))
            for raw, halves in ((1, wk3), (0, wq3)):
                wsrc = wraw[:, raw, :].rearrange("p (h d) -> p h d", h=H)
                for c in range(3):
                    link(v.tensor_copy(wst[:].rearrange("p g j r -> p (g j) r")[:, :, 8 * c:8 * c + 8], wsrc))
                link(v.tensor_copy(halves[0][:], wst[:]))
                link(v.tensor_tensor(halves[1][:], wst[:], halves[0][:], ALU.subtract))
            dve.wait_ge(wr_T, 2)
            link(v.tensor_copy(bsb[:, :, 0:HC], small[0][:, E:E + E * HC].rearrange("p (e c) -> p e c", e=E)))
            link(v.tensor_copy(bsb[:, :, HC:HC + 1], small[0][:, E + E * HC:2 * E + E * HC].rearrange("p (e a) -> p e a", a=1)))
            v.tensor_copy(wrT[:, :], small[0][:, 0:E]).then_inc(prep, 1)
            dve.wait_ge(w_in2, 48)
            dve.wait_ge(kept, 9)
            link(v.tensor_copy(tri[:, :], trif[:, :]))
            link(v.memset(ones[:, :], 1.0))
            link(v.memset(before[:, :], 0.0))

            def normalise(m, first):
                s, k = m
                src = small[0][:, :].rearrange("p (h r) -> p h r", h=H)
                dve.wait_ge(ott_full, s.count(2, k + 1))
                if not first:
                    dve.wait_ge(on_done, s.count(2, k))
                v.reciprocal(rden[:].rearrange("p g j -> p (g j)"), src[:, :, DH]).then_inc(rc_done, 1)
                dve.wait_ge(rc_done, s.count(2, k + 1))
                if not first:
                    dve.wait_ge(ont_full, s.count(2, k))
                v.tensor_tensor(on[:], src[:, :, 0:DH],
                                rden[:].rearrange("p g (j a) -> p (g j) a", a=1).to_broadcast([P, H, DH]),
                                ALU.mult).then_inc(on_done, 1)

            def residual(m):
                s, k = m
                dve.wait_ge(wo_full, s.count(2, k + 1))
                dve.wait_ge(xbo_done, s.count(1, 0 if k < 0 else 1))
                xb = xres[:, bass.ds(s.count(2, k), 1), :].rearrange("p a d -> p (a d)")
                v.tensor_tensor(xb, small[1][:, 0:D], xb, ALU.add).then_inc(x1_done, 1)

            def slot(s, n):
                c = s + 1
                k = c.parity
                LN = 14
                if exists(n, 1) and (n is None or n >= 1):
                    dve.wait_ge(b_full, s.count(8))
                    dve.wait_ge(pv_done, s.count(8))

                def unsplit(u):
                    dve.wait_ge(w_part, c.count(4, u + 1))
                    gs = slice(2 * (u % 2), 2 * (u % 2) + 2)
                    if u < 2:
                        views = ks[k][:, gs, :], *(w[:, 0:2 * KW].rearrange("p (g n) -> p g n", g=2)[:, :, 0:K2]
                                                   for w in (wide[u % 3], part[u % 2]))
                    else:
                        views = qs[k][:, :, gs, :], *(w[:, 0:2 * N2].rearrange("p (g b q) -> p b g q", g=2, b=2)
                                                      for w in (wide[u % 3], part[u % 2]))
                    v.tensor_tensor(*views, ALU.subtract).then_inc(w_free, 1)

                def add_values():
                    dve.wait_ge(v_full, c.count(1, 1))
                    v.tensor_tensor(vs[k][:, :, :, 0:DH].rearrange("p b h d -> p (b h) d"),
                                    small[0][0:KL, 0:2 * D].rearrange("p (b h d) -> p (b h) d", b=2, h=H),
                                    bvb[0:KL].rearrange("p b (h d) -> p (b h) d", h=H), ALU.add).then_inc(v_taken, 1)

                def best(u):
                    b, gg = divmod(u, G)
                    dve.wait_ge(w_full, c.count(12, 5 + u))
                    v.tensor_reduce(mx[:, b, gg, :], wide[(4 + u) % 3][:, 0:J * KL].rearrange("p (j k) -> p j k", j=J),
                                    op=ALU.max, axis=AX.X).then_inc(w_free, 1)

                def newton(k):
                    if not todo:
                        return
                    dve.wait_ge(ln_chain, (s + 3).count(LN, 3 + k))
                    if k == 0:
                        v.tensor_scalar(nve[:, :], ve[:, :], -0.5, None, ALU.mult)
                        last = v.tensor_scalar(vbits[:, :], ve[:, :].bitcast(I32), 1, None, ALU.logical_shift_right)
                    elif k == 1:
                        last = v.tensor_scalar(ys[0][:, :].bitcast(I32), vbits[:, :], -1.0, float(0x5F3759DF), ALU.mult, ALU.add)
                    elif k % 3 == 2:
                        last = v.tensor_tensor(yy[:, :], ys[(k - 2) // 3 % 2][:, :], ys[(k - 2) // 3 % 2][:, :], ALU.mult)
                    elif k % 3 == 0:
                        last = v.tensor_tensor(vyy[:, :], yy[:, :], nve[:, :], ALU.mult)
                    else:
                        old, new = (k - 4) // 3 % 2, 1 - (k - 4) // 3 % 2
                        last = v.scalar_tensor_tensor(ys[new][:, :], vyy[:, :], 1.5, ys[old][:, :], ALU.add, ALU.mult)
                    last.then_inc(ln_chain, 1)

                r = s + -2

                def route(k):
                    if not exists(n, -2):
                        return
                    if k == 0:
                        dve.wait_ge(rl_taken, r.count(1, 1))
                        v.tensor_copy(pick[:, :].rearrange("p (b k) -> p b k", b=2), tidx[:, :, 0:2]).then_inc(top_chain, 1)
                    elif k == 1:
                        dve.wait_ge(top_exp, r.count(1, 1))
                        v.tensor_reduce(tsum[:, :], tope[:], op=ALU.add, axis=AX.X).then_inc(top_chain, 1)
                    elif k == 2:
                        dve.wait_ge(top_chain, r.count(6, 2))
                        v.reciprocal(tinv[:, :], tsum[:, :]).then_inc(top_chain, 1)
                    elif k == 3:
                        if exists(n, -3):
                            dve.wait_ge(pos_done, r.count(1))
                        for b in range(2):
                            last = v.tensor_tensor(hot[:, b], pick[:, 2 * b:2 * b + 2].rearrange("p (k a) -> p k a", a=1).to_broadcast([P, 2, E]),
                                                   eidx[:].rearrange("p (a e) -> p a e", a=1).to_broadcast([P, 2, E]), ALU.is_equal)
                        last.then_inc(top_chain, 1)
                    elif k == 4:
                        dve.wait_ge(top_chain, r.count(6, 4))
                        v.tensor_tensor(prob[:, bass.ds(r.count(2), 2), :], tope[:, :, 0:2],
                                        tinv[:].rearrange("p (b a) -> p b a", a=1).to_broadcast([P, 2, 2]),
                                        ALU.mult).then_inc(routed, 1)
                        if exists(n, -3):
                            dve.wait_ge(pos_chain, r.count(3))
                        v.tensor_tensor(taken[:], hot[:, :, 0, :], hot[:, :, 1, :], ALU.add).then_inc(top_chain, 1)
                    else:
                        dve.wait_ge(top_chain, r.count(6, 5))
                        v.tensor_tensor(taken2[:, :], taken[:, 0, :], taken[:, 1, :], ALU.add).then_inc(top_chain, 1)

                def position(k):
                    if not exists(n, -2):
                        return
                    if k == 0:
                        dve.wait_ge(pos_full, r.count(1, 1))
                        v.tensor_tensor(place[:], small[1][:, 16:16 + 2 * E].rearrange("p (b e) -> p b e", b=2),
                                        region[:].rearrange("p (a e) -> p a e", a=1).to_broadcast([P, 2, E]), ALU.add).then_inc(pos_taken, 1)
                        v.tensor_tensor(before[:, :], before[:, :], taken2[:, :], ALU.add).then_inc(pos_chain, 1)
                    elif k == 1:
                        dve.wait_ge(pos_taken, r.count(1, 1))
                        for b in range(2):
                            last = v.tensor_tensor(placed[:, 2 * b:2 * b + 2, :], hot[:, b, :, :],
                                                   place[:, b:b + 1, :].to_broadcast([P, 2, E]), ALU.mult)
                        last.then_inc(pos_chain, 1)
                    elif k == 2:
                        dve.wait_ge(pos_chain, r.count(3, 2))
                        v.tensor_reduce(posf[:, :], placed[:], op=ALU.add, axis=AX.X).then_inc(pos_chain, 1)
                    else:
                        dve.wait_ge(pos_chain, r.count(3, 3))
                        if exists(n, -4):
                            dve.wait_ge(scat[r.parity], r.uses(64, -64))
                        v.tensor_copy(posi[r.parity][:, :], posf[:, :]).then_inc(pos_done, 1)

                def norm_x():
                    if exists(n, 3):
                        f = s + 3
                        dve.wait_ge(ln_chain, (s + 3).count(LN, 14))
                        if exists(n, 1):
                            dve.wait_ge(tx_full, s.count(1, 2))
                        for b in range(2):
                            last = v.tensor_scalar(xn[f.parity][:, b:b + 1, :], xres[:, bass.ds(f.count(2, b), 1), :],
                                                   mv[:, b, 0:1], ys[1][:, b:b + 1], ALU.subtract, ALU.mult)
                        last.then_inc(lnx_done, 1)

                def norm_x1():
                    if exists(n, -1):
                        m = s + -1
                        dve.wait_ge(ln_chain, (s + 3).count(LN, 14))
                        if exists(n, -2):
                            dve.wait_ge(x2t_full, s.count(1, -1))
                        if exists(n, -3):
                            dve.wait_ge(scat[m.parity], m.uses(64, -64))
                        for b in range(2):
                            last = v.tensor_scalar(rows[m.parity][:, b:b + 1, 0, 0:D], xres[:, bass.ds(m.count(2, b), 1), :],
                                                   mv[:, 2 + b, 0:1], ys[1][:, 2 + b:3 + b], ALU.subtract, ALU.mult)
                        last.then_inc(ln2_done, 1)

                if exists(n, -1):
                    normalise((s, -1), False)
                route(0)
                if exists(n, 1):
                    unsplit(0)
                    route(1)
                    unsplit(1)
                else:
                    route(1)
                route(2)
                route(3)
                if exists(n, -1):
                    residual((s, -1))
                route(4)
                todo = []
                if exists(n, 3):
                    f = s + 3
                    dve.wait_ge(x_in[f.parity], f.uses(16))
                    todo += [(b, xres[:, bass.ds(f.count(2, b), 1), :]) for b in range(2)]
                if exists(n, -1):
                    dve.wait_ge(x1_done, s.count(2))
                    todo += [(2 + b, xres[:, bass.ds(s.count(2, b - 2), 1), :]) for b in range(2)]
                if todo:
                    if exists(n, 2):
                        dve.wait_ge(lnx_done, (s + 3).count(1))
                    if exists(n, -2):
                        dve.wait_ge(ln2_done, s.count(1, -1))
                    for b, src in todo:
                        last = v.bn_stats(stats[:, b, :], src.rearrange("p a d -> p (a d)"))
                    last.then_inc(ln_chain, 1)
                route(5)
                if todo:
                    alone(dve, ln_chain, (s + 3).count(LN, 1))
                    for b, src in todo:
                        last = v.bn_aggr(mv[:, b, :], stats[:, b, :])
                    last.then_inc(ln_chain, 1)
                if exists(n, 1):
                    unsplit(2)
                if todo:
                    dve.wait_ge(ln_chain, (s + 3).count(LN, 2))
                    v.tensor_scalar(ve[:, :], mv[:, :, 1], EPS, None, ALU.add).then_inc(ln_chain, 1)
                if exists(n, 1):
                    unsplit(3)
                newton(0)
                if exists(n, 1):
                    add_values()
                newton(1)
                position(0)
                newton(2)
                if exists(n, 1) and (n is None or n >= 0):
                    dve.wait_ge(nm_full, c.count(1))
                for u in range(8):
                    if exists(n, 1):
                        best(u)
                    if u < 4:
                        newton(2 * u + 3)
                    if u < 3:
                        position(u + 1)
                    if u == 3 and exists(n, 0):
                        normalise((s, 0), n == 0)
                    if u < 4:
                        newton(2 * u + 4)
                    if u == 4:
                        norm_x1()
                    if u == 5:
                        norm_x()
                if exists(n, 0):
                    residual((s, 0))
                if exists(n, 1):
                    dve.wait_ge(nm_full, c.count(1, 1))
                    nsrc = small[0][0:J * G * 2, 0:S]
                    v.tensor_scalar(negm[k][:, 0, :], nsrc, -1.0, None, ALU.mult).then_inc(nm_split, 1)
                    dve.wait_ge(nm_split, c.count(2, 1))
                    v.scalar_tensor_tensor(negm[k][:, 1, :], nsrc, -1.0, negm[k][:, 0, :], ALU.mult, ALU.subtract).then_inc(nm_split, 1)
                if exists(n, -1):
                    alone(dve, rl_full, s.count(1))
                    lg = small[1][:, 0:2 * E].rearrange("p (b e) -> p b e", b=2)
                    if n != 1:
                        alone(dve, routed, s.count(1, -1))
                    for b in range(2):
                        last = v.max(top[:, b, :], lg[:, b, :])
                    last.then_inc(top_max, 1)
                    alone(dve, top_max, s.count(1))
                    for b in range(2):
                        last = v.max_index(tidx[:, b, :], top[:, b, :], lg[:, b, :])
                    last.then_inc(rl_taken, 1)
                    v.tensor_tensor(topd[:], top[:], top[:, :, 0:1].to_broadcast([P, 2, E]), ALU.subtract).then_inc(top_sub, 1)

            slots(dve, slot)

            dve.wait_ge(cnt_full, 1)
            link(v.tensor_copy(cnt[:, :], small[0][0:1, 0:E]))
            link(v.tensor_tensor(over[:], cnt[:].rearrange("a (e j) -> a e j", j=1).to_broadcast([1, E, NTOK // TB]), thr[:], ALU.is_gt))
            link(v.tensor_reduce(cum[0][:, :], over[:], op=ALU.add, axis=AX.X))
            for k, step in enumerate((1, 2, 4)):
                old, new = cum[k], cum[k + 1]
                link(v.tensor_copy(new[:, 0:step], old[:, 0:step]))
                link(v.tensor_tensor(new[:, step:E], old[:, step:E], old[:, 0:E - step], ALU.add))
            link(v.tensor_tensor(past[:], tix[:], cum[3][:].rearrange("a (j e) -> a j e", j=1).to_broadcast([1, NT, E]), ALU.is_ge))
            link(v.tensor_reduce(tile_e[:, :], past[:], op=ALU.add, axis=AX.X))
            link(v.tensor_tensor(pastn[:], past[:], cum[0][:].rearrange("a (j e) -> a j e", j=1).to_broadcast([1, NT, E]), ALU.mult))
            link(v.tensor_reduce(tile_s[:, :], pastn[:], op=ALU.add, axis=AX.X))
            link(v.tensor_tensor(tile_r[0][:, :], tix[:, :, 0], tile_s[:, :], ALU.subtract))
            link(v.tensor_scalar(tile_r[1][:, :], tile_e[:, :], float(REGION), None, ALU.mult))
            link(v.scalar_tensor_tensor(tile_r[2][:, :], tile_r[0][:, :], float(TB), tile_r[1][:, :], ALU.mult, ALU.add))
            link(v.tensor_scalar(tab_r[:, :], tile_r[2][:, :], float(SPARE), None, ALU.min))
            link(v.tensor_scalar(tab_e[:, :], tile_e[:, :], float(E - 1), None, ALU.min))
            v.tensor_tensor(tab_t[:, :], cnt[:, :], region[0:1, :], ALU.add).then_inc(tables, 1)

            def lower(t, c):
                dve.wait_ge(h_val, t.count(HC, c + 1))
                v.tensor_tensor(hhl[:, 1, c, :], hid[:, c % 2, :], hhl[:, 0, c, :], ALU.subtract).then_inc(h_lo, 1)

            def lower_x(t):
                dve.wait_ge(xt_hi, t.count(1, 1))
                v.tensor_tensor(xTl[:, :], bank[4][:, :], xTh[:, :], ALU.subtract).then_inc(xt_lo, 1)

            def rows_out(t, first):
                dve.wait_ge(yr_full, t.count(1, 1))
                if not first:
                    dve.wait_ge(y_out[t.parity], t.uses(64, -64))
                v.tensor_copy(yrow[t.parity][:].rearrange("p n d -> p (n d)"), bank[6][:, :]).then_inc(yr_taken, 1)

            def tile(t, n):
                if n == 0:
                    lower_x(t)
                for c in range(HC):
                    if n != NT:
                        lower(t, c)
                if n is None or n + 1 < NT:
                    lower_x(t + 1)
                if n != 0:
                    rows_out(t + -1, n is not None and n <= 2)

            tiles(dve, tile)

            def combine(q):
                dve.wait_ge(y_in[q.parity], q.uses(32))
                for i, done in enumerate((fin_a, fin_b)):
                    if i:
                        dve.wait_ge(fin_a, q.count(1, 1))
                    for b in range(TN):
                        xb = xres[:, bass.ds(q.count(TN, b), 1), :].rearrange("p a d -> p (a d)")
                        last = v.scalar_tensor_tensor(xb, yin[i][q.parity][:, b, :],
                                                      prob[:, bass.ds(q.count(TN, b), 1), i:i + 1].rearrange("p a k -> p (a k)"),
                                                      xb, ALU.mult, ALU.add)
                    last.then_inc(done, 1)

            with dve.Fori(0, B // TN // 2) as pair:
                for k in range(2):
                    combine(At(pair, k))

        @block.scalar
        def _(act):
            a = nc.scalar

            def halve(c, u, n):
                if n == -1 and u == 0:
                    act.wait_ge(prep, 1)
                act.wait_ge(w_full, c.count(12, u + 1))
                if u >= 2:
                    act.wait_ge(w_free, c.count(12, u - 1))
                width, used = ((KW, K2), (N2, N2))[u // 2]
                dst, src = (w[:, 0:2 * width].rearrange("p (g n) -> p g n", g=2)[:, :, 0:used] for w in (part[u % 2], wide[u % 3]))
                a.activation(dst, src, ACT.Identity, scale=rowsel[1 - u // 2][:, 0:1]).then_inc(w_part, 1)

            def slot(s, n):
                c = s + 1
                if exists(n, 1):
                    halve(c, 0, n)
                    halve(c, 1, n)
                if exists(n, -1):
                    take_on(s, -1)
                for t in range(8):
                    if exists(n, 0):
                        act.wait_ge(b_full, s.count(8, t + 1))
                        if t >= NP:
                            act.wait_ge(pv_done, s.count(8, t - NP + 1))
                        elif n != 0:
                            act.wait_ge(pv_done, s.count(8, t - NP + 1))
                        a.activation(pt[t % NP][:].rearrange("p j q -> p (j q)"), scores[t % 2][0:KL, :], ACT.Exp,
                                     scale=SCALE).then_inc(exp_done, 1)
                    if t in (1, 2) and exists(n, 1):
                        halve(c, t + 1, n)
                    if t == 4 and exists(n, 0):
                        take_heads(s, 0, n)
                    if t == 2 and exists(n, 2):
                        f = s + 2
                        act.wait_ge(tx_full, f.count(1, 1))
                        if n is None or n >= 0:
                            act.wait_ge(hl_done, s.count(1, 1))
                            act.wait_ge(v_full, s.count(1, 1))
                        a.activation(xcT[f.parity][:, 0:N2 + K2], small[1][:, 0:N2 + K2], ACT.Copy).then_inc(tx_taken, 1)
                    if t == 6 and exists(n, 0):
                        take_on(s, 0)
                    if t == 6 and exists(n, -1):
                        act.wait_ge(x2t_full, s.count(1))
                        if n != 1:
                            act.wait_ge(rl_full, s.count(1, -1))
                        a.activation(x2s[:, :], small[0][:, 0:N2], ACT.Copy).then_inc(x2t_taken, 1)
                if exists(n, 0):
                    take_heads(s, 1, n)
                if exists(n, -1):
                    act.wait_ge(top_sub, s.count(1))
                    a.activation(tope[:].rearrange("p b e -> p (b e)"), topd[:].rearrange("p b e -> p (b e)"), ACT.Exp).then_inc(top_exp, 1)

            def take_heads(s, b, n):
                act.wait_ge(pv_done, s.count(8, 4 * b + 4))
                if n != 0:
                    act.wait_ge(ott_full, s.count(2, b - 1))
                a.activation(ots[b][:].rearrange("p g q -> p (g q)"), heads[:, :], ACT.Copy).then_inc(ot_taken, 1)

            def take_on(s, k):
                act.wait_ge(ont_full, s.count(2, k + 1))
                if isinstance(s.pair, int) and s.count(2, k) == 0:
                    pass
                else:
                    act.wait_ge(wo_full, s.count(2, k))
                a.activation(onT[:, :], small[1][:, 0:S], ACT.Copy).then_inc(ont_taken, 1)

            slots(act, slot)

            def upper_x(t):
                act.wait_ge(xt_full, t.count(1, 1))
                a.activation(xTh[:, :], bank[4][:, :], ACT.Copy).then_inc(xt_hi, 1)

            def tile(t, n):
                k = t.parity
                if n == 0:
                    upper_x(t)
                if n == NT:
                    return
                act.wait_ge(w_tile[k], t.uses(32))
                for c in range(HC):
                    act.wait_ge(h_full, t.count(HC, c + 1))
                    a.activation(hhl[:, 0, c, :], bank[c][:, :], ACT.Gelu, bias=btile[k][:, c:c + 1]).then_inc(h_hi, 1)
                    if c >= 2:
                        act.wait_ge(h_lo, t.count(HC, c - 1))
                    elif n != 0:
                        act.wait_ge(h_lo, t.count(HC, c - 1))
                    a.activation(hid[:, c % 2, :], bank[c][:, :], ACT.Gelu, bias=btile[k][:, c:c + 1]).then_inc(h_val, 1)
                if n is None or n + 1 < NT:
                    upper_x(t + 1)
                act.wait_ge(yt_full, t.count(1, 1))
                a.activation(yT[:, :], bank[5][:, :], ACT.Identity, bias=btile[k][:, HC:HC + 1]).then_inc(yt_taken, 1)

            tiles(act, tile)

        @block.tensor
        def _(pe):
            t_ = nc.tensor
            pe.wait_ge(ident_done, 2)
            pe.wait_ge(w_in, 7 * 16)
            pe.wait_ge(b_in, 32)
            t_.transpose(small[0][:, 0:E], wrraw[:, :], ident[0:E, 0:E]).then_inc(wr_T, 1)
            nb = E * (HC + 1)
            t_.transpose(small[0][:, E:E + nb], braw[:, :], ident[0:nb, 0:nb]).then_inc(wr_T, 1)
            pe.wait_ge(prep, 1)

            def project(c, u, n):
                k = c.parity
                halves, cols, am = (((wk3, slice(N2, N2 + KW), aug[1]), (wq3, slice(0, N2), aug[0]))[u // 2])
                width = (KW, N2)[u // 2]
                if n != -1:
                    pe.wait_ge(w_free, c.count(12, u - 2))
                elif u == 3:
                    pe.wait_ge(w_free, 1)
                if u == 0:
                    pe.wait_ge(hl_done, c.count(1, 1))
                    pe.wait_ge(mask_row[k], c.uses(16))
                for gg in range(2):
                    g = 2 * (u % 2) + gg
                    dst = wide[u % 3][:, gg * width:(gg + 1) * width]
                    hi, lo = (w[:, g].rearrange("p j r -> p (j r)") for w in halves)
                    t_.matmul(dst, hi, xcTh[k][:, cols], start=True, stop=False)
                    t_.matmul(dst, hi, xcTl[k][:, cols], start=False, stop=False)
                    t_.matmul(dst, lo, xcTh[k][:, cols], start=False, stop=False)
                    if u < 2:
                        last = t_.matmul(dst, am[0:3, g].rearrange("p j r -> p (j r)"), augx[k][0:3, :], start=False, stop=True)
                    else:
                        last = t_.matmul(dst, am[0:2, g].rearrange("p j r -> p (j r)"), ones2[0:2, :], start=False, stop=True)
                last.then_inc(w_full, 1)

            def values(c, n):
                if n == 0:
                    pe.wait_ge(nm_split, 2)
                elif n != -1:
                    pe.wait_ge(on_done, (c + -1).count(2))
                for b in range(2):
                    last = t_.matmul(small[0][0:KL, b * D:(b + 1) * D],
                                     xcT[c.parity][:, N2 + b * KL:N2 + (b + 1) * KL], wraw[:, 2, :], start=True, stop=True)
                last.then_inc(v_full, 1)

            def turn_heads(s, k):
                pe.wait_ge(ot_taken, s.count(2, k + 1))
                for g in range(G):
                    last = t_.transpose(small[0][:, g * P:(g + 1) * P], ots[k % 2][:, g, :], ident[:, :])
                last.then_inc(ott_full, 1)

            def turn_on(s, k):
                pe.wait_ge(on_done, s.count(2, k + 1))
                t_.transpose(small[1][:, 0:S], on[:].rearrange("p h d -> p (h d)"), ident[:, :]).then_inc(ont_full, 1)

            def project_out(s, k):
                pe.wait_ge(ont_taken, s.count(2, k + 1))
                t_.matmul(small[1][:, 0:D], onT[:, :], wraw[:, 3, :], start=True, stop=True).then_inc(wo_full, 1)

            def by_query(c, u, n):
                b, g = divmod(u, G)
                if u == 0:
                    pe.wait_ge(kblk[c.parity], c.uses(64))
                pe.wait_ge(w_free, c.count(12, 4 + max(u - 2, 0)))
                t_.matmul(wide[(4 + u) % 3][:, 0:J * KL].rearrange("p (j k) -> p j k", j=J), qs[c.parity][:, b, g, :],
                          kb[c.parity][:, g, :, b * KL:(b + 1) * KL], start=True, stop=True).then_inc(w_full, 1)

            def by_key(s, t, n):
                b, g = divmod(t, G)
                if t == 0:
                    pe.wait_ge(mrow[s.parity], s.uses(32))
                if n != 0 or t >= 2:
                    pe.wait_ge(exp_done, s.count(8, t - 1))
                t_.matmul(scores[t % 2][0:KL, :].rearrange("p (j q) -> p j q", j=J), ks[s.parity][:, g, b * KL:(b + 1) * KL],
                          qb[s.parity][:, b, g, :, :], start=True, stop=True).then_inc(b_full, 1)

            def weigh(s, t, n):
                b, g = divmod(t, G)
                pe.wait_ge(exp_done, s.count(8, t + 1))
                if g == 0 and not (n == 0 and b == 0):
                    pe.wait_ge(ot_taken, s.count(2, b))
                for j in range(J):
                    last = t_.matmul(heads[R * j:R * j + R, g * S:(g + 1) * S], vs[s.parity][:, b, G * g + j, :],
                                     pt[t % NP][:, j, :], start=True, stop=True, tile_position=(0, R * j))
                last.then_inc(pv_done, 1)

            def slot(s, n):
                c = s + 1
                if exists(n, 1):
                    project(c, 0, n)
                if exists(n, -1):
                    if n == NCH:
                        pe.wait_ge(x2t_taken, NCH - 1)
                    else:
                        pe.wait_ge(nm_split, s.count(2, 2))
                    turn_heads(s, -1)
                if exists(n, 1):
                    project(c, 1, n)
                if exists(n, -1):
                    if exists(n, -2):
                        pe.wait_ge(rl_taken, s.count(1, -1))
                    turn_on(s, -1)
                if exists(n, 0):
                    by_key(s, 0, n)
                    by_key(s, 1, n)
                if exists(n, -1):
                    project_out(s, -1)
                for t in range(8):
                    if exists(n, 0):
                        weigh(s, t, n)
                        if t < 6:
                            by_key(s, t + 2, n)
                    if exists(n, 1) and t in (0, 1):
                        project(c, t + 2, n)
                        if t == 1:
                            values(c, n)
                    if exists(n, 2) and t == 1:
                        f = s + 2
                        pe.wait_ge(lnx_done, f.count(1, 1))
                        pe.wait_ge(ctx_in[f.parity], f.uses(16))
                        if exists(n, -1):
                            pe.wait_ge(x1_done, s.count(2, 0))
                        elif n != -2:
                            pe.wait_ge(tx_taken, n + 2)
                        for b in range(2):
                            t_.transpose(small[1][:, b * S:(b + 1) * S], xn[f.parity][:, b, :], ident[:, :])
                        for b in range(2):
                            last = t_.transpose(small[1][:, N2 + b * KL:N2 + (b + 1) * KL], ctxin[f.parity][:, b, :], ident[0:KL, 0:KL])
                        last.then_inc(tx_full, 1)
                    if exists(n, -2) and t == 2:
                        if exists(n, 2):
                            pe.wait_ge(tx_taken, s.count(1, 3))
                        else:
                            pe.wait_ge(x1_done, s.count(2, 0) if exists(n, -1) else 2 * NCH)
                        if n == NCH + 1:
                            pe.wait_ge(rl_taken, NCH)
                        pe.wait_ge(top_chain, s.count(6, -6))
                        for b in range(2):
                            dst = small[1][:, 16 + b * E:16 + (b + 1) * E]
                            t_.matmul(dst, tri[:, :], taken[:, b, :], start=True, stop=False)
                            last = t_.matmul(dst, ones[:, :], before[:, :], start=False, stop=b == 0)
                            if b:
                                last = t_.matmul(dst, ones[:, :], taken[:, 0, :], start=False, stop=True)
                        last.then_inc(pos_full, 1)
                    if exists(n, 1) and 2 <= t < 6:
                        by_query(c, 2 * t - 4, n)
                        by_query(c, 2 * t - 3, n)
                    if exists(n, 0) and t == 4:
                        if exists(n, 1):
                            pe.wait_ge(v_taken, c.count(1, 1))
                        else:
                            pe.wait_ge(on_done, s.count(2))
                        turn_heads(s, 0)
                    if exists(n, 0) and t == 5:
                        if exists(n, -2):
                            pe.wait_ge(pos_taken, s.count(1, -1))
                        else:
                            pe.wait_ge(tx_taken, n + 3)
                        turn_on(s, 0)
                    if exists(n, -1) and t == 6:
                        pe.wait_ge(ln2_done, s.count(1))
                        pe.wait_ge(on_done, s.count(2, 1 if exists(n, 0) else 0))
                        for b in range(2):
                            last = t_.transpose(small[0][:, b * S:(b + 1) * S], rows[1 - s.parity][:, b, 0, 0:D], ident[:, :])
                        last.then_inc(x2t_full, 1)
                    if exists(n, 0) and t == 6:
                        project_out(s, 0)
                    if exists(n, 1) and t == 7:
                        pe.wait_ge(w_free, c.count(12, 12))
                        if n == -1:
                            pe.wait_ge(v_taken, 1)
                        elif n == 0:
                            pe.wait_ge(on_done, 1)
                        else:
                            pe.wait_ge(x2t_taken, s.count(1))
                        t_.transpose(small[0][0:J * G * 2, 0:S], mx[:].rearrange("p b g j -> p (b g j)"), ident[:, :]).then_inc(nm_full, 1)
                    if exists(n, -1) and t == 7:
                        pe.wait_ge(x2t_taken, s.count(1))
                        if exists(n, 0):
                            pe.wait_ge(x1_done, s.count(2, 1))
                        else:
                            pe.wait_ge(pos_taken, NCH - 1)
                        for b in range(2):
                            last = t_.matmul(small[1][:, b * E:(b + 1) * E], x2s[:, b * S:(b + 1) * S],
                                             wrT[:, :], start=True, stop=True)
                        last.then_inc(rl_full, 1)

            slots(pe, slot)

            pe.wait_ge(pos_chain, 3 * NCH)
            pe.wait_ge(x2t_taken, NCH)
            t_.matmul(small[0][:, 0:E], ones[:, :], before[:, :], start=True, stop=True).then_inc(cnt_full, 1)

            def turn_x(t):
                k = t.parity
                pe.wait_ge(x_tile[k], t.uses(16))
                if not isinstance(t.pair, int) or t.count(1) > 0:
                    pe.wait_ge(xt_lo, t.count(1))
                for j in range(TN):
                    last = t_.transpose(bank[4][:, j * P:(j + 1) * P], xrow[k][:, j, 0:D], ident[:, :])
                last.then_inc(xt_full, 1)

            def turn_y(t):
                pe.wait_ge(yt_taken, t.count(1, 1))
                if not isinstance(t.pair, int) or t.count(1) > 0:
                    pe.wait_ge(yr_taken, t.count(1))
                else:
                    pe.wait_ge(tables, 1)
                for j in range(TN):
                    last = t_.transpose(bank[6][:, j * P:(j + 1) * P], yT[:, j * P:(j + 1) * P], ident[:, :])
                last.then_inc(yr_full, 1)

            def tile(t, n):
                k = t.parity
                if n == 0:
                    pe.wait_ge(pv_done, 8 * NCH)
                    turn_x(t)
                if n != NT:
                    pe.wait_ge(xt_lo, t.count(1, 1))
                    pe.wait_ge(w_tile[k], t.uses(32))
                    w = wtile[k]
                    for c in range(HC):
                        if n != 0:
                            pe.wait_ge(h_val, t.count(HC, c - HC + 1))
                        cs = slice(c * P, (c + 1) * P)
                        t_.matmul(bank[c][:, :], w[:, 0, 0, cs], xTh[:, :], start=True, stop=False)
                        t_.matmul(bank[c][:, :], w[:, 0, 0, cs], xTl[:, :], start=False, stop=False)
                        t_.matmul(bank[c][:, :], w[:, 1, 0, cs], xTh[:, :], start=False, stop=True).then_inc(h_full, 1)
                if n is None or n + 1 < NT:
                    turn_x(t + 1)
                if n != 0:
                    turn_y(t + -1)
                if n != NT:
                    for c in range(HC):
                        cs = slice(c * P, (c + 1) * P)
                        pe.wait_ge(h_hi, t.count(HC, c + 1))
                        t_.matmul(bank[5][:, :], w[:, 0, 1, cs], hhl[:, 0, c, :], start=c == 0, stop=False)
                        t_.matmul(bank[5][:, :], w[:, 1, 1, cs], hhl[:, 0, c, :], start=False, stop=False)
                        pe.wait_ge(h_lo, t.count(HC, c + 1))
                        last = t_.matmul(bank[5][:, :], w[:, 0, 1, cs], hhl[:, 1, c, :], start=False, stop=c == HC - 1)
                    last.then_inc(yt_full, 1)

            tiles(pe, tile)


_INS = ['x', 'ctx_1024', 'mask_BxS2_bf0', 'L0_xattn_Wq', 'L0_xattn_bq', 'L0_xattn_Wk', 'L0_xattn_bk', 'L0_xattn_Wv',
        'L0_xattn_bv', 'L0_xattn_Wo', 'L0_xattn_bo', 'L0_ffn_Wr', 'L0_ffn_W1', 'L0_ffn_b1', 'L0_ffn_W2', 'L0_ffn_b2']


def kernel(**inputs):
    import numpy as _np
    import concourse.bacc as _bacc
    from concourse import mybir as _mybir
    from concourse.bass_utils import run_bass_kernel_spmd as _run

    nc = _bacc.Bacc("TRN2", target_bir_lowering=False, num_devices=1)
    arrays, args = {}, []
    for name in _INS:
        a = _np.ascontiguousarray(inputs[name])
        arrays[f"in_{name}"] = a
        args.append(nc.dram_tensor(f"in_{name}", a.shape, _mybir.dt.from_np(a.dtype), kind="ExternalInput").ap())
    out = nc.dram_tensor("out_0", inputs["x"].shape, F32, kind="ExternalOutput").ap()
    moe_attention(nc, *args, out)
    r = _run(nc, [arrays], core_ids=[0])
    return r.results[0]["out_0"]
```

```python
from contextlib import ExitStack

import concourse.bass as bass
from concourse import mybir

F32 = mybir.dt.float32
F32R = mybir.dt.float32r
U32 = mybir.dt.uint32
I32 = mybir.dt.int32
BF16 = mybir.dt.bfloat16
ALU = mybir.AluOpType
ACT = mybir.ActivationFunctionType
AX = mybir.AxisListType

P = 128
MASKED = -float(2**100)
EPS = 1e-5


class At:

    def __init__(self, pair, parity):
        self.pair, self.parity = pair, parity

    def __add__(self, k):
        n = self.parity + k
        return At(self.pair + n // 2 if n // 2 else self.pair, n % 2)

    def count(self, each, more=0):
        return self.pair * (2 * each) + (self.parity * each + more)

    def uses(self, each, more=0):
        return self.pair * each + (each + more)


def moe_attention(nc, x, ctx, mask, Wq, bq, Wk, bk, Wv, bv, Wo, bo, Wr, W1, b1, W2, b2, out):
    B, S, D = x.shape
    KL = ctx.shape[1]
    E, _, HID = W1.shape
    H, DH = 16, 8
    G, J = 4, 4
    R = 32
    HI2, MHI, MLO, MSK = 16, 24, 25, 26
    NCH = B // 2
    HC = HID // P
    TB = 512
    NTOK = B * S
    TN = TB // P
    NT = (2 * NTOK + E * (TB - 1)) // TB
    REGION = NTOK + TB
    SPARE = E * REGION
    ROW = D + 4
    NOWHERE = 1 << 20
    NQ = B // TN
    SCALE = float(DH) ** -0.5
    N2 = 2 * S
    K2 = 2 * KL
    KW = 256

    with ExitStack() as st:
        sb = lambda name, shape, dt=F32: st.enter_context(nc.sbuf_tensor(name, shape, dt))
        sem = lambda name: st.enter_context(nc.semaphore(name))
        two = lambda name: [sem(f"{name}{k}") for k in range(2)]

        xres = sb("xres", [P, B, D])
        x2s = sb("x2s", [P, N2])
        ctxin = [sb(f"ctxin{k}", [KL, 2, D]) for k in range(2)]
        xn = [sb(f"xn{k}", [P, 2, D]) for k in range(2)]
        rows = [sb(f"rows{k}", [P, 2, 2, ROW]) for k in range(2)]
        xcT = [sb(f"xcT{k}", [P, N2 + KW]) for k in range(2)]
        xcTh = [sb(f"xcTh{k}", [P, N2 + KW], F32R) for k in range(2)]
        xcTl = [sb(f"xcTl{k}", [P, N2 + KW], F32R) for k in range(2)]
        part = [sb(f"part{k}", [P, 2 * N2], F32R) for k in range(2)]
        qs = [sb(f"qs{k}", [P, 2, G, S], F32R) for k in range(2)]
        ks = [sb(f"ks{k}", [P, G, K2], F32R) for k in range(2)]
        qb = [sb(f"qb{k}", [P, 2, G, J, S], F32R) for k in range(2)]
        kb = [sb(f"kb{k}", [P, G, J, K2], F32R) for k in range(2)]
        vs_all = [sb(f"vs{k}", [P, 2, H, R]) for k in range(2)]
        vs = [v[0:KL] for v in vs_all]
        NP = 4
        pt_all = [sb(f"pt{k}", [P, J, S]) for k in range(NP)]
        pt = [p[0:KL] for p in pt_all]
        mx = sb("mx", [P, 2, G, J])
        negm = [sb(f"negm{k}", [J * G * 2, 2, S], F32R) for k in range(2)]
        ots = [sb(f"ots{k}", [P, G, S]) for k in range(2)]
        rden = sb("rden", [P, G, J])
        on = sb("on", [P, H, DH])
        onT = sb("onT", [P, S])
        wq3 = [sb(f"wq{k}", [P, G, J, R], F32R) for k in ("hi", "lo")]
        wk3 = [sb(f"wk{k}", [P, G, J, R], F32R) for k in ("hi", "lo")]
        wst = [o[:].rearrange("p g (j r) -> p g j r", j=J) for o in ots]
        wraw = sb("wraw", [P, 4, D])
        brow = sb("brow", [3, 2, D])
        bst = [p[0:3].rearrange("p g (j r) -> p g j r", j=J) for p in pt_all]
        augw = part[0][0:3, :].rearrange("p (g j r) -> p g j r", g=G, j=J)
        aug = [sb(f"aug{k}", [3, G, J, R], F32R) for k in "qk"]
        augx = [sb(f"augx{k}", [3, KW], F32R) for k in range(2)]
        ones2 = sb("ones2", [2, N2], F32R)
        masku = sb("masku", [B, KL], mask.dtype)
        maskf = sb("maskf", [B, KL], F32R)
        keep = sb("keep", [3, 1])
        rowsel = [sb(f"rowsel{k}", [P, 1]) for k in "qk"]
        bvb = sb("bvb", [P, D])
        bvT = sb("bvT", [P, P])
        bob = sb("bob", [P, D])
        ident = sb("ident", [P, P])
        wrT = sb("wrT", [P, E])
        wrraw = sb("wrraw", [E, D])
        stats = sb("stats", [P, 4, 6])
        mv = sb("mv", [P, 4, 2])
        ve = sb("ve", [P, 4])
        nve = sb("nve", [P, 4])
        vbits = sb("vbits", [P, 4], I32)
        ys = [sb(f"y{k}", [P, 4]) for k in range(2)]
        yy = sb("yy", [P, 4])
        vyy = sb("vyy", [P, 4])
        top = sb("top", [P, 2, 8])
        topd = sb("topd", [P, 2, 8])
        tope = sb("tope", [P, 2, 8])
        tsum = sb("tsum", [P, 2])
        tinv = sb("tinv", [P, 2])
        tidx = sb("tidx", [P, 2, 8], U32)
        pick = sb("pick", [P, 4])
        hot = sb("hot", [P, 2, 2, E], BF16)
        taken = sb("taken", [P, 2, E], BF16)
        taken2 = sb("taken2", [P, E], BF16)
        before = sb("before", [P, E], BF16)
        tri = sb("tri", [P, P], BF16)
        trif = sb("trif", [P, P])
        ones = sb("ones", [P, P], BF16)
        eidx = sb("eidx", [P, E])
        region = sb("region", [P, E])
        place = sb("place", [P, 2, E])
        placed = sb("placed", [P, 4, E])
        posf = sb("posf", [P, 4])
        posi = [sb(f"posi{k}", [P, 4], I32) for k in range(2)]
        idf = sb("idf", [P, 4])
        zrows = sb("zrows", [P, TN, ROW])
        cnt = sb("cnt", [1, E])
        thr = sb("thr", [1, E, NTOK // TB])
        over = sb("over", [1, E, NTOK // TB])
        cum = [sb(f"cum{k}", [1, E]) for k in range(4)]
        tix = sb("tix", [1, NT, E])
        past = sb("past", [1, NT, E])
        pastn = sb("pastn", [1, NT, E])
        tile_e = sb("tile_e", [1, NT])
        tile_s = sb("tile_s", [1, NT])
        tile_r = [sb(f"tile_r{k}", [1, NT]) for k in range(3)]
        tail_r = sb("tail_r", [1, E])
        tab_e = sb("tab_e", [1, NT], I32)
        tab_r = sb("tab_r", [1, NT], I32)
        tab_t = sb("tab_t", [1, E], I32)
        bsb = sb("bsb", [P, E, HC + 1])
        wsp = sb("wsp", [P, 2, 2, HID], F32R)
        hid = sb("hid", [P, 2, HID])
        braw = hid[0:E * (HC + 1), 0, 0:P]
        b1tile = [sb(f"b1tile{k}", [P, HC]) for k in range(2)]
        b2tile = [sb(f"b2tile{k}", [P, 1]) for k in range(2)]
        idt = [sb(f"idt{k}", [P, TN], I32) for k in range(2)]
        idn = [sb(f"idn{k}", [P, TN], I32) for k in range(2)]
        sht = [sb(f"sht{k}", [P, TN]) for k in range(2)]
        shn = [sb(f"shn{k}", [P, TN]) for k in range(2)]
        flat = lambda t, spec: t[:].rearrange(f"{spec} -> p ({spec[2:]})")
        kflat = [flat(kb[k], "p g j n") for k in range(2)]
        wtile = [kflat[k][:, 0:4 * HID].rearrange("p (k w n) -> p k w n", k=2, w=2) for k in range(2)]
        xTh, xTl = ([kflat[k][:, 4 * HID + i * TB:4 * HID + (i + 1) * TB] for k in range(2)] for i in range(2))
        hhl = flat(qb[0], "p b g j q").rearrange("p (k c t) -> p k c t", k=2, c=HC)
        xrow = [rows[k][:].rearrange("p a b w -> p (a b) w") for k in range(2)]
        yT = flat(ots[0], "p g q")
        yrow = [vs_all[0][:, k].rearrange("p h r -> p (h r)").rearrange("p (n d) -> p n d", n=TN) for k in range(2)]
        NY = 4
        wflat = flat(wsp, "p k w n").bitcast(F32).rearrange("p (k b d) -> p k b d", k=NY, b=TN)
        yin = [pt_all, [wflat[:, k] for k in range(NY)]]

        bank = [st.enter_context(nc.psum_tensor(f"bank{k}", [P, 512], F32)) for k in range(8)]
        wide = bank[0:3]
        scores = bank[3:5]
        heads = bank[5]
        small = bank[6:8]
        ysum = (bank[5], bank[7])

        w_in, w_in2 = sem("w_in"), sem("w_in2")
        x_in, ctx_in = two("x_in"), two("ctx_in")
        mask_in, mask_f, mask_dram = sem("mask_in"), sem("mask_f"), sem("mask_dram")
        mask_row = two("mask_row")
        ident_done, pool_done, bo_done = sem("ident_done"), sem("pool_done"), sem("bo_done")
        wst_zero, wst_done, wst_hi, vs_zero = sem("wst_zero"), sem("wst_done"), sem("wst_hi"), sem("vs_zero")
        prep = sem("prep")
        wr_T, prep2 = sem("wr_T"), sem("prep2")
        lnx_done, ln2_done, ln_chain, dve_chain = sem("lnx_done"), sem("ln2_done"), sem("ln_chain"), sem("dve_chain")
        tx_full, tx_taken, hi_done, hl_done, xbo_done = (sem(k) for k in ("tx_full", "tx_taken", "hi_done", "hl_done", "xbo_done"))
        w_full, w_part, w_free = sem("w_full"), sem("w_part"), sem("w_free")
        qblk, kblk, mrow = two("qblk"), two("kblk"), two("mrow")
        v_full, v_taken = sem("v_full"), sem("v_taken")
        mx_done, nm_full, nm_split = sem("mx_done"), sem("nm_full"), sem("nm_split")
        b_full, exp_done, pv_done = sem("b_full"), sem("exp_done"), sem("pv_done")
        ot_taken, ott_full, rc_done, on_done = sem("ot_taken"), sem("ott_full"), sem("rc_done"), sem("on_done")
        ont_full, ont_taken, wo_full, x1_done = sem("ont_full"), sem("ont_taken"), sem("wo_full"), sem("x1_done")
        x2t_full, x2t_taken, rl_full, rl_taken = sem("x2t_full"), sem("x2t_taken"), sem("rl_full"), sem("rl_taken")
        top_max, top_sub, top_exp, top_chain, routed = (sem(k) for k in ("top_max", "top_sub", "top_exp", "top_chain", "routed"))
        pos_full, pos_taken, pos_chain, pos_done, hot_done, kept = (
            sem(k) for k in ("pos_full", "pos_taken", "pos_chain", "pos_done", "hot_done", "kept"))
        scat, rows2, ids_done = two("scat"), sem("rows2"), sem("ids_done")
        zrow_done, spare_done, b_in = sem("zrow_done"), sem("spare_done"), sem("b_in")
        wraw_in, wsplit, wsave = sem("wraw_in"), sem("wsplit"), sem("wsave")
        cnt_full, tables, tail_done = sem("cnt_full"), sem("tables"), sem("tail_done")
        x_tile, w1_tile, w2_tile, y_out = two("x_tile"), two("w1_tile"), two("w2_tile"), two("y_out")
        xt_full, xt_hi, xt_lo, id_done, idn_done = (sem(k) for k in ("xt_full", "xt_hi", "xt_lo", "id_done", "idn_done"))
        h_full, h_hi, h_val, h_lo = sem("h_full"), sem("h_hi"), sem("h_val"), sem("h_lo")
        yt_full, yt_taken, yr_full, yr_taken = sem("yt_full"), sem("yt_taken"), sem("yr_full"), sem("yr_taken")
        y_in, fin_a, fin_b = [sem(f"y_in{k}") for k in range(4)], sem("fin_a"), sem("fin_b")
        xd = nc.dram_tensor("xd", (SPARE + TB, ROW), F32, kind="Internal").ap()
        yd = nc.dram_tensor("yd", (2 * NTOK, D), F32, kind="Internal").ap()
        wd = nc.dram_tensor("wd", (E, P, 4 * HID), F32R, kind="Internal").ap()
        maskd = nc.dram_tensor("maskd", (B, KL), F32R, kind="Internal").ap()
        out_done = sem("out_done")

        def slots(eng, body):
            for s in range(-2, 4):
                body(At(s // 2, s % 2), s)
            with eng.Fori(2, NCH // 2 - 2) as pair:
                body(At(pair, 0), None)
                body(At(pair, 1), None)
            for s in range(NCH - 4, NCH + 2):
                body(At(s // 2, s % 2), s)

        def tiles(eng, body):
            for t in range(-1, 4):
                body(At(t // 2, t % 2), t)
            with eng.Fori(2, NT // 2 - 1) as pair:
                body(At(pair, 0), None)
                body(At(pair, 1), None)
            for t in range(2 * (NT // 2 - 1), NT + 1):
                body(At(t // 2, t % 2), t)

        WSLOTS = {n: e for e, n in enumerate((0, 1, *range(NCH - 4, NCH + 2)))}

        def alone(eng, semaphore, value):
            if not isinstance(value, int):
                value = eng.to_reg(value)
                eng.wait_ge(ident_done, 2)
            eng.wait_ge(semaphore, value)

        def has(n, ahead):
            return n is None or 0 <= n + ahead < NT

        def third(n, ahead):
            return n is None or n + ahead >= 2

        def exists(s, back):
            return s is None or 0 <= s + back < NCH

        block = st.enter_context(nc.Block())

        @block.sync
        def _(sp):
            def load_x(c):
                sp.dma_start(xres[:, bass.ds(c.count(2), 2), :],
                             x[bass.ds(c.count(2), 2), :, :].rearrange("b s d -> s b d")).then_inc(x_in[c.parity], 16)

            load_x(At(0, 0))
            for k, w in enumerate((Wq, Wk, Wv, Wo)):
                sp.dma_start(wraw[:, k, :], w).then_inc(w_in, 16)
            for k, b in enumerate((bq, bk)):
                sp.dma_start(brow[:, k, :], b.rearrange("(a n) -> a n", a=1).to_broadcast([3, D])).then_inc(w_in, 16)
            sp.dma_start(wrraw[:, :], Wr).then_inc(w_in, 16)
            sp.dma_start(masku[:, :], mask).then_inc(mask_in, 16)
            sp.dma_start(braw[0:E * HC, :], b1.rearrange("e (c p) -> (e c) p", p=P)).then_inc(b_in, 16)
            sp.dma_start(braw[E * HC:E * HC + E, :], b2).then_inc(b_in, 16)
            sp.dma_start(bvb[:, :], bv.rearrange("(a n) -> a n", a=1).to_broadcast([P, D])).then_inc(w_in2, 16)
            sp.dma_start(bob[:, :], bo.rearrange("(a n) -> a n", a=1).to_broadcast([P, D])).then_inc(w_in2, 16)

            def load_ctx(c):
                sp.dma_start(ctxin[c.parity][:, :, :],
                             ctx[bass.ds(c.count(2), 2), :, :].rearrange("b s d -> s b d")).then_inc(ctx_in[c.parity], 16)

            load_ctx(At(0, 0))
            load_x(At(0, 1))
            load_ctx(At(0, 1))
            sp.wait_ge(mask_f, 1)
            sp.dma_start(maskd.bitcast(F32), maskf[:, :].bitcast(F32)).then_inc(mask_dram, 16)
            sp.wait_ge(mask_dram, 16)

            sp.wait_ge(zrow_done, 2)
            sp.dma_start(xd[SPARE:SPARE + TB, :].rearrange("(p n) w -> p n w", p=P), zrows[:, :, :]).then_inc(spare_done, 16)

            def slot(s, n):
                if n in WSLOTS:
                    e = WSLOTS[n]
                    if e >= 1:
                        sp.wait_ge(wsplit, 2 * e)
                    sp.dma_start(hid[:, 0, :], W1[e]).then_inc(wraw_in, 16)
                    sp.dma_start(hid[:, 1, :].rearrange("p (c n) -> p c n", c=HC),
                                 W2[e].rearrange("(c p) n -> p c n", p=P)).then_inc(wraw_in, 16)
                if exists(n, 2):
                    c = s + 2
                    if n is None or n >= 0:
                        sp.wait_ge(w_full, s.count(12, 4))
                    if n is not None and n < 0:
                        sp.wait_ge(prep, 1)
                    sp.dma_start(augx[c.parity][2:3, 0:K2].bitcast(F32).rearrange("a (b k) -> a b k", b=2),
                                 maskd.bitcast(F32)[bass.ds(c.count(2), 2), :].rearrange("(a b) k -> a b k", a=1)).then_inc(mask_row[c.parity], 16)
                if exists(n, 4):
                    if exists(n, 2):
                        sp.wait_ge(lnx_done, s.count(1, 3))
                    load_x(s + 4)
                if exists(n, 3) and (n is None or n >= -1):
                    sp.wait_ge(tx_full, s.count(1, 2))
                    load_ctx(s + 3)
                if exists(n, 1):
                    c = s + 1
                    for ready, dense, blocks, done in ((2, ks, kb, kblk), (4, qs, qb, qblk)):
                        sp.wait_ge(w_free, c.count(12, ready))
                        if n is not None and n < 1:
                            sp.wait_ge(pool_done, 4)
                        for j in range(J):
                            src, dst = (x[c.parity][R * j:R * j + R] for x in (dense, blocks))
                            if blocks is qb:
                                src, dst = src.rearrange("p b g q -> p (b g) q"), dst.rearrange("p b g j q -> p (b g) j q")
                            sp.dma_start(dst[:, :, j, :].bitcast(F32), src.bitcast(F32)).then_inc(done[c.parity], 16)
                    sp.wait_ge(nm_split, c.count(2, 2))
                    sp.wait_ge(qblk[c.parity], c.uses(64))
                    for half in range(2):
                        row = MHI + half
                        sp.dma_start(qb[c.parity][row:row + 1].rearrange("a b g j q -> a (b g j) q").bitcast(F32),
                                     negm[c.parity][:, half, :].bitcast(F32)).then_inc(mrow[c.parity], 16)

                if n in WSLOTS:
                    sp.wait_ge(wsplit, 2 * (WSLOTS[n] + 1))
                    sp.dma_start(wd[WSLOTS[n]].bitcast(F32), wsp[:].rearrange("p k w n -> p (k w n)").bitcast(F32)).then_inc(wsave, 16)

            slots(sp, slot)
            sp.wait_ge(tables, 1)
            for e in range(E):
                row = sp.value_load(tab_t[0:1, e:e + 1], min_val=0, max_val=SPARE - TB)
                sp.dma_start(xd[bass.ds(row, TB), :].rearrange("(p n) w -> p n w", p=P), zrows[:, :, :]).then_inc(tail_done, 16)
            for k in range(2):
                sp.wait_ge(scat[k], 64 * (NCH // 2))
            sp.wait_ge(wsave, 16 * E)
            sp.wait_ge(tail_done, 16 * E)
            sp.wait_ge(spare_done, 16)

            def expert(t):
                return sp.value_load(tab_e[0:1, bass.ds(t.count(1), 1)], min_val=0, max_val=E - 1)

            def step(t, n):
                ahead = range(0, 4) if n == -1 else (3,)
                for d in ahead:
                    if has(n, d - 1):
                        em = expert(t + (d - 1))
                    if has(n, d):
                        f = t + d
                        e = expert(f)
                        row = sp.value_load(tab_r[0:1, bass.ds(f.count(1), 1)], min_val=0, max_val=SPARE)
                        if third(n, d):
                            sp.wait_ge(xt_full, f.count(1, -1))
                            sp.wait_ge(id_done, f.count(1, -1))
                        sp.dma_start(xrow[f.parity][:, :, :],
                                     xd[bass.ds(row, TB), :].rearrange("(p n) w -> p n w", p=P)).then_inc(x_tile[f.parity], 16)
                        if third(n, d):
                            sp.wait_ge(h_full, f.count(HC, -HC))
                        sp.dma_start(wtile[f.parity][:, :, 0, :].bitcast(F32),
                                     wd.bitcast(F32)[bass.ds(e, 1)].rearrange("a p (k w n) -> (a p) k w n", k=2, w=2)[:, :, 0, :]).then_inc(w1_tile[f.parity], 16)
                    if has(n, d - 1):
                        m = t + (d - 1)
                        if third(n, d - 1):
                            sp.wait_ge(yt_full, m.count(1, -1))
                        sp.dma_start(wtile[m.parity][:, :, 1, :].bitcast(F32),
                                     wd.bitcast(F32)[bass.ds(em, 1)].rearrange("a p (k w n) -> (a p) k w n", k=2, w=2)[:, :, 1, :]).then_inc(w2_tile[m.parity], 16)
                    if has(n, d):
                        if third(n, d):
                            sp.wait_ge(h_val, f.count(HC, -HC))
                        sp.dma_start(b1tile[f.parity][:, :], bsb[:, bass.ds(e, 1), 0:HC].rearrange("p a c -> p (a c)")).then_inc(w1_tile[f.parity], 16)
                    if has(n, d - 1):
                        if third(n, d - 1):
                            sp.wait_ge(yt_taken, m.count(1, -1))
                        sp.dma_start(b2tile[m.parity][:, :], bsb[:, bass.ds(em, 1), HC:HC + 1].rearrange("p a c -> p (a c)")).then_inc(w2_tile[m.parity], 16)

            tiles(sp, step)

            for k in range(2):
                last = NT - 1 - (NT - 1 - k) % 2
                sp.wait_ge(y_out[k], 64 * (last // 2 + 1))

            def load_y(k, q):
                for i in range(2):
                    sp.dma_start(yin[i][k][:, :, :],
                                 yd[bass.ds(q * TB + i * NTOK, TB), :].rearrange("(b t) d -> t b d", t=P)).then_inc(y_in[k], 16)

            for k in range(NY):
                load_y(k, k)
            with sp.Fori(0, NQ // NY - 1) as it:
                for k in range(NY):
                    sp.wait_ge(fin_b, it * NY + (k + 1))
                    load_y(k, it * NY + (k + NY))

        @block.gpsimd
        def _(pool):
            g = nc.gpsimd
            g.memset(ident[:, :], 0.0).then_inc(ident_done, 1)
            pool.wait_ge(ident_done, 1)
            g.affine_select(out=ident[:, :], in_=ident[:, :], compare_op=ALU.not_equal, fill=1.0, base=0,
                            pattern=[[-1, P]], channel_multiplier=1).then_inc(ident_done, 1)
            for k in range(2):
                g.memset(kb[k][:, :, :, :].bitcast(F32), 0.0).then_inc(pool_done, 1)
                g.memset(qb[k][:].bitcast(F32), 0.0).then_inc(pool_done, 1)

            for k in range(2):
                g.memset(vs[k][:], 0.0).then_inc(vs_zero, 1)
            pool.wait_ge(vs_zero, 2)
            for k in range(2):
                g.memset(vs[k][:, :, :, DH:DH + 1], 1.0).then_inc(vs_zero, 1)
            g.memset(trif[:, :], 1.0).then_inc(kept, 1)
            pool.wait_ge(kept, 1)
            g.affine_select(out=trif[:, :], in_=trif[:, :], compare_op=ALU.is_gt, fill=0.0, base=0,
                            pattern=[[1, P]], channel_multiplier=-1).then_inc(kept, 1)
            g.memset(zrows[:, :, :], 0.0).then_inc(zrow_done, 1)
            pool.wait_ge(zrow_done, 1)
            g.memset(zrows[:, :, D:D + 1].bitcast(I32), NOWHERE).then_inc(zrow_done, 1)
            for k in range(2):
                g.memset(rows[k][:, :, :, D:ROW], 0.0).then_inc(kept, 1)
            g.iota(eidx[:, :], [[1, E]], base=0, channel_multiplier=0, allow_small_or_imprecise_dtypes=True).then_inc(kept, 1)
            g.iota(region[:, :], [[REGION, E]], base=0, channel_multiplier=0, allow_small_or_imprecise_dtypes=True).then_inc(kept, 1)
            g.iota(idf[:, :], [[S, 2], [NTOK, 2]], base=0, channel_multiplier=1, allow_small_or_imprecise_dtypes=True).then_inc(kept, 1)
            g.iota(thr[:], [[0, E], [TB, NTOK // TB]], base=0, channel_multiplier=0, allow_small_or_imprecise_dtypes=True).then_inc(kept, 1)
            g.iota(tix[:], [[1, NT], [0, E]], base=0, channel_multiplier=0, allow_small_or_imprecise_dtypes=True).then_inc(kept, 1)
            pool.wait_ge(kept, 9)

            def slot(s, n):
                if exists(n, 2):
                    c = s + 2
                    if n == -2:
                        pool.wait_ge(bo_done, 4)
                    alone(pool, lnx_done, c.count(1, 1))
                    for b in range(2):
                        xb = xres[:, bass.ds(c.count(2, b), 1), :]
                        last = g.tensor_tensor(xb, xb, bob[:, :].rearrange("p (a d) -> p a d", a=1), ALU.add)
                    last.then_inc(xbo_done, 1)
                if exists(n, 2):
                    k = c.parity
                    pool.wait_ge(tx_taken, c.count(1, 1))
                    if n is None or n >= 0:
                        alone(pool, w_full, s.count(12, 4))
                    g.tensor_scalar(xcTh[k][:, :], xcT[k][:, :], 1.0, 0.0, ALU.mult, ALU.add).then_inc(hi_done, 1)
                    alone(pool, hi_done, c.count(1, 1))
                    g.tensor_tensor(xcTl[k][:, :], xcT[k][:, :], xcTh[k][:, :], ALU.subtract).then_inc(hl_done, 1)
                if n in WSLOTS:
                    e = WSLOTS[n]
                    pool.wait_ge(wraw_in, 32 * (e + 1))
                    if e >= 1:
                        pool.wait_ge(wsave, 16 * e)
                    g.tensor_scalar(wsp[:, 0], hid[:], 1.0, 0.0, ALU.mult, ALU.add).then_inc(wsplit, 1)
                    pool.wait_ge(wsplit, 2 * e + 1)
                    g.tensor_tensor(wsp[:, 1], hid[:], wsp[:, 0], ALU.subtract).then_inc(wsplit, 1)
                if exists(n, -1):
                    r = s + -1
                    alone(pool, ln2_done, r.count(1, 1))
                    rw = rows[r.parity]
                    g.tensor_scalar(rw[:, :, 1, 0:D], rw[:, :, 0, 0:D], 1.0, 0.0, ALU.mult, ALU.add).then_inc(rows2, 1)
                    g.tensor_scalar(rw[:, :, :, D:D + 1].bitcast(I32).rearrange("p b k a -> p (b k a)"), idf[:, :], 1.0, 0.0, ALU.mult, ALU.add).then_inc(rows2, 1)
                    alone(pool, rows2, r.count(3, 2))
                    g.tensor_scalar(idf[:, :], idf[:, :], 1.0, float(N2), ALU.mult, ALU.add).then_inc(rows2, 1)
                    alone(pool, rows2, r.count(3, 3))
                if exists(n, -2):
                    r = s + -2
                    alone(pool, pos_done, r.count(1, 1))
                    for bk in range(4):
                        g.indirect_dma_start(xd, bass.IndirectOffsetOnAxis(ap=posi[r.parity][:, bk:bk + 1], axis=0),
                                             rows[r.parity][:, bk // 2, bk % 2, :], None,
                                             bounds_check=SPARE - 1, oob_is_err=False).then_inc(scat[r.parity], 16)

            slots(pool, slot)

            def keep_places(t, n, d):
                f = t + d
                alone(pool, x_tile[f.parity], f.uses(16))
                if third(n, d):
                    alone(pool, idn_done, f.count(1, -1))
                g.tensor_copy(sht[f.parity][:, :], xrow[f.parity][:, :, D + 1])
                g.tensor_copy(idt[f.parity][:, :], xrow[f.parity][:, :, D:D + 1].bitcast(I32).rearrange("p n a -> p (n a)")).then_inc(id_done, 1)

            def step(t, n):
                if n == -1:
                    keep_places(t, n, 1)
                if has(n, -1):
                    p = t + -1
                    k = p.parity
                    alone(pool, id_done, p.count(1, 1))
                    if third(n, -1):
                        alone(pool, y_out[k], p.uses(64, -64))
                    g.tensor_copy(shn[k][:, :], sht[k][:, :])
                    g.tensor_copy(idn[k][:, :], idt[k][:, :]).then_inc(idn_done, 1)
                if has(n, 1) and n != -1:
                    keep_places(t, n, 1)
                if has(n, -1):
                    alone(pool, idn_done, p.count(1, 1))
                    alone(pool, yr_taken, p.count(1, 1))
                    for j in range(TN):
                        g.indirect_dma_start(yd, bass.IndirectOffsetOnAxis(ap=idn[k][:, j:j + 1], axis=0), yrow[k][:, j, :], None,
                                             bounds_check=2 * NTOK - 1, oob_is_err=False).then_inc(y_out[k], 16)

            tiles(pool, step)

        @block.vector
        def _(dve):
            v = nc.vector
            chain = [0]

            def link(ins):
                chain[0] += 1
                ins.then_inc(dve_chain, 1)
                dve.wait_ge(dve_chain, chain[0])

            def put(ins):
                chain[0] += 1
                ins.then_inc(dve_chain, 1)

            def settle():
                dve.wait_ge(dve_chain, chain[0])

            def normalise(m, first):
                s, k = m
                src = small[0][:, :].rearrange("p (h r) -> p h r", h=H)
                dve.wait_ge(ott_full, s.count(2, k + 1))
                if not first:
                    dve.wait_ge(on_done, s.count(2, k))
                v.reciprocal(rden[:].rearrange("p g j -> p (g j)"), src[:, :, DH]).then_inc(rc_done, 1)
                dve.wait_ge(rc_done, s.count(2, k + 1))
                if not first:
                    dve.wait_ge(ont_full, s.count(2, k))
                v.tensor_tensor(on[:], src[:, :, 0:DH],
                                rden[:].rearrange("p g (j a) -> p (g j) a", a=1).to_broadcast([P, H, DH]),
                                ALU.mult).then_inc(on_done, 1)

            def residual(m):
                s, k = m
                dve.wait_ge(wo_full, s.count(2, k + 1))
                dve.wait_ge(xbo_done, s.count(1, 0 if k < 0 else 1))
                xb = xres[:, bass.ds(s.count(2, k), 1), :].rearrange("p a d -> p (a d)")
                v.tensor_tensor(xb, small[1][:, 0:D], xb, ALU.add).then_inc(x1_done, 1)

            def slot(s, n):
                c = s + 1
                k = c.parity
                LN = 14
                if exists(n, 1) and (n is None or n >= 1):
                    dve.wait_ge(b_full, s.count(8))
                    dve.wait_ge(pv_done, s.count(8))

                def unsplit(u):
                    dve.wait_ge(w_part, c.count(4, u + 1))
                    gs = slice(2 * (u % 2), 2 * (u % 2) + 2)
                    if u < 2:
                        views = ks[k][:, gs, :], *(w[:, 0:2 * KW].rearrange("p (g n) -> p g n", g=2)[:, :, 0:K2]
                                                   for w in (wide[u % 3], part[u % 2]))
                    else:
                        views = qs[k][:, :, gs, :], *(w[:, 0:2 * N2].rearrange("p (g b q) -> p b g q", g=2, b=2)
                                                      for w in (wide[u % 3], part[u % 2]))
                    v.tensor_tensor(*views, ALU.subtract).then_inc(w_free, 1)

                def best(u):
                    b, gg = divmod(u, G)
                    dve.wait_ge(w_full, c.count(12, 5 + u))
                    v.tensor_reduce(mx[:, b, gg, :], wide[(4 + u) % 3][:, 0:J * KL].rearrange("p (j k) -> p j k", j=J),
                                    op=ALU.max, axis=AX.X).then_inc(w_free, 1)

                def newton(k):
                    if not todo:
                        return
                    dve.wait_ge(ln_chain, (s + 3).count(LN, 3 + k))
                    if k == 0:
                        v.tensor_scalar(nve[:, :], ve[:, :], -0.5, None, ALU.mult)
                        last = v.tensor_scalar(vbits[:, :], ve[:, :].bitcast(I32), 1, None, ALU.logical_shift_right)
                    elif k == 1:
                        last = v.tensor_scalar(ys[0][:, :].bitcast(I32), vbits[:, :], -1.0, float(0x5F3759DF), ALU.mult, ALU.add)
                    elif k % 3 == 2:
                        last = v.tensor_tensor(yy[:, :], ys[(k - 2) // 3 % 2][:, :], ys[(k - 2) // 3 % 2][:, :], ALU.mult)
                    elif k % 3 == 0:
                        last = v.tensor_tensor(vyy[:, :], yy[:, :], nve[:, :], ALU.mult)
                    else:
                        old, new = (k - 4) // 3 % 2, 1 - (k - 4) // 3 % 2
                        last = v.scalar_tensor_tensor(ys[new][:, :], vyy[:, :], 1.5, ys[old][:, :], ALU.add, ALU.mult)
                    last.then_inc(ln_chain, 1)

                r = s + -2

                def route(k):
                    if not exists(n, -2):
                        return
                    if k == 0:
                        dve.wait_ge(rl_taken, r.count(1, 1))
                        v.tensor_copy(pick[:, :].rearrange("p (b k) -> p b k", b=2), tidx[:, :, 0:2]).then_inc(top_chain, 1)
                    elif k == 1:
                        dve.wait_ge(top_exp, r.count(1, 1))
                        v.tensor_reduce(tsum[:, :], tope[:], op=ALU.add, axis=AX.X).then_inc(top_chain, 1)
                    elif k == 2:
                        dve.wait_ge(top_chain, r.count(6, 2))
                        v.reciprocal(tinv[:, :], tsum[:, :]).then_inc(top_chain, 1)
                    elif k == 3:
                        if exists(n, -3):
                            dve.wait_ge(pos_done, r.count(1))
                        for b in range(2):
                            last = v.tensor_tensor(hot[:, b], pick[:, 2 * b:2 * b + 2].rearrange("p (k a) -> p k a", a=1).to_broadcast([P, 2, E]),
                                                   eidx[:].rearrange("p (a e) -> p a e", a=1).to_broadcast([P, 2, E]), ALU.is_equal)
                        last.then_inc(top_chain, 1)
                    elif k == 4:
                        dve.wait_ge(top_chain, r.count(6, 4))
                        v.tensor_tensor(rows[r.parity][:, :, :, D + 1], tope[:, :, 0:2],
                                        tinv[:].rearrange("p (b a) -> p b a", a=1).to_broadcast([P, 2, 2]),
                                        ALU.mult).then_inc(routed, 1)
                        if exists(n, -3):
                            dve.wait_ge(pos_chain, r.count(3))
                        v.tensor_tensor(taken[:], hot[:, :, 0, :], hot[:, :, 1, :], ALU.add).then_inc(top_chain, 1)
                    else:
                        dve.wait_ge(top_chain, r.count(6, 5))
                        v.tensor_tensor(taken2[:, :], taken[:, 0, :], taken[:, 1, :], ALU.add).then_inc(top_chain, 1)

                def position(k):
                    if not exists(n, -2):
                        return
                    if k == 0:
                        dve.wait_ge(pos_full, r.count(1, 1))
                        v.tensor_tensor(place[:], small[1][:, 16:16 + 2 * E].rearrange("p (b e) -> p b e", b=2),
                                        region[:].rearrange("p (a e) -> p a e", a=1).to_broadcast([P, 2, E]), ALU.add).then_inc(pos_taken, 1)
                        v.tensor_tensor(before[:, :], before[:, :], taken2[:, :], ALU.add).then_inc(pos_chain, 1)
                    elif k == 1:
                        dve.wait_ge(pos_taken, r.count(1, 1))
                        for b in range(2):
                            last = v.tensor_tensor(placed[:, 2 * b:2 * b + 2, :], hot[:, b, :, :],
                                                   place[:, b:b + 1, :].to_broadcast([P, 2, E]), ALU.mult)
                        last.then_inc(pos_chain, 1)
                    elif k == 2:
                        dve.wait_ge(pos_chain, r.count(3, 2))
                        v.tensor_reduce(posf[:, :], placed[:], op=ALU.add, axis=AX.X).then_inc(pos_chain, 1)
                    else:
                        dve.wait_ge(pos_chain, r.count(3, 3))
                        if exists(n, -4):
                            dve.wait_ge(scat[r.parity], r.uses(64, -64))
                        v.tensor_copy(posi[r.parity][:, :], posf[:, :]).then_inc(pos_done, 1)

                def norm_x():
                    if exists(n, 3):
                        f = s + 3
                        dve.wait_ge(ln_chain, (s + 3).count(LN, 14))
                        if exists(n, 1):
                            dve.wait_ge(tx_full, s.count(1, 2))
                        for b in range(2):
                            last = v.tensor_scalar(xn[f.parity][:, b:b + 1, :], xres[:, bass.ds(f.count(2, b), 1), :],
                                                   mv[:, b, 0:1], ys[1][:, b:b + 1], ALU.subtract, ALU.mult)
                        last.then_inc(lnx_done, 1)

                def norm_x1():
                    if exists(n, -1):
                        m = s + -1
                        dve.wait_ge(ln_chain, (s + 3).count(LN, 14))
                        if exists(n, -2):
                            dve.wait_ge(x2t_full, s.count(1, -1))
                        if exists(n, -3):
                            dve.wait_ge(scat[m.parity], m.uses(64, -64))
                        for b in range(2):
                            last = v.tensor_scalar(rows[m.parity][:, b:b + 1, 0, 0:D], xres[:, bass.ds(m.count(2, b), 1), :],
                                                   mv[:, 2 + b, 0:1], ys[1][:, 2 + b:3 + b], ALU.subtract, ALU.mult)
                        last.then_inc(ln2_done, 1)

                if exists(n, -1):
                    normalise((s, -1), False)
                route(0)
                if exists(n, 1):
                    unsplit(0)
                    route(1)
                    unsplit(1)
                else:
                    route(1)
                route(2)
                route(3)
                if exists(n, -1):
                    residual((s, -1))
                route(4)
                todo = []
                if exists(n, 3):
                    f = s + 3
                    dve.wait_ge(x_in[f.parity], f.uses(16))
                    todo += [(b, xres[:, bass.ds(f.count(2, b), 1), :]) for b in range(2)]
                if exists(n, -1):
                    dve.wait_ge(x1_done, s.count(2))
                    todo += [(2 + b, xres[:, bass.ds(s.count(2, b - 2), 1), :]) for b in range(2)]
                if todo:
                    if exists(n, 2):
                        dve.wait_ge(lnx_done, (s + 3).count(1))
                    if exists(n, -2):
                        dve.wait_ge(ln2_done, s.count(1, -1))
                    for b, src in todo:
                        last = v.bn_stats(stats[:, b, :], src.rearrange("p a d -> p (a d)"))
                    last.then_inc(ln_chain, 1)
                route(5)
                if todo:
                    alone(dve, ln_chain, (s + 3).count(LN, 1))
                    for b, src in todo:
                        last = v.bn_aggr(mv[:, b, :], stats[:, b, :])
                    last.then_inc(ln_chain, 1)
                if exists(n, 1):
                    unsplit(2)
                if todo:
                    dve.wait_ge(ln_chain, (s + 3).count(LN, 2))
                    v.tensor_scalar(ve[:, :], mv[:, :, 1], EPS, None, ALU.add).then_inc(ln_chain, 1)
                if exists(n, 1):
                    unsplit(3)
                newton(0)
                newton(1)
                newton(2)
                if exists(n, 1) and (n is None or n >= 0):
                    dve.wait_ge(nm_full, c.count(1))
                for u in range(8):
                    if exists(n, 1):
                        best(u)
                    if u < 4:
                        newton(2 * u + 3)
                    if u in (0, 7):
                        position(u // 7)
                    if u == 3 and exists(n, 0):
                        normalise((s, 0), n == 0)
                    if u < 4:
                        newton(2 * u + 4)
                    if u == 4:
                        norm_x1()
                if exists(n, 0):
                    residual((s, 0))
                if exists(n, 1):
                    dve.wait_ge(nm_full, c.count(1, 1))
                    nsrc = small[0][0:J * G * 2, 0:S]
                    v.tensor_scalar(negm[k][:, 0, :], nsrc, -1.0, None, ALU.mult).then_inc(nm_split, 1)
                    dve.wait_ge(nm_split, c.count(2, 1))
                    v.scalar_tensor_tensor(negm[k][:, 1, :], nsrc, -1.0, negm[k][:, 0, :], ALU.mult, ALU.subtract).then_inc(nm_split, 1)
                if exists(n, -1):
                    alone(dve, rl_full, s.count(1))
                    lg = small[1][:, 0:2 * E].rearrange("p (b e) -> p b e", b=2)
                    if n != 1:
                        alone(dve, routed, s.count(1, -1))
                    for b in range(2):
                        last = v.max(top[:, b, :], lg[:, b, :])
                    last.then_inc(top_max, 1)
                    alone(dve, top_max, s.count(1))
                    for b in range(2):
                        last = v.max_index(tidx[:, b, :], top[:, b, :], lg[:, b, :])
                    last.then_inc(rl_taken, 1)
                    v.tensor_tensor(topd[:], top[:], top[:, :, 0:1].to_broadcast([P, 2, E]), ALU.subtract).then_inc(top_sub, 1)
                position(2)
                norm_x()
                position(3)

            v.memset(wst[0][:], 0.0)
            v.memset(wst[1][:], 0.0).then_inc(wst_zero, 1)
            put(v.memset(mv[:], 1.0))
            for k in range(2):
                put(v.memset(xcT[k][:, N2 + K2:N2 + KW], 0.0))
            link(v.memset(stats[:], 1.0))
            dve.wait_ge(ident_done, 2)
            slot(At(-2, 1), -3)

            dve.wait_ge(mask_in, 16)
            v.tensor_copy(maskf[:, :], masku[:, :]).then_inc(mask_f, 1)
            for k in range(4):
                put(v.memset(bst[k][:], 0.0))
            put(v.memset(ones2[:].bitcast(F32), 1.0))
            for k in range(2):
                put(v.memset(augx[k][:].bitcast(F32), 1.0))
            settle()
            put(v.memset(bst[2][:, :, :, MSK:MSK + 1], MASKED))
            put(v.memset(bst[0][:, :, :, MSK:MSK + 1], 1.0))
            put(v.memset(bst[1][:, :, :, MHI:MLO + 1], 1.0))
            dve.wait_ge(ident_done, 2)
            idv = ident[:, :].rearrange("p (j r) -> p j r", j=J)
            for k, r0 in ((0, 16), (1, 8)):
                put(v.tensor_reduce(rowsel[k][:, :], idv[:, :, r0:r0 + 8], op=ALU.add, axis=AX.XY))
            dve.wait_ge(w_in, 7 * 16)
            link(v.tensor_scalar(keep[:, :], ident[0:3, 2:3], -1.0, 1.0, ALU.mult, ALU.add))
            for k in range(2):
                bsrc = brow[:, k, :].rearrange("a (g j d) -> a (g j) d", g=G, j=J)
                for c in range(3):
                    put(v.tensor_copy(bst[k][:].rearrange("a g j r -> a (g j) r")[:, :, 8 * c:8 * c + 8], bsrc))
            dve.wait_ge(bo_done, 1)
            v.tensor_copy(bvT[:, :], bank[3][:, 0:P]).then_inc(bo_done, 1)
            dve.wait_ge(w_in2, 32)
            dve.wait_ge(bo_done, 3)
            v.tensor_tensor(bob[:, :], bank[4][:, 0:D], bob[:, :], ALU.add).then_inc(bo_done, 1)

            settle()
            for k in range(2):
                link(v.tensor_scalar(bst[k][:], bst[k][:], keep[:, 0:1], None, ALU.mult))
                if k == 1:
                    link(v.scalar_tensor_tensor(bst[3][:], bst[2][:], ident[0:3, 2:3], bst[1][:], ALU.mult, ALU.add))
                src = bst[3] if k == 1 else bst[0]
                link(v.tensor_scalar(augw[:], src[:], ident[0:3, 1:2], None, ALU.mult))
                link(v.tensor_tensor(aug[k][:], src[:], augw[:], ALU.subtract))
            for k, halves in enumerate((wk3, wq3)):
                dve.wait_ge(wst_hi, k + 1)
                put(v.tensor_tensor(halves[1][:], wst[k][:], halves[0][:], ALU.subtract))
            dve.wait_ge(wr_T, 2)
            put(v.tensor_copy(bsb[:, :, 0:HC], small[0][:, E:E + E * HC].rearrange("p (e c) -> p e c", e=E)))
            put(v.tensor_copy(bsb[:, :, HC:HC + 1], small[0][:, E + E * HC:2 * E + E * HC].rearrange("p (e a) -> p e a", a=1)))
            v.tensor_copy(wrT[:, :], small[0][:, 0:E]).then_inc(prep, 1)
            dve.wait_ge(kept, 9)
            put(v.tensor_copy(tri[:, :], trif[:, :]))
            put(v.memset(ones[:, :], 1.0))
            link(v.memset(before[:, :], 0.0))

            slots(dve, slot)

            dve.wait_ge(cnt_full, 1)
            link(v.tensor_copy(cnt[:, :], small[0][0:1, 0:E]))
            link(v.tensor_tensor(over[:], cnt[:].rearrange("a (e j) -> a e j", j=1).to_broadcast([1, E, NTOK // TB]), thr[:], ALU.is_gt))
            link(v.tensor_reduce(cum[0][:, :], over[:], op=ALU.add, axis=AX.X))
            for k, step in enumerate((1, 2, 4)):
                old, new = cum[k], cum[k + 1]
                link(v.tensor_copy(new[:, 0:step], old[:, 0:step]))
                link(v.tensor_tensor(new[:, step:E], old[:, step:E], old[:, 0:E - step], ALU.add))
            link(v.tensor_tensor(past[:], tix[:], cum[3][:].rearrange("a (j e) -> a j e", j=1).to_broadcast([1, NT, E]), ALU.is_ge))
            link(v.tensor_reduce(tile_e[:, :], past[:], op=ALU.add, axis=AX.X))
            link(v.tensor_tensor(pastn[:], past[:], cum[0][:].rearrange("a (j e) -> a j e", j=1).to_broadcast([1, NT, E]), ALU.mult))
            link(v.tensor_reduce(tile_s[:, :], pastn[:], op=ALU.add, axis=AX.X))
            link(v.tensor_tensor(tile_r[0][:, :], tix[:, :, 0], tile_s[:, :], ALU.subtract))
            link(v.tensor_scalar(tile_r[1][:, :], tile_e[:, :], float(REGION), None, ALU.mult))
            link(v.scalar_tensor_tensor(tile_r[2][:, :], tile_r[0][:, :], float(TB), tile_r[1][:, :], ALU.mult, ALU.add))
            link(v.tensor_scalar(tab_r[:, :], tile_r[2][:, :], float(SPARE), None, ALU.min))
            link(v.tensor_scalar(tab_e[:, :], tile_e[:, :], float(E - 1), None, ALU.min))
            v.tensor_tensor(tab_t[:, :], cnt[:, :], region[0:1, :], ALU.add).then_inc(tables, 1)

            def lower(t, c):
                dve.wait_ge(h_val, t.count(HC, c + 1))
                v.tensor_tensor(hhl[:, 1, c, :], hid[:, c % 2, :], hhl[:, 0, c, :], ALU.subtract).then_inc(h_lo, 1)

            def lower_x(t):
                dve.wait_ge(xt_hi, t.count(1, 1))
                v.tensor_tensor(xTl[t.parity], bank[4][:, :], xTh[t.parity], ALU.subtract).then_inc(xt_lo, 1)

            def step(t, n):
                if n == -1:
                    lower_x(t + 1)
                for c in range(HC):
                    if has(n, 1):
                        lower(t + 1, c)
                    if c == 1 and has(n, 2):
                        lower_x(t + 2)
                    if c == 2 and has(n, -1):
                        p = t + -1
                        dve.wait_ge(yr_full, p.count(1, 1))
                        if third(n, -1):
                            dve.wait_ge(y_out[p.parity], p.uses(64, -64))
                        dve.wait_ge(idn_done, p.count(1, 1))
                        v.tensor_tensor(yrow[p.parity][:], bank[6][:, :].rearrange("p (n d) -> p n d", n=TN),
                                        shn[p.parity][:].rearrange("p (n a) -> p n a", a=1).to_broadcast([P, TN, D]), ALU.mult).then_inc(yr_taken, 1)
                if has(n, 0):
                    dve.wait_ge(yt_full, t.count(1, 1))
                    if has(n, -1):
                        dve.wait_ge(yr_full, t.count(1))
                    v.tensor_scalar(yT[:, :], ysum[t.parity][:, :], b2tile[t.parity][:, 0:1], None, ALU.add).then_inc(yt_taken, 1)

            tiles(dve, step)

            def combine(k, it):
                q = it * NY + k
                dve.wait_ge(y_in[k], it * 32 + 32)
                for i, done in enumerate((fin_a, fin_b)):
                    if i:
                        dve.wait_ge(fin_a, q + 1)
                    xb = xres[:, bass.ds(q * TN, TN), :]
                    v.tensor_tensor(xb, yin[i][k][:, :, :], xb, ALU.add).then_inc(done, 1)

            with dve.Fori(0, NQ // NY) as it:
                for k in range(NY):
                    combine(k, it)

        @block.scalar
        def _(act):
            a = nc.scalar

            act.wait_ge(wst_zero, 1)
            act.wait_ge(w_in, 7 * 16)
            for k, (raw, halves) in enumerate(((1, wk3), (0, wq3))):
                wsrc = wraw[:, raw, :].rearrange("p (h d) -> p h d", h=H)
                for c in range(3):
                    a.activation(wst[k][:].rearrange("p g j r -> p (g j) r")[:, :, 8 * c:8 * c + 8], wsrc, ACT.Copy).then_inc(wst_done, 1)
                act.wait_ge(wst_done, 3 * k + 3)
                a.activation(halves[0][:], wst[k][:], ACT.Copy).then_inc(wst_hi, 1)

            def halve(c, u, n):
                if n == -1 and u == 0:
                    act.wait_ge(prep, 1)
                act.wait_ge(w_full, c.count(12, u + 1))
                if u >= 2:
                    act.wait_ge(w_free, c.count(12, u - 1))
                width, used = ((KW, K2), (N2, N2))[u // 2]
                dst, src = (w[:, 0:2 * width].rearrange("p (g n) -> p g n", g=2)[:, :, 0:used] for w in (part[u % 2], wide[u % 3]))
                a.activation(dst, src, ACT.Identity, scale=rowsel[1 - u // 2][:, 0:1]).then_inc(w_part, 1)

            def exponentials(s, t, n):
                if exists(n, 0):
                    act.wait_ge(b_full, s.count(8, t + 1))
                    if t >= NP or n != 0:
                        act.wait_ge(pv_done, s.count(8, t - NP + 1))
                    a.activation(pt[t % NP][:].rearrange("p j q -> p (j q)"), scores[t % 2][0:KL, :], ACT.Exp,
                                 scale=SCALE).then_inc(exp_done, 1)

            def slot(s, n):
                c = s + 1
                if exists(n, 1):
                    halve(c, 0, n)
                    halve(c, 1, n)
                if exists(n, -1):
                    take_on(s, -1)
                for t in range(8):
                    if t < 7:
                        exponentials(s, t, n)
                    if t == 6:
                        exponentials(s, 7, n)
                    if t in (1, 2) and exists(n, 1):
                        halve(c, t + 1, n)
                    if t == 4 and exists(n, 0):
                        take_heads(s, 0, n)
                    if t == 2 and exists(n, 1):
                        if n == -1:
                            act.wait_ge(vs_zero, 4)
                        act.wait_ge(v_full, c.count(1, 1))
                        if n is None or n >= 1:
                            act.wait_ge(pv_done, s.count(8))
                        a.activation(vs[c.parity][:, :, :, 0:DH].rearrange("p b h d -> p (b h) d"),
                                     small[0][0:KL, 0:2 * D].rearrange("p (b h d) -> p (b h) d", b=2, h=H), ACT.Copy).then_inc(v_taken, 1)
                    if t == 2 and exists(n, 2):
                        f = s + 2
                        act.wait_ge(tx_full, f.count(1, 1))
                        if n is None or n >= 0:
                            act.wait_ge(hl_done, s.count(1, 1))
                            act.wait_ge(v_full, s.count(1, 1))
                        a.activation(xcT[f.parity][:, 0:N2 + K2], small[1][:, 0:N2 + K2], ACT.Copy).then_inc(tx_taken, 1)
                    if t == 6 and exists(n, 0):
                        take_on(s, 0)
                    if t == 6 and exists(n, -1):
                        act.wait_ge(x2t_full, s.count(1))
                        if n != 1:
                            act.wait_ge(rl_full, s.count(1, -1))
                        a.activation(x2s[:, :], small[0][:, 0:N2], ACT.Copy).then_inc(x2t_taken, 1)
                if exists(n, 0):
                    take_heads(s, 1, n)
                if exists(n, -1):
                    act.wait_ge(top_sub, s.count(1))
                    a.activation(tope[:].rearrange("p b e -> p (b e)"), topd[:].rearrange("p b e -> p (b e)"), ACT.Exp).then_inc(top_exp, 1)

            def take_heads(s, b, n):
                act.wait_ge(pv_done, s.count(8, 4 * b + 4))
                if n != 0:
                    act.wait_ge(ott_full, s.count(2, b - 1))
                a.activation(ots[b][:].rearrange("p g q -> p (g q)"), heads[:, :], ACT.Copy).then_inc(ot_taken, 1)

            def take_on(s, k):
                act.wait_ge(ont_full, s.count(2, k + 1))
                if isinstance(s.pair, int) and s.count(2, k) == 0:
                    pass
                else:
                    act.wait_ge(wo_full, s.count(2, k))
                a.activation(onT[:, :], small[1][:, 0:S], ACT.Copy).then_inc(ont_taken, 1)

            slots(act, slot)

            def upper_x(t, n, d):
                f = t + d
                act.wait_ge(xt_full, f.count(1, 1))
                if third(n, d):
                    act.wait_ge(h_full, f.count(HC, -HC))
                a.activation(xTh[f.parity], bank[4][:, :], ACT.Copy).then_inc(xt_hi, 1)

            def step(t, n):
                if n == -1:
                    upper_x(t, n, 1)
                f = t + 1
                for c in range(HC):
                    if has(n, 1):
                        if c == 0:
                            act.wait_ge(w1_tile[f.parity], f.uses(32))
                        bias = b1tile[f.parity][:, c:c + 1]
                        act.wait_ge(h_full, f.count(HC, c + 1))
                        a.activation(hhl[:, 0, c, :], bank[c][:, :], ACT.Gelu, bias=bias).then_inc(h_hi, 1)
                        if c >= 2 or n != -1:
                            act.wait_ge(h_lo, f.count(HC, c - 1))
                        a.activation(hid[:, c % 2, :], bank[c][:, :], ACT.Gelu, bias=bias).then_inc(h_val, 1)
                    if c == 1 and has(n, 2):
                        upper_x(t, n, 2)

            tiles(act, step)

            with act.Fori(0, NQ) as q:
                act.wait_ge(fin_b, q + 1)
                act.dma_start(out[bass.ds(q * TN, TN), :, :].rearrange("b s d -> s b d"),
                              xres[:, bass.ds(q * TN, TN), :]).then_inc(out_done, 16)
            act.wait_ge(out_done, 16 * NQ)

        @block.tensor
        def _(pe):
            t_ = nc.tensor
            pe.wait_ge(ident_done, 2)
            pe.wait_ge(w_in, 7 * 16)
            pe.wait_ge(b_in, 32)
            t_.transpose(small[0][:, 0:E], wrraw[:, :], ident[0:E, 0:E]).then_inc(wr_T, 1)
            nb = E * (HC + 1)
            t_.transpose(small[0][:, E:E + nb], braw[:, :], ident[0:nb, 0:nb]).then_inc(wr_T, 1)
            pe.wait_ge(w_in2, 32)
            t_.transpose(bank[3][:, 0:P], bvb[:, :], ident[:, :]).then_inc(bo_done, 1)
            pe.wait_ge(bo_done, 2)
            t_.matmul(bank[4][:, 0:D], bvT[:, :], wraw[:, 3, :], start=True, stop=True).then_inc(bo_done, 1)

            def project(c, u, n):
                k = c.parity
                halves, cols, am = (((wk3, slice(N2, N2 + KW), aug[1]), (wq3, slice(0, N2), aug[0]))[u // 2])
                width = (KW, N2)[u // 2]
                if n == -1 and u == 0:
                    pe.wait_ge(prep, 1)
                if n != -1:
                    pe.wait_ge(w_free, c.count(12, u - 2))
                elif u == 3:
                    pe.wait_ge(w_free, 1)
                if u == 0:
                    pe.wait_ge(hl_done, c.count(1, 1))
                    pe.wait_ge(mask_row[k], c.uses(16))
                for gg in range(2):
                    g = 2 * (u % 2) + gg
                    dst = wide[u % 3][:, gg * width:(gg + 1) * width]
                    hi, lo = (w[:, g].rearrange("p j r -> p (j r)") for w in halves)
                    t_.matmul(dst, hi, xcTh[k][:, cols], start=True, stop=False)
                    t_.matmul(dst, hi, xcTl[k][:, cols], start=False, stop=False)
                    t_.matmul(dst, lo, xcTh[k][:, cols], start=False, stop=False)
                    if u < 2:
                        last = t_.matmul(dst, am[0:3, g].rearrange("p j r -> p (j r)"), augx[k][0:3, :], start=False, stop=True)
                    else:
                        last = t_.matmul(dst, am[0:2, g].rearrange("p j r -> p (j r)"), ones2[0:2, :], start=False, stop=True)
                last.then_inc(w_full, 1)

            def values(c, n):
                if n == 0:
                    pe.wait_ge(nm_split, 2)
                elif n != -1:
                    pe.wait_ge(on_done, (c + -1).count(2))
                for b in range(2):
                    last = t_.matmul(small[0][0:KL, b * D:(b + 1) * D],
                                     xcT[c.parity][:, N2 + b * KL:N2 + (b + 1) * KL], wraw[:, 2, :], start=True, stop=True)
                last.then_inc(v_full, 1)

            def turn_heads(s, k):
                pe.wait_ge(ot_taken, s.count(2, k + 1))
                for g in range(G):
                    last = t_.transpose(small[0][:, g * P:(g + 1) * P], ots[k % 2][:, g, :], ident[:, :])
                last.then_inc(ott_full, 1)

            def turn_on(s, k):
                pe.wait_ge(on_done, s.count(2, k + 1))
                t_.transpose(small[1][:, 0:S], on[:].rearrange("p h d -> p (h d)"), ident[:, :]).then_inc(ont_full, 1)

            def project_out(s, k):
                pe.wait_ge(ont_taken, s.count(2, k + 1))
                t_.matmul(small[1][:, 0:D], onT[:, :], wraw[:, 3, :], start=True, stop=True).then_inc(wo_full, 1)

            def by_query(c, u, n):
                b, g = divmod(u, G)
                if u == 0:
                    pe.wait_ge(kblk[c.parity], c.uses(64))
                pe.wait_ge(w_free, c.count(12, 4 + max(u - 2, 0)))
                t_.matmul(wide[(4 + u) % 3][:, 0:J * KL].rearrange("p (j k) -> p j k", j=J), qs[c.parity][:, b, g, :],
                          kb[c.parity][:, g, :, b * KL:(b + 1) * KL], start=True, stop=True).then_inc(w_full, 1)

            def by_key(s, t, n):
                b, g = divmod(t, G)
                if t == 0:
                    pe.wait_ge(mrow[s.parity], s.uses(32))
                if n != 0 or t >= 2:
                    pe.wait_ge(exp_done, s.count(8, t - 1))
                t_.matmul(scores[t % 2][0:KL, :].rearrange("p (j q) -> p j q", j=J), ks[s.parity][:, g, b * KL:(b + 1) * KL],
                          qb[s.parity][:, b, g, :, :], start=True, stop=True).then_inc(b_full, 1)

            def weigh(s, t, n):
                b, g = divmod(t, G)
                pe.wait_ge(exp_done, s.count(8, t + 1))
                if g == 0 and not (n == 0 and b == 0):
                    pe.wait_ge(ot_taken, s.count(2, b))
                for j in range(J):
                    last = t_.matmul(heads[R * j:R * j + R, g * S:(g + 1) * S], vs[s.parity][:, b, G * g + j, :],
                                     pt[t % NP][:, j, :], start=True, stop=True, tile_position=(0, R * j))
                last.then_inc(pv_done, 1)

            def slot(s, n):
                c = s + 1
                if exists(n, 1):
                    project(c, 0, n)
                if exists(n, -1):
                    if n == NCH:
                        pe.wait_ge(x2t_taken, NCH - 1)
                    else:
                        pe.wait_ge(nm_split, s.count(2, 2))
                    turn_heads(s, -1)
                if exists(n, 1):
                    project(c, 1, n)
                if exists(n, -1):
                    if exists(n, -2):
                        pe.wait_ge(rl_taken, s.count(1, -1))
                    turn_on(s, -1)
                if exists(n, 0):
                    by_key(s, 0, n)
                    by_key(s, 1, n)
                if exists(n, -1):
                    project_out(s, -1)
                for t in range(8):
                    if exists(n, 0):
                        weigh(s, t, n)
                        if t < 6:
                            by_key(s, t + 2, n)
                    if exists(n, 1) and t in (0, 1):
                        project(c, t + 2, n)
                        if t == 1:
                            values(c, n)
                    if exists(n, 2) and t == 1:
                        f = s + 2
                        pe.wait_ge(lnx_done, f.count(1, 1))
                        pe.wait_ge(ctx_in[f.parity], f.uses(16))
                        if exists(n, -1):
                            pe.wait_ge(x1_done, s.count(2, 0))
                        elif n != -2:
                            pe.wait_ge(tx_taken, n + 2)
                        for b in range(2):
                            t_.transpose(small[1][:, b * S:(b + 1) * S], xn[f.parity][:, b, :], ident[:, :])
                        for b in range(2):
                            last = t_.transpose(small[1][:, N2 + b * KL:N2 + (b + 1) * KL], ctxin[f.parity][:, b, :], ident[0:KL, 0:KL])
                        last.then_inc(tx_full, 1)
                    if exists(n, 1) and 2 <= t < 6:
                        by_query(c, 2 * t - 4, n)
                        by_query(c, 2 * t - 3, n)
                    if exists(n, -2) and t == 2:
                        if exists(n, 2):
                            pe.wait_ge(tx_taken, s.count(1, 3))
                        else:
                            pe.wait_ge(x1_done, s.count(2, 0) if exists(n, -1) else 2 * NCH)
                        if n == NCH + 1:
                            pe.wait_ge(rl_taken, NCH)
                        pe.wait_ge(top_chain, s.count(6, -6))
                        for b in range(2):
                            dst = small[1][:, 16 + b * E:16 + (b + 1) * E]
                            t_.matmul(dst, tri[:, :], taken[:, b, :], start=True, stop=False)
                            last = t_.matmul(dst, ones[:, :], before[:, :], start=False, stop=b == 0)
                            if b:
                                last = t_.matmul(dst, ones[:, :], taken[:, 0, :], start=False, stop=True)
                        last.then_inc(pos_full, 1)
                    if exists(n, 0) and t == 4:
                        if exists(n, 1):
                            pe.wait_ge(v_taken, c.count(1, 1))
                        else:
                            pe.wait_ge(on_done, s.count(2))
                        turn_heads(s, 0)
                    if exists(n, 0) and t == 5:
                        if exists(n, -2):
                            pe.wait_ge(pos_taken, s.count(1, -1))
                        else:
                            pe.wait_ge(tx_taken, n + 3)
                        turn_on(s, 0)
                    if exists(n, -1) and t == 6:
                        pe.wait_ge(ln2_done, s.count(1))
                        pe.wait_ge(on_done, s.count(2, 1 if exists(n, 0) else 0))
                        for b in range(2):
                            last = t_.transpose(small[0][:, b * S:(b + 1) * S], rows[1 - s.parity][:, b, 0, 0:D], ident[:, :])
                        last.then_inc(x2t_full, 1)
                    if exists(n, 0) and t == 6:
                        project_out(s, 0)
                    if exists(n, 1) and t == 7:
                        pe.wait_ge(w_free, c.count(12, 12))
                        if n == -1:
                            pe.wait_ge(v_taken, 1)
                        elif n == 0:
                            pe.wait_ge(on_done, 1)
                        else:
                            pe.wait_ge(x2t_taken, s.count(1))
                        t_.transpose(small[0][0:J * G * 2, 0:S], mx[:].rearrange("p b g j -> p (b g j)"), ident[:, :]).then_inc(nm_full, 1)
                    if exists(n, -1) and t == 7:
                        pe.wait_ge(x2t_taken, s.count(1))
                        if exists(n, 0):
                            pe.wait_ge(x1_done, s.count(2, 1))
                        else:
                            pe.wait_ge(pos_taken, NCH - 1)
                        for b in range(2):
                            last = t_.matmul(small[1][:, b * E:(b + 1) * E], x2s[:, b * S:(b + 1) * S],
                                             wrT[:, :], start=True, stop=True)
                        last.then_inc(rl_full, 1)

            slots(pe, slot)

            pe.wait_ge(pos_chain, 3 * NCH)
            pe.wait_ge(x2t_taken, NCH)
            t_.matmul(small[0][:, 0:E], ones[:, :], before[:, :], start=True, stop=True).then_inc(cnt_full, 1)

            def turn_x(t, n, d):
                f = t + d
                pe.wait_ge(x_tile[f.parity], f.uses(16))
                if not (n == -1 and d == 1):
                    pe.wait_ge(xt_lo, f.count(1))
                for j in range(TN):
                    last = t_.transpose(bank[4][:, j * P:(j + 1) * P], xrow[f.parity][:, j, 0:D], ident[:, :])
                last.then_inc(xt_full, 1)

            def step(t, n):
                if n == -1:
                    pe.wait_ge(pv_done, 8 * NCH)
                    turn_x(t, n, 1)
                for c in range(HC):
                    cs = slice(c * P, (c + 1) * P)
                    if has(n, 0):
                        w, y = wtile[t.parity], ysum[t.parity]
                        if c == 0:
                            pe.wait_ge(w2_tile[t.parity], t.uses(32))
                            if third(n, 0):
                                pe.wait_ge(yt_taken, t.count(1, -1))
                        pe.wait_ge(h_hi, t.count(HC, c + 1))
                        t_.matmul(y[:, :], w[:, 0, 1, cs], hhl[:, 0, c, :], start=c == 0, stop=False)
                        t_.matmul(y[:, :], w[:, 1, 1, cs], hhl[:, 0, c, :], start=False, stop=False)
                        pe.wait_ge(h_lo, t.count(HC, c + 1))
                        last = t_.matmul(y[:, :], w[:, 0, 1, cs], hhl[:, 1, c, :], start=False, stop=c == HC - 1)
                        if c == HC - 1:
                            last.then_inc(yt_full, 1)
                    if has(n, 1):
                        f = t + 1
                        w, xh, xl = wtile[f.parity], xTh[f.parity], xTl[f.parity]
                        if c == 0:
                            pe.wait_ge(xt_lo, f.count(1, 1))
                            pe.wait_ge(w1_tile[f.parity], f.uses(32))
                        if n != -1:
                            pe.wait_ge(h_val, t.count(HC, c + 1))
                        t_.matmul(bank[c][:, :], w[:, 0, 0, cs], xh, start=True, stop=False)
                        t_.matmul(bank[c][:, :], w[:, 0, 0, cs], xl, start=False, stop=False)
                        t_.matmul(bank[c][:, :], w[:, 1, 0, cs], xh, start=False, stop=True).then_inc(h_full, 1)
                    if c == 1 and has(n, 2):
                        turn_x(t, n, 2)
                    if c == 2 and has(n, -1):
                        p = t + -1
                        pe.wait_ge(yt_taken, p.count(1, 1))
                        if n == 1:
                            pe.wait_ge(tables, 1)
                        else:
                            pe.wait_ge(yr_taken, p.count(1))
                        for j in range(TN):
                            last = t_.transpose(bank[6][:, j * P:(j + 1) * P], yT[:, j * P:(j + 1) * P], ident[:, :])
                        last.then_inc(yr_full, 1)

            tiles(pe, step)


_INS = ['x', 'ctx_1024', 'mask_BxS2_bf0', 'L0_xattn_Wq', 'L0_xattn_bq', 'L0_xattn_Wk', 'L0_xattn_bk', 'L0_xattn_Wv',
        'L0_xattn_bv', 'L0_xattn_Wo', 'L0_xattn_bo', 'L0_ffn_Wr', 'L0_ffn_W1', 'L0_ffn_b1', 'L0_ffn_W2', 'L0_ffn_b2']


def kernel(**inputs):
    import numpy as _np
    import concourse.bacc as _bacc
    from concourse import mybir as _mybir
    from concourse.bass_utils import run_bass_kernel_spmd as _run

    nc = _bacc.Bacc("TRN2", target_bir_lowering=False, num_devices=1)
    arrays, args = {}, []
    for name in _INS:
        a = _np.ascontiguousarray(inputs[name])
        arrays[f"in_{name}"] = a
        args.append(nc.dram_tensor(f"in_{name}", a.shape, _mybir.dt.from_np(a.dtype), kind="ExternalInput").ap())
    out = nc.dram_tensor("out_0", inputs["x"].shape, F32, kind="ExternalOutput").ap()
    moe_attention(nc, *args, out)
    r = _run(nc, [arrays], core_ids=[0])
    return r.results[0]["out_0"]
```
